# Optimizing a Trainium2 kernel written in Bass

```python
import numpy as np
import jax
import jax.numpy as jnp

def _softmax(x, axis=-1):
    return jax.nn.softmax(x, axis=axis)

def _gelu(x):
    return jax.nn.gelu(x, approximate=True)

def _silu(x):
    return jax.nn.silu(x)

def _sigmoid(x):
    return jax.nn.sigmoid(x)

def _layernorm(x, axis=-1, eps=1e-05):
    m = jnp.mean(x, axis=axis, keepdims=True)
    v = jnp.var(x, axis=axis, keepdims=True)
    return (x - m) / jnp.sqrt(v + eps)

def _scatter_add(tgt, idx, src, axis=0):
    return tgt.at[idx].add(src)

def _segment_sum(src, seg, n):
    return jax.ops.segment_sum(src, seg, n)
kernel_name = 'mk_gps_d1_gnn_r8_1771de'

def setup_inputs(seed: int=0):
    np.random.seed(seed)
    _w = jnp.asarray

    def _rec_inputs():
        import jax
        import jax.numpy as jnp
        _gk = jax.random.key(seed)
        x = -0.0003713 + 1 * jax.random.normal(jax.random.fold_in(_gk, 1), (6250, 256), jnp.float32)
        src = jax.random.randint(jax.random.fold_in(_gk, 2), (200000,), 0, 6250, jnp.int32)
        dst = jnp.minimum((6250 * jax.random.uniform(jax.random.fold_in(_gk, 3), (200000,)) ** 2.0).astype(jnp.int32), 49999)
        _o = jnp.argsort(dst, stable=True)
        src = src[_o]
        dst = dst[_o]
        edge_attr_96 = -4.21973e-05 + 0.999841 * jax.random.normal(jax.random.fold_in(_gk, 12), (200000, 96), jnp.float32)
        return (x, src, dst, edge_attr_96)
    x, src, dst, edge_attr_96 = _rec_inputs()

    def _L0_gnn_setup():
        import jax, jax.numpy as jnp
        import numpy as np
        N_NODES = 6250
        N_EDGES = 100000
        EDGE_F = 96
        NODE_F = 256
        GLOB_F = 64
        HIDDEN = 1024
        N_GRAPHS = 8
        MLP_IN = NODE_F + 3 * EDGE_F + GLOB_F
        key = jax.random.key(seed)
        ks = jax.random.split(key, 9)
        x = jax.random.normal(ks[0], (N_NODES, NODE_F), dtype=jnp.float32)
        edge_attr = jax.random.normal(ks[1], (N_EDGES, EDGE_F), dtype=jnp.float32)
        u = jax.random.normal(ks[2], (N_GRAPHS, GLOB_F), dtype=jnp.float32)
        W1 = jax.random.normal(ks[3], (MLP_IN, HIDDEN), dtype=jnp.float32) * (1.0 / np.sqrt(MLP_IN))
        b1 = jax.random.normal(ks[4], (HIDDEN,), dtype=jnp.float32) * 0.01
        W2 = jax.random.normal(ks[5], (HIDDEN, NODE_F), dtype=jnp.float32) * (1.0 / np.sqrt(HIDDEN))
        b2 = jax.random.normal(ks[6], (NODE_F,), dtype=jnp.float32) * 0.01
        edge_index = jax.random.randint(ks[7], (2, N_EDGES), 0, N_NODES, dtype=jnp.int64 if jax.config.jax_enable_x64 else jnp.int32)
        batch = jnp.sort(jax.random.randint(ks[8], (N_NODES,), 0, N_GRAPHS, dtype=jnp.int32))
        return {'x': x, 'edge_attr': edge_attr, 'u': u, 'W1': W1, 'b1': b1, 'W2': W2, 'b2': b2, 'edge_index': edge_index, 'batch': batch}
    _L0_gnn_all = _L0_gnn_setup()
    _L0_gnn_in = {k: v for k, v in _L0_gnn_all.items() if k in ('u', 'W1', 'b1', 'W2', 'b2')}
    del _L0_gnn_all

    def _L0_mix_setup():
        import math
        import jax, jax.numpy as jnp
        import numpy as np
        EPS_DIV = 1e-07
        EPS_NORM = 1e-12

        def _l2_normalize(x, axis):
            n = jnp.sqrt(jnp.sum(x * x, axis=axis, keepdims=True))
            return x / jnp.maximum(n, EPS_NORM)
        key = jax.random.key(seed)
        ks = jax.random.split(key, 5)
        b, N, C = (8, 512, 256)
        x = jax.random.normal(ks[0], (b, N, C), dtype=jnp.float32)
        W_qkv = jax.random.normal(ks[1], (C, 3 * C), dtype=jnp.float32) * (1.0 / math.sqrt(C))
        b_qkv = jax.random.normal(ks[2], (3 * C,), dtype=jnp.float32) * 0.02
        W_out = jax.random.normal(ks[3], (C, C), dtype=jnp.float32) * (1.0 / math.sqrt(C))
        b_out = jax.random.normal(ks[4], (C,), dtype=jnp.float32) * 0.02
        return {'x': x, 'W_qkv': W_qkv, 'b_qkv': b_qkv, 'W_out': W_out, 'b_out': b_out}
    _L0_mix_all = _L0_mix_setup()
    _L0_mix_in = {k: v for k, v in _L0_mix_all.items() if k in ('W_qkv', 'b_qkv', 'W_out', 'b_out')}
    del _L0_mix_all

    def _L0_ffn_setup():
        import jax, jax.numpy as jnp
        import numpy as np
        B, S, D = (8, 512, 256)
        H = 4 * D
        CAPACITY = 0.5
        key = jax.random.key(seed)
        ks = jax.random.split(key, 6)
        x = jax.random.normal(ks[0], (B, S, D), dtype=jnp.float32)
        attention_mask = jnp.zeros((B, 1, 1, S), dtype=jnp.float32)
        wr = jax.random.normal(ks[1], (D, 1), dtype=jnp.float32) * 0.02
        br = jnp.zeros((1,), dtype=jnp.float32)
        w1 = jax.random.normal(ks[2], (D, H), dtype=jnp.float32) * 0.02
        b1 = jnp.zeros((H,), dtype=jnp.float32)
        w2 = jax.random.normal(ks[3], (H, D), dtype=jnp.float32) * 0.02
        b2 = jnp.zeros((D,), dtype=jnp.float32)
        return {'x': x, 'attention_mask': attention_mask, 'wr': wr, 'br': br, 'w1': w1, 'b1': b1, 'w2': w2, 'b2': b2}
    _L0_ffn_all = _L0_ffn_setup()
    _L0_ffn_in = {k: v for k, v in _L0_ffn_all.items() if k in ('attention_mask', 'wr', 'br', 'w1', 'b1', 'w2', 'b2')}
    del _L0_ffn_all
    return {'x': x, 'src': src, 'dst': dst, 'edge_attr_96': edge_attr_96, 'L0_gnn_u': _L0_gnn_in['u'], 'L0_gnn_W1': _L0_gnn_in['W1'], 'L0_gnn_b1': _L0_gnn_in['b1'], 'L0_gnn_W2': _L0_gnn_in['W2'], 'L0_gnn_b2': _L0_gnn_in['b2'], 'L0_mix_W_qkv': _L0_mix_in['W_qkv'], 'L0_mix_b_qkv': _L0_mix_in['b_qkv'], 'L0_mix_W_out': _L0_mix_in['W_out'], 'L0_mix_b_out': _L0_mix_in['b_out'], 'L0_ffn_attention_mask': _L0_ffn_in['attention_mask'], 'L0_ffn_wr': _L0_ffn_in['wr'], 'L0_ffn_br': _L0_ffn_in['br'], 'L0_ffn_w1': _L0_ffn_in['w1'], 'L0_ffn_b1': _L0_ffn_in['b1'], 'L0_ffn_w2': _L0_ffn_in['w2'], 'L0_ffn_b2': _L0_ffn_in['b2']}

def reference(x, src, dst, edge_attr_96, L0_gnn_u, L0_gnn_W1, L0_gnn_b1, L0_gnn_W2, L0_gnn_b2, L0_mix_W_qkv, L0_mix_b_qkv, L0_mix_W_out, L0_mix_b_out, L0_ffn_attention_mask, L0_ffn_wr, L0_ffn_br, L0_ffn_w1, L0_ffn_b1, L0_ffn_w2, L0_ffn_b2):
    import jax
    import jax.numpy as jnp

    def _L0_gnn_ref(x, edge_attr, u, W1, b1, W2, b2, edge_index, batch):
        import jax, jax.numpy as jnp
        import numpy as np
        N_NODES = 6250
        N_EDGES = 100000
        EDGE_F = 96
        NODE_F = 256
        GLOB_F = 64
        HIDDEN = 1024
        N_GRAPHS = 8
        MLP_IN = NODE_F + 3 * EDGE_F + GLOB_F
        col = edge_index[1]
        n = x.shape[0]
        out1 = jax.ops.segment_sum(edge_attr, col, num_segments=n)
        cnt = jax.ops.segment_sum(jnp.ones((edge_attr.shape[0], 1), edge_attr.dtype), col, num_segments=n)
        out2 = jax.ops.segment_max(edge_attr, col, num_segments=n)
        out2 = jnp.where(cnt > 0, out2, jnp.zeros_like(out2))
        out3 = out1 / jnp.maximum(cnt, 1.0)
        h = jnp.concatenate([x, out1, out2, out3, u[batch]], axis=1)
        h = jax.nn.relu(h @ W1 + b1) @ W2 + b2
        return h + x

    def _L0_mix_ref(x, W_qkv, b_qkv, W_out, b_out):
        import math
        import jax, jax.numpy as jnp
        import numpy as np
        EPS_DIV = 1e-07
        EPS_NORM = 1e-12

        def _l2_normalize(x, axis):
            n = jnp.sqrt(jnp.sum(x * x, axis=axis, keepdims=True))
            return x / jnp.maximum(n, EPS_NORM)
        b, N, C = x.shape
        qkv = x @ W_qkv + b_qkv
        q, k, v = jnp.split(qkv, 3, axis=2)
        q = q - jnp.mean(q, axis=2, keepdims=True)
        k = k - jnp.mean(k, axis=2, keepdims=True)
        q2 = q * q
        k2 = k * k
        q2s = jnp.sum(q2, axis=2, keepdims=True)
        k2s = jnp.sum(k2, axis=2, keepdims=True)
        k2 = _l2_normalize(k2 / (k2s + EPS_DIV), axis=-2)
        q2 = _l2_normalize(q2 / (q2s + EPS_DIV), axis=-1)
        kv = jnp.einsum('bnc,bnd->bcd', k2, v)
        t2 = jnp.einsum('bnc,bcd->bnd', q2, kv) / math.sqrt(N)
        attn = v + t2
        return attn @ W_out + b_out

    def _L0_ffn_ref(x, attention_mask, wr, br, w1, b1, w2, b2):
        import jax, jax.numpy as jnp
        import numpy as np
        B, S, D = (8, 512, 256)
        H = 4 * D
        CAPACITY = 0.5
        b, s, d = x.shape
        weights = (jnp.einsum('bsd,do->bso', x, wr) + br)[..., 0]
        k = max(1, int(CAPACITY * s))
        kk = k - 1 if k > 1 else 1
        _, idx = jax.lax.top_k(weights, k)
        sel_idx = idx[:, :kk]
        sel = jnp.take_along_axis(x, sel_idx[:, :, None], axis=1)
        h = jax.nn.gelu(jnp.einsum('bkd,dh->bkh', sel, w1) + b1)
        y = jnp.einsum('bkh,hd->bkd', h, w2) + b2
        w_sel = jnp.take_along_axis(weights, sel_idx, axis=1)
        y = y * w_sel[..., None]
        batch_idx = jnp.arange(b)[:, None]
        processed = jnp.zeros_like(x).at[batch_idx, sel_idx].set(y)
        return processed + x
    edge_index = jnp.stack([src, dst])
    batch0 = jnp.zeros((6250,), jnp.int32)
    xn = _layernorm(x, axis=-1)
    x = x + _L0_gnn_ref(xn, edge_attr_96, L0_gnn_u, L0_gnn_W1, L0_gnn_b1, L0_gnn_W2, L0_gnn_b2, edge_index, batch0) + _L0_mix_ref(xn[None], L0_mix_W_qkv, L0_mix_b_qkv, L0_mix_W_out, L0_mix_b_out)[0]
    x = x + _L0_ffn_ref(_layernorm(x, axis=-1)[None], L0_ffn_attention_mask, L0_ffn_wr, L0_ffn_br, L0_ffn_w1, L0_ffn_b1, L0_ffn_w2, L0_ffn_b2)[0]
    return x

_drawn_inputs = setup_inputs


def setup_inputs(seed=0):
    import zlib

    import numpy as np

    out = dict(_drawn_inputs(seed))
    spreads = {'L0_ffn_b1': (0.0, 0.8), 'L0_ffn_b2': (0.0, 0.8)}
    factors = {'L0_gnn_b1': 8.0,
     'L0_gnn_b2': 8.0,
     'L0_mix_b_out': 8.0,
     'L0_ffn_wr': 6.796,
     'L0_ffn_w1': 8.0,
     'L0_ffn_w2': 8.0}
    for name, (base, spread) in spreads.items():
        noise = np.random.default_rng([zlib.crc32(name.encode()), seed]).standard_normal(out[name].shape)
        drawn = base * np.exp(spread * noise) if base else spread * noise
        out[name] = jnp.asarray(drawn.astype(out[name].dtype))
    for name, factor in factors.items():
        out[name] = (out[name] * factor).astype(out[name].dtype)
    return out
```

```python
import numpy as np
import concourse.bass as bass
from concourse import mybir
from concourse.alu_op_type import AluOpType as ALU
from contextlib import ExitStack

ACT = mybir.ActivationFunctionType
f32 = mybir.dt.float32
i32 = mybir.dt.int32
FMAX = float(np.finfo(np.float32).max)

P = 128
NODES, NF = 6250, 256
EDGES, EF = 200000, 96
HID = 1024
GF = 64
TILES = -(-NODES // P)
GT = 4
GROUPS = TILES // GT
LAST = NODES - (TILES - 1) * P
SIDE = 448
EPAD = SIDE * SIDE
R = EPAD // P
Q = R // 4
T = 32
TQ = T // 4
CHUNKS = R // T
XB, MB, OB = 4, 2, 2
SEL = NODES // 2 - 1
STILES = -(-SEL // P)
SGROUPS = STILES // GT
SLAST = SEL - (STILES - 1) * P
AGG = 2 * EF
EPS = 1e-5
KF = NF // P
KH = HID // P
YROW = 2 * NF + 8


def build(nc, x, dstp, edges, u, W1, b1, W2, b2, Wqkv, bqkv, Wout, bout, wr, br, w1, fb1, w2, fb2, out):
    dram = lambda n, s, d=f32: nc.dram_tensor(n, s, d).ap()
    xT_d = dram("xT_d", (GROUPS + 1, P, KF, GT * P))
    qT_d = dram("qT_d", (GROUPS + 1, P, KF, GT * P))
    scan_d = dram("scan_d", (P * Q, AGG))
    carry_d = dram("carry_d", (P, AGG))
    end_d = dram("end_d", (TILES * P + P,))
    yrow_d = dram("yrow_d", (NODES, YROW))
    list_d = dram("list_d", (SEL, 1), i32)

    keep = ExitStack()
    with keep:
        ksb = lambda n, s, d=f32: keep.enter_context(nc.sbuf_tensor(n, s, d))
        ident = ksb("ident", [P, P])
        ones = ksb("ones", [P, P])
        node = ksb("node", [P, TILES])
        q2s = ksb("q2s", [P, TILES])
        q4s = ksb("q4s", [P, TILES])
        rq = ksb("rq", [P, TILES])
        M = ksb("M", [P, KF, NF])
        WvoI = ksb("WvoI", [P, KF, NF])
        brow = ksb("brow", [1, NF])
        Eend = ksb("Eend", [P, TILES])
        Sbeg = ksb("Sbeg", [P, TILES])
        idx = ksb("idx", [P, 3, TILES], i32)
        iRaw, iScan, iCarry = (idx[:, i, :] for i in range(3))
        has = ksb("has", [P, TILES])
        rcnt = ksb("rcnt", [P, TILES])
        kSel = ksb("kSel", [P, 5, TILES])
        mSel = ksb("mSel", [P, 5, TILES])
        wgt = ksb("wgt", [P, TILES])

        with ExitStack() as ctx:
            sb = lambda n, s, d=f32: ctx.enter_context(nc.sbuf_tensor(n, s, d))
            ps = lambda n, s: ctx.enter_context(nc.psum_tensor(n, s, f32))
            sem = lambda n: ctx.enter_context(nc.semaphore(n))
            dcur = sb("dcur", [P, R], i32)
            dprv = sb("dprv", [P, R], i32)
            kTri = sb("kTri", [P, Q, 3])
            pTri = sb("pTri", [P, Q, 3])
            kQ = sb("kQ", [P, Q])
            mQ = sb("mQ", [P, Q])
            xb = [sb(f"xb{i}", [P, TQ, 4, EF]) for i in range(XB)]
            mx = [sb(f"mx{i}", [P, TQ, 3, EF]) for i in range(MB)]
            ob = [sb(f"ob{i}", [P, TQ, AGG]) for i in range(OB)]
            xg = sb("xg", [P, GT, NF])
            xn = sb("xn", [P, GT, NF])
            xT = sb("xT", [P, KF, GT * P])
            qT = sb("qT", [P, KF, GT * P])
            q2 = sb("q2", [P, GT, NF])
            k2 = sb("k2", [P, GT, NF])
            kc = sb("kc", [P, GT, 2 * NF])
            junk = sb("junk", [P, NF])
            jc = [sb(f"jc{i}", [P, SIDE], mybir.dt.bfloat16) for i in range(4)]
            Wqk = sb("Wqk", [P, KF, 2 * NF])
            Wv = sb("Wv", [P, KF, NF])
            Wo = sb("Wo", [P, KF, NF])
            WvT = sb("WvT", [P, KF, NF])
            kvT = sb("kvT", [P, KF, NF])
            kxT = sb("kxT", [P, KF, NF])
            bqk = sb("bqk", [1, 3 * NF])
            bv = sb("bv", [P, KF])
            b2r = sb("b2r", [1, 2, NF])
            wm = sb("wm", [P, 8])
            krow = sb("krow", [1, 2 * NF])
            kcol = sb("kcol", [P, 8])
            st = sb("st", [P, TILES, 6])
            mean = sb("mean", [P, TILES])
            va = sb("va", [P, TILES])
            sd = sb("sd", [P, TILES])
            rstd = sb("rstd", [P, TILES])
            nmr = sb("nmr", [P, TILES])
            k2s = sb("k2s", [P, GT])
            rk = sb("rk", [P, GT])
            nodei = sb("nodei", [P, TILES], i32)
            nhalf = sb("nhalf", [P, TILES])
            crow = sb("crow", [1, SIDE], i32)
            crowf = sb("crowf", [1, SIDE])
            csum = sb("csum", [P, TILES])
            ridx = sb("ridx", [P, TILES])
            ridxi = sb("ridxi", [P, TILES], i32)
            fr = [sb(f"fr{i}", [P, SIDE], i32) for i in range(8)]
            fsum = sb("fsum", [P, TILES])
            rcol = [sb(f"rcol{i}", [P, 4], i32) for i in range(2)]
            a1, a2, a3, a4, a5 = (sb(f"a{i}", [P, TILES]) for i in range(5))
            ai = sb("ai", [P, TILES], i32)
            keepc = sb("keepc", [P, 1])
            diag = sb("diag", [P, P])
            cT = sb("cT", [EF, 4, P])
            cs = sb("cs", [EF, 2, P])
            cr = sb("cr", [P, AGG])

            psT = [ps(f"psT{i}", [P, 512]) for i in range(2)]
            psQ = [ps(f"psQ{i}", [P, 512]) for i in range(2)]
            psKx = [ps(f"psKx{i}", [P, 512]) for i in range(2)]
            psR = ps("psR", [P, 512])
            psC = ps("psC", [P, 512])

            s_dst = sem("s_dst")
            s_load = [sem(f"s_load{i}") for i in range(XB)]
            s_dump = [sem(f"s_dump{i}") for i in range(OB)]
            s_const = sem("s_const")
            s_wload = sem("s_wload")
            s_masks = sem("s_masks")
            s_pen = sem("s_pen")
            s_mul = sem("s_mul")
            s_tree = sem("s_tree")
            s_max = sem("s_max")
            s_sum = sem("s_sum")
            s_v = sem("s_v")
            s_stat = sem("s_stat")
            s_sqrt = sem("s_sqrt")
            s_ln = sem("s_ln")
            s_xg = sem("s_xg")
            s_xn = sem("s_xn")
            s_tr = sem("s_tr")
            s_evac = sem("s_evac")
            s_qk = sem("s_qk")
            s_sq = sem("s_sq")
            s_rk = sem("s_rk")
            s_kk = sem("s_kk")
            s_kx = sem("s_kx")
            s_xTo = sem("s_xTo")
            s_qTo = sem("s_qTo")
            s_wq = sem("s_wq")
            s_crow = sem("s_crow")
            s_cbc = sem("s_cbc")
            s_csum = sem("s_csum")
            s_ridx = sem("s_ridx")
            s_fr = [sem(f"s_fr{i}") for i in range(8)]
            s_fs = sem("s_fs")
            s_col = sem("s_col")
            s_turn = sem("s_turn")
            s_end = sem("s_end")
            s_endo = sem("s_endo")
            s_beg = sem("s_beg")
            s_zero = sem("s_zero")
            s_pt = sem("s_pt")
            s_at = sem("s_at")
            s_pc = sem("s_pc")
            s_vc = sem("s_vc")
            s_cro = sem("s_cro")
            s_act = sem("s_act")
            s_pairs = sem("s_pairs")
            s_pc0 = sem("s_pc0")
            s_id = sem("s_id")
            s_xs = [sem(f"s_xs{i}") for i in range(4)]

            ev = edges.rearrange("(p r) f -> p r f", r=R)
            dcur_v = dstp[SIDE:SIDE + EPAD].rearrange("(p r) -> p r", r=R)
            dprv_v = dstp[SIDE - 1:SIDE - 1 + EPAD].rearrange("(p r) -> p r", r=R)
            rows_v = dstp.rearrange("(a b) -> a b", b=SIDE)
            scan_v = scan_d.rearrange("(p q) f -> p q f", q=Q)
            end_w = end_d[1:TILES * P + 1].rearrange("(t p) -> p t", p=P)
            end_r = end_d[0:TILES * P].rearrange("(t p) -> p t", p=P)

            def quads(c):
                return bass.ds(c * TQ, TQ)

            def x_group(g, nt, rows):
                return x[bass.ds(g * GT * P, nt * rows), :].rearrange("(t p) f -> p t f", p=rows)

            xs = [xg, xn, q2, k2]

            block = ctx.enter_context(nc.Block())

            @block.sync
            def _(sp):
                sp.dma_start(dcur[:, :], dcur_v).then_inc(s_dst, 16)
                sp.dma_start(dprv[:, :], dprv_v).then_inc(s_dst, 16)
                for b in range(XB):
                    sp.dma_start(xb[b][:, :, :, :].rearrange("p q i f -> p (q i) f"),
                                 ev[:, b * T:(b + 1) * T, :]).then_inc(s_load[b], 16)

                def dump_and_load(c, b, load):
                    sp.wait_ge(s_sum, c * TQ + TQ + 1)
                    sp.wait_ge(s_max, c * TQ + TQ + 1)
                    sp.dma_start(scan_v[:, quads(c), :], ob[b % OB][:, :, :]).then_inc(s_dump[b % OB], 16)
                    if load:
                        sp.dma_start(xb[b][:, :, :, :].rearrange("p q i f -> p (q i) f"),
                                     ev[:, bass.ds(c * T + XB * T, T), :]).then_inc(s_load[b], 16)

                with sp.Fori(0, 11) as g:
                    for b in range(XB):
                        dump_and_load(g * XB + b, b, True)
                for c in range(44, CHUNKS):
                    dump_and_load(c, c % XB, c + XB < CHUNKS)
                sp.wait_ge(s_vc, 3)
                sp.dma_start(carry_d, cr[:, :]).then_inc(s_cro, 16)
                sp.wait_ge(s_end, 1)
                sp.wait_ge(s_zero, 1)
                sp.dma_start(end_w, Eend[:, :], allow_slow_non_contiguous=True).then_inc(s_endo, 16)
                sp.dma_start(end_d[0:1].rearrange("(a b) -> a b", b=1), a5[0:1, 0:1]).then_inc(s_endo, 16)
                sp.wait_ge(s_endo, 32)
                sp.dma_start(Sbeg[:, :], end_r, allow_slow_non_contiguous=True).then_inc(s_beg, 16)
                sp.wait_ge(s_dump[0], 16 * 25)
                sp.wait_ge(s_dump[1], 16 * 24)
                sp.wait_ge(s_cro, 16)
                sp.wait_ge(s_beg, 16)

            @block.gpsimd
            def _(pool):
                nc.gpsimd.memset(ident[:, :], 0.0).then_inc(s_id, 1)
                pool.wait_ge(s_id, 1)
                nc.gpsimd.affine_select(out=ident[:, :], in_=ident[:, :], compare_op=ALU.not_equal, fill=1.0, base=0,
                                        pattern=[[-1, P]], channel_multiplier=1).then_inc(s_const, 1)
                nc.gpsimd.memset(ones[:, :], 1.0).then_inc(s_const, 1)
                nc.gpsimd.iota(nodei[:, :], pattern=[[P, TILES]], base=0, channel_multiplier=1).then_inc(s_const, 1)
                pool.wait_ge(s_masks, 1)

                def mask(c, b, g):
                    pool.wait_ge(s_load[b], g * 16 + 16)
                    if not isinstance(c, int) or c >= MB:
                        pool.wait_ge(s_max, c * TQ - TQ * MB + TQ + 1)
                    x3 = xb[b][:, :, 0:3, :]
                    k = kTri[:, quads(c), :].rearrange("p q (i o) -> p q i o", o=1).broadcast_to([P, TQ, 3, EF])
                    p_ = pTri[:, quads(c), :].rearrange("p q (i o) -> p q i o", o=1).broadcast_to([P, TQ, 3, EF])
                    nc.gpsimd.tensor_tensor(mx[b % MB][:, :, :, :], x3, p_, ALU.add).then_inc(s_pen, 1)
                    pool.wait_ge(s_pen, c + 1)
                    nc.gpsimd.tensor_tensor(x3, x3, k, ALU.mult).then_inc(s_mul, 1)

                def columns(t, e):
                    nc.gpsimd.tensor_copy(rcol[e][:, :], ridxi[:, bass.ds(t, 4)]).then_inc(s_col, 1)

                def rows(b, n):
                    pool.wait_ge(s_col, n)
                    pool.sem_inc(s_turn, 1)
                    nc.gpsimd.indirect_dma_start(
                        out=fr[b][:, :], out_offset=None, in_=rows_v,
                        in_offset=bass.IndirectOffsetOnAxis(ap=rcol[b // 4][:, b % 4:b % 4 + 1], axis=0)).then_inc(s_fr[b], 16)

                for g in range(2):
                    for b in range(XB):
                        mask(g * XB + b, b, g)
                pool.wait_ge(s_ridx, 1)
                for g in range(2, 4):
                    columns(g * 4 - 8, g % 2)
                    for b in range(XB):
                        mask(g * XB + b, b, g)
                        rows((g % 2) * 4 + b, g - 1)
                with pool.Fori(2, 6) as h:
                    for e in range(2):
                        for b in range(XB):
                            mask(h * (2 * XB) + e * XB + b, b, h * 2 + e)
                            pool.wait_ge(s_fs, h * 8 + e * 4 + b - 15)
                            if b == 0:
                                pool.wait_ge(s_fs, h * 8 + e * 4 - 12)
                                columns(h * 8 + e * 4 - 8, e)
                            rows(e * 4 + b, h * 2 + e - 1)
                mask(CHUNKS - 1, 0, 12)
                for t in range(40, TILES):
                    pool.wait_ge(s_fs, t - 7)
                    if t % 4 == 0:
                        pool.wait_ge(s_fs, t - 4)
                        nc.gpsimd.tensor_copy(rcol[t // 4 % 2][:, 0:min(4, TILES - t)], ridxi[:, t:min(t + 4, TILES)]).then_inc(s_col, 1)
                    rows(t % 8, t // 4 + 1)

            @block.vector
            def _(dve):
                nv = [0]

                def step(ins, wait=True):
                    nv[0] += 1
                    ins.then_inc(s_v, 1)
                    if wait:
                        dve.wait_ge(s_v, nv[0])

                dve.wait_ge(s_dst, 32)
                cq = dcur[:, :].rearrange("p (q i) -> p q i", i=4)
                pq = dprv[:, :].rearrange("p (q i) -> p q i", i=4)
                step(nc.vector.tensor_tensor(kTri[:, :, :], cq[:, :, 0:3], cq[:, :, 3:4].broadcast_to([P, Q, 3]), ALU.is_equal), False)
                step(nc.vector.tensor_tensor(kQ[:, :], pq[:, :, 0], cq[:, :, 3], ALU.is_equal))
                step(nc.vector.tensor_scalar(pTri[:, :, :], kTri[:, :, :], 1.0, FMAX, ALU.subtract, ALU.mult), False)
                step(nc.vector.tensor_scalar(mQ[:, :], kQ[:, :], 0.5, 2.0, ALU.subtract, ALU.mult))
                step(nc.vector.tensor_scalar(mQ[:, :], mQ[:, :], FMAX, None, ALU.mult))
                step(nc.vector.tensor_tensor(keepc[:, :], dprv[:, 0:1], dcur[:, R - 1:R], ALU.is_equal), False)
                step(nc.vector.memset(a5[:, :], 0.0))
                dve.sem_inc(s_masks, 1)
                dve.sem_inc(s_zero, 1)
                nc.vector.memset(ob[1][:, TQ - 1, 0:EF], -FMAX).then_inc(s_max, 1)
                nc.vector.memset(ob[1][:, TQ - 1, EF:AGG], 0.0).then_inc(s_sum, 1)
                dve.wait_ge(s_const, 3)
                step(nc.vector.tensor_copy(node[:, :], nodei[:, :]))
                step(nc.vector.tensor_scalar(nhalf[:, :], node[:, :], 0.5, None, ALU.add))
                dve.wait_ge(s_crow, 16)
                step(nc.vector.tensor_copy(crowf[:, :], crow[:, :]))
                dve.sem_inc(s_cbc, 1)
                dve.wait_ge(s_wload, 16 * 8)
                for c in range(KF):
                    for h in range(2):
                        step(nc.vector.tensor_reduce(wm[:, 2 * c + h:2 * c + h + 1], Wqk[:, c, h * NF:(h + 1) * NF],
                                                     mybir.AxisListType.X, ALU.add), False)
                for h in range(2):
                    step(nc.vector.tensor_reduce(wm[0:1, 4 + h:5 + h], bqk[0:1, h * NF:(h + 1) * NF],
                                                 mybir.AxisListType.X, ALU.add))
                step(nc.vector.tensor_scalar(wm[:, 0:4], wm[:, 0:4], 1.0 / NF, None, ALU.mult), False)
                step(nc.vector.tensor_scalar(wm[0:1, 4:6], wm[0:1, 4:6], 1.0 / NF, None, ALU.mult))
                for c in range(KF):
                    for h in range(2):
                        w_ = Wqk[:, c, h * NF:(h + 1) * NF]
                        step(nc.vector.tensor_scalar(w_, w_, wm[:, 2 * c + h:2 * c + h + 1], None, ALU.subtract), False)
                for h in range(2):
                    w_ = bqk[0:1, h * NF:(h + 1) * NF]
                    step(nc.vector.tensor_scalar(w_, w_, wm[0:1, 4 + h:5 + h], None, ALU.subtract))
                dve.sem_inc(s_wq, 1)

                step(nc.vector.memset(st[:, :, :], 1.0), False)
                step(nc.vector.memset(q2s[:, :], 1.0), False)
                step(nc.vector.memset(q4s[:, :], 1.0))
                def stats(g, nt, rows, buf, sem_, n):
                    dve.wait_ge(sem_, n)
                    for t in range(nt):
                        nc.vector.bn_stats(st[0:rows, bass.ds(g * GT + t, 1), :].rearrange("p o s -> p (o s)"),
                                           buf[0:rows, t, :]).then_inc(s_stat, 1)
                with dve.Fori(0, GROUPS // 4) as h:
                    for e in range(4):
                        stats(h * 4 + e, GT, P, xs[e], s_xs[e], h * 16 + 16)
                stats(GROUPS, 1, LAST, xs[0], s_xs[0], 64)
                dve.wait_ge(s_stat, TILES)
                step(nc.vector.tensor_tensor(a1[:, :], st[:, :, 1], st[:, :, 4], ALU.add), False)
                step(nc.vector.tensor_tensor(a2[:, :], st[:, :, 1], st[:, :, 4], ALU.subtract), False)
                step(nc.vector.tensor_tensor(a3[:, :], st[:, :, 2], st[:, :, 5], ALU.add))
                step(nc.vector.tensor_scalar(mean[:, :], a1[:, :], 0.5, None, ALU.mult), False)
                step(nc.vector.scalar_tensor_tensor(a2[:, :], a2[:, :], 0.25, a2[:, :], ALU.mult, ALU.mult))
                step(nc.vector.scalar_tensor_tensor(va[:, :], a3[:, :], 1.0 / NF, a2[:, :], ALU.mult, ALU.add))
                step(nc.vector.tensor_scalar(va[:, :], va[:, :], EPS, None, ALU.add))
                dve.sem_inc(s_ln, 1)
                dve.wait_ge(s_sqrt, 1)
                step(nc.vector.reciprocal(a1[:, :], sd[:, :]))
                step(nc.vector.tensor_tensor(a1[:, :], va[:, :], a1[:, :], ALU.mult))
                step(nc.vector.tensor_tensor(a1[:, :], a1[:, :], sd[:, :], ALU.add))
                step(nc.vector.tensor_scalar(a1[:, :], a1[:, :], 0.5, None, ALU.mult))
                step(nc.vector.reciprocal(rstd[:, :], a1[:, :]))
                step(nc.vector.scalar_tensor_tensor(nmr[:, :], mean[:, :], -1.0, rstd[:, :], ALU.mult, ALU.mult))
                dve.sem_inc(s_ln, 1)

                def edge_chunk(c, b, g):
                    X, m, o, oprev = xb[b], mx[b % MB], ob[b % OB], ob[(b + 1) % OB]
                    dve.wait_ge(s_mul, c + 1)
                    dve.wait_ge(s_pen, c + 1)
                    nc.vector.tensor_tensor(m[:, :, 0, :], m[:, :, 0, :], m[:, :, 1, :], ALU.max).then_inc(s_tree, 1)
                    nc.vector.tensor_tensor(m[:, :, 2, :], m[:, :, 2, :], X[:, :, 3, :], ALU.max).then_inc(s_tree, 1)
                    xp = X[:, :, :, :].rearrange("p q (h two) f -> p q h two f", two=2)
                    for h in range(2):
                        ins = nc.vector.tensor_tensor(X[:, :, 2 * h, :], X[:, :, 2 * h, :], X[:, :, 2 * h + 1, :], ALU.add)
                        ins.then_inc(s_pairs, 1)
                    dve.wait_ge(s_tree, c * 4 + 2)
                    nc.vector.tensor_tensor(m[:, :, 0, :], m[:, :, 0, :], m[:, :, 2, :], ALU.max).then_inc(s_tree, 1)
                    dve.wait_ge(s_pairs, c * 2 + 2)
                    nc.vector.tensor_tensor(X[:, :, 0, :], X[:, :, 0, :], X[:, :, 2, :], ALU.add).then_inc(s_tree, 1)
                    if not isinstance(c, int) or c >= OB:
                        dve.wait_ge(s_dump[b % OB], g * 32 + (b // OB) * 16)
                    dve.wait_ge(s_tree, c * 4 + 4)
                    for q in range(TQ):
                        prev = oprev[:, TQ - 1, :] if q == 0 else o[:, q - 1, :]
                        dve.wait_ge(s_max, c * TQ + q + 1)
                        nc.vector.scalar_tensor_tensor(o[:, q, 0:EF], prev[:, 0:EF], mQ[:, bass.ds(c * TQ + q, 1)],
                                                       m[:, q, 0, :], ALU.min, ALU.max).then_inc(s_max, 1)
                        dve.wait_ge(s_sum, c * TQ + q + 1)
                        nc.vector.scalar_tensor_tensor(o[:, q, EF:AGG], prev[:, EF:AGG], kQ[:, bass.ds(c * TQ + q, 1)],
                                                       X[:, q, 0, :], ALU.mult, ALU.add).then_inc(s_sum, 1)

                def key_norm(g, nt, rows):
                    dve.wait_ge(s_sq, g * (3 * GT) + 3 * nt)
                    nc.vector.tensor_scalar(rk[0:rows, 0:nt], k2s[0:rows, 0:nt], 1e-7, None, ALU.add).then_inc(s_rk, 1)
                    dve.wait_ge(s_rk, g * 2 + 1)
                    nc.vector.reciprocal(rk[0:rows, 0:nt], rk[0:rows, 0:nt]).then_inc(s_rk, 1)

                for b in range(XB):
                    edge_chunk(b, b, 0)
                dve.wait_ge(s_csum, TILES)
                step(nc.vector.tensor_scalar(ridx[:, :], csum[:, :], float(SIDE), 0.5, ALU.add, ALU.mult))
                step(nc.vector.tensor_scalar(ridx[:, :], ridx[:, :], float(SIDE - 1), None, ALU.min))
                step(nc.vector.tensor_scalar(ridxi[:, :], ridx[:, :], 1.0, None, ALU.add))
                dve.sem_inc(s_ridx, 1)
                key_norm(0, GT, P)
                with dve.Fori(1, GROUPS) as g:
                    for b in range(XB):
                        edge_chunk(g * XB + b, b, g)
                    key_norm(g, GT, P)
                edge_chunk(CHUNKS - 1, 0, 12)
                key_norm(GROUPS, 1, LAST)

                step(nc.vector.tensor_scalar(diag[:, :], ident[:, :], keepc[:, 0:1], None, ALU.mult))
                dve.sem_inc(s_vc, 1)
                dve.wait_ge(s_pc, 1)
                step(nc.vector.tensor_copy(cT[:, 0, :], psC[0:EF, 2 * P:3 * P]), False)
                step(nc.vector.tensor_copy(cT[:, 2, :], psC[0:EF, 0:P]), False)
                step(nc.vector.tensor_copy(cT[:, 3, :], psC[0:EF, P:2 * P]))
                step(nc.vector.tensor_scalar(cT[:, 1, :], cT[:, 0, :], 0.5, 2.0, ALU.subtract, ALU.mult))
                step(nc.vector.tensor_scalar(cT[:, 1, :], cT[:, 1, :], FMAX, None, ALU.mult))
                step(nc.vector.tensor_tensor_scan(cs[:, 0, :], cT[:, 1, :], cT[:, 2, :], -FMAX, ALU.min, ALU.max), False)
                step(nc.vector.tensor_tensor_scan(cs[:, 1, :], cT[:, 0, :], cT[:, 3, :], 0.0, ALU.mult, ALU.add))
                dve.sem_inc(s_vc, 1)
                dve.wait_ge(s_pc, 2)
                step(nc.vector.tensor_copy(cr[:, 0:EF], psT[0][:, 0:EF]), False)
                step(nc.vector.tensor_copy(cr[:, EF:AGG], psT[0][:, P:P + EF]))
                dve.sem_inc(s_vc, 1)

                dve.wait_ge(s_at, 2)
                step(nc.vector.tensor_scalar(kcol[:, 2:4], kcol[:, 0:2], 1e-12, float(np.sqrt(float(NODES))), ALU.max, ALU.mult))
                step(nc.vector.reciprocal(kcol[:, 4:6], kcol[:, 2:4]))
                dve.wait_ge(s_pt, 4)
                for c in range(KF):
                    step(nc.vector.tensor_scalar(M[:, c, :], psQ[0][:, c * NF:(c + 1) * NF], kcol[:, 4 + c:5 + c], None, ALU.mult), False)
                    step(nc.vector.tensor_copy(WvoI[:, c, :], psQ[1][:, c * NF:(c + 1) * NF]))
                for c in range(KF):
                    w_ = WvoI[:, c, c * P:(c + 1) * P]
                    step(nc.vector.tensor_tensor(w_, w_, ident[:, :], ALU.add), False)
                step(nc.vector.tensor_tensor(b2r[0:1, 0, :], b2r[0:1, 0, :], b2r[0:1, 1, :], ALU.add))
                step(nc.vector.tensor_tensor(brow[0:1, :], b2r[0:1, 0, :], psR[0:1, 0:NF], ALU.add))
                dve.wait_ge(s_at, 3)
                step(nc.vector.tensor_scalar(a1[:, :], q2s[:, :], 1e-7, None, ALU.add))
                step(nc.vector.reciprocal(a2[:, :], a1[:, :]))
                step(nc.vector.tensor_tensor(a3[:, :], sd[:, :], a2[:, :], ALU.mult))
                step(nc.vector.tensor_scalar(a3[:, :], a3[:, :], 1e-12, None, ALU.max))
                step(nc.vector.reciprocal(a3[:, :], a3[:, :]))
                step(nc.vector.tensor_tensor(rq[:, :], a3[:, :], a2[:, :], ALU.mult))

                dve.wait_ge(s_fs, TILES)
                step(nc.vector.tensor_scalar(a1[:, :], fsum[:, :], float(SIDE), 0.5, ALU.add, ALU.mult))
                step(nc.vector.scalar_tensor_tensor(Eend[:, :], ridx[:, :], float(SIDE), a1[:, :], ALU.mult, ALU.add))
                dve.sem_inc(s_end, 1)
                dve.wait_ge(s_beg, 16)
                step(nc.vector.tensor_tensor(a1[:, :], Eend[:, :], Sbeg[:, :], ALU.subtract))
                step(nc.vector.tensor_scalar(has[:, :], a1[:, :], 0.0, None, ALU.is_gt))
                step(nc.vector.tensor_scalar(a1[:, :], a1[:, :], 1.0, None, ALU.max))
                step(nc.vector.reciprocal(rcnt[:, :], a1[:, :]))
                step(nc.vector.tensor_scalar(a1[:, :], Eend[:, :], 1.0, 0.0, ALU.subtract, ALU.max))
                step(nc.vector.tensor_copy(ai[:, :], a1[:, :]))
                step(nc.vector.tensor_scalar(iRaw, ai[:, :], 2, None, ALU.logical_shift_right))
                step(nc.vector.tensor_copy(a2[:, :], iRaw))
                step(nc.vector.scalar_tensor_tensor(a3[:, :], a2[:, :], -4.0, a1[:, :], ALU.mult, ALU.add))
                step(nc.vector.tensor_scalar(a3[:, :], a3[:, :], 3.0, None, ALU.is_equal))
                for i in range(3):
                    step(nc.vector.tensor_scalar(a4[:, :], a2[:, :], 4.0, float(i), ALU.mult, ALU.add))
                    step(nc.vector.tensor_tensor(a5[:, :], a4[:, :], a1[:, :], ALU.is_le))
                    step(nc.vector.tensor_tensor(a4[:, :], a4[:, :], Sbeg[:, :], ALU.is_ge))
                    step(nc.vector.tensor_tensor(a4[:, :], a4[:, :], a5[:, :], ALU.mult))
                    step(nc.vector.tensor_tensor(a4[:, :], a4[:, :], has[:, :], ALU.mult))
                    step(nc.vector.tensor_scalar(a5[:, :], a3[:, :], -1.0, 1.0, ALU.mult, ALU.add))
                    step(nc.vector.tensor_tensor(kSel[:, i, :], a4[:, :], a5[:, :], ALU.mult))
                step(nc.vector.tensor_tensor(a2[:, :], a2[:, :], a3[:, :], ALU.add))
                step(nc.vector.tensor_scalar(a4[:, :], a2[:, :], 4.0, -1.0, ALU.mult, ALU.add))
                step(nc.vector.tensor_tensor(a4[:, :], Sbeg[:, :], a4[:, :], ALU.is_le))
                step(nc.vector.tensor_tensor(kSel[:, 3, :], a4[:, :], has[:, :], ALU.mult))
                step(nc.vector.tensor_scalar(a2[:, :], a2[:, :], 1.0, 0.0, ALU.subtract, ALU.max))
                step(nc.vector.tensor_copy(iScan, a2[:, :]))
                step(nc.vector.tensor_scalar(a3[:, :], a2[:, :], 1.0 / Q, None, ALU.mult))
                step(nc.vector.tensor_copy(ai[:, :], a3[:, :]))
                step(nc.vector.tensor_copy(a3[:, :], ai[:, :]))
                step(nc.vector.scalar_tensor_tensor(a4[:, :], a3[:, :], -float(Q), a2[:, :], ALU.mult, ALU.add))
                step(nc.vector.tensor_scalar(a5[:, :], a4[:, :], 0.0, None, ALU.is_lt))
                step(nc.vector.tensor_tensor(a3[:, :], a3[:, :], a5[:, :], ALU.subtract))
                step(nc.vector.tensor_scalar(a5[:, :], a4[:, :], float(Q), None, ALU.is_ge))
                step(nc.vector.tensor_tensor(a3[:, :], a3[:, :], a5[:, :], ALU.add))
                step(nc.vector.tensor_scalar(a4[:, :], a3[:, :], float(R), None, ALU.mult))
                step(nc.vector.tensor_tensor(a4[:, :], Sbeg[:, :], a4[:, :], ALU.is_lt))
                step(nc.vector.tensor_tensor(kSel[:, 4, :], a4[:, :], has[:, :], ALU.mult))
                step(nc.vector.tensor_scalar(a3[:, :], a3[:, :], 1.0, 0.0, ALU.subtract, ALU.max))
                step(nc.vector.tensor_copy(iCarry, a3[:, :]))
                step(nc.vector.tensor_scalar(mSel[:, :, :], kSel[:, :, :], 0.5, 2.0, ALU.subtract, ALU.mult))
                step(nc.vector.tensor_scalar(mSel[:, :, :], mSel[:, :, :], FMAX, None, ALU.mult))

            @block.scalar
            def _(act):
                act.dma_start(crow[0:1, :], rows_v[1:SIDE + 1, SIDE - 1:SIDE].rearrange("a b -> b a"), allow_slow_non_contiguous=True).then_inc(s_crow, 16)
                act.dma_start(Wqk[:, :, :], Wqkv[:, 0:2 * NF].rearrange("(c p) n -> p c n", p=P)).then_inc(s_wload, 16)
                act.dma_start(Wv[:, :, :], Wqkv[:, 2 * NF:3 * NF].rearrange("(c p) n -> p c n", p=P)).then_inc(s_wload, 16)
                act.dma_start(Wo[:, :, :], Wout.rearrange("(c p) n -> p c n", p=P)).then_inc(s_wload, 16)
                act.dma_start(bqk[0:1, :], bqkv.rearrange("(a b) -> a b", a=1)).then_inc(s_wload, 16)
                act.dma_start(bv[:, :], bqkv[2 * NF:3 * NF].rearrange("(c p) -> p c", p=P), allow_slow_non_contiguous=True).then_inc(s_wload, 16)
                act.dma_start(b2r[0:1, 0, :], b2.rearrange("(a b) -> a b", a=1)).then_inc(s_wload, 16)
                act.dma_start(b2r[0:1, 1, :], bout.rearrange("(a b) -> a b", a=1)).then_inc(s_wload, 16)
                act.dma_start(krow[0:1, 0:1], b2[0:1].rearrange("(a b) -> a b", a=1)).then_inc(s_wload, 16)
                for e in range(4):
                    act.dma_start(xs[e][:, :, :], x_group(e, GT, P)).then_inc(s_xs[e], 16)
                with act.Fori(1, GROUPS // 4) as h:
                    for e in range(4):
                        act.wait_ge(s_stat, h * (4 * GT) + e * GT - 3 * GT)
                        act.dma_start(xs[e][:, :, :], x_group(h * 4 + e, GT, P)).then_inc(s_xs[e], 16)
                act.wait_ge(s_stat, (GROUPS - 3) * GT)
                act.dma_start(xs[0][0:LAST, 0:1, :], x_group(GROUPS, 1, LAST)).then_inc(s_xs[0], 16)
                act.wait_ge(s_stat, TILES)
                act.dma_start(xg[:, :, :], x_group(0, GT, P)).then_inc(s_xg, 16)
                act.wait_ge(s_ln, 1)
                nc.scalar.sqrt(sd[:, :], va[:, :]).then_inc(s_sqrt, 1)
                act.wait_ge(s_pc0, 1)
                def coarse(t, b):
                    if not isinstance(t, int) or t >= 4:
                        act.wait_ge(s_csum, t - 3)
                    nc.scalar.activation(jc[b][:, :], psC[:, 0:SIDE], ACT.Sign, bias=nhalf[:, bass.ds(t, 1)], scale=-1.0,
                                         accum_out=csum[:, bass.ds(t, 1)]).then_inc(s_csum, 1)
                for t in range(4):
                    coarse(t, t)
                with act.Fori(1, TILES // 4) as h:
                    for b in range(4):
                        coarse(h * 4 + b, b)
                coarse(TILES - 1, 0)
                act.wait_ge(s_csum, TILES)

                def fine(t, b, n):
                    if not isinstance(t, int) or t >= 4:
                        act.wait_ge(s_fs, t - 3)
                    act.wait_ge(s_fr[b], n)
                    nc.scalar.activation(jc[b % 4][:, :], fr[b][:, :], ACT.Sign, bias=nhalf[:, bass.ds(t, 1)], scale=-1.0,
                                         accum_out=fsum[:, bass.ds(t, 1)]).then_inc(s_fs, 1)

                act.wait_ge(s_ln, 2)

                def node_group(g, nt, rows, first):
                    act.wait_ge(s_xg, g * 16 + 16)
                    if not first:
                        act.wait_ge(s_kx, g * GT)
                    for t in range(nt):
                        col = bass.ds(g * GT + t, 1)
                        nc.scalar.activation(xn[0:rows, t, :], xg[0:rows, t, :], ACT.Identity, bias=nmr[0:rows, col],
                                             scale=rstd[0:rows, col]).then_inc(s_xn, 1)
                    if nt == GT:
                        act.wait_ge(s_xn, g * GT + GT)
                        if isinstance(g, int) and g == GROUPS - 1:
                            act.dma_start(xg[0:LAST, 0:1, :], x_group(GROUPS, 1, LAST)).then_inc(s_xg, 16)
                        else:
                            act.dma_start(xg[:, :, :], x_group(g + 1, GT, P)).then_inc(s_xg, 16)
                    if not first:
                        act.wait_ge(s_xTo, g * 16)
                        act.wait_ge(s_qTo, g * 16)
                    for t in range(nt):
                        act.wait_ge(s_tr, g * (2 * GT) + t + 1)
                        nc.scalar.copy(xT[:, :, t * P:t * P + rows],
                                       psT[t % 2][:, 0:2 * P].rearrange("p (c n) -> p c n", c=KF)[:, :, 0:rows]).then_inc(s_evac, 1)
                    act.wait_ge(s_evac, g * (2 * GT) + nt)
                    act.dma_start(xT_d[bass.ds(g, 1), :, :, 0:nt * rows].rearrange("o p c n -> p (o c) n"), xT[:, :, 0:nt * rows]).then_inc(s_xTo, 16)
                    for t in range(nt):
                        act.wait_ge(s_qk, g * GT + t + 1)
                        col = bass.ds(g * GT + t, 1)
                        nc.scalar.activation(q2[0:rows, t, :], psQ[t % 2][0:rows, 0:NF], ACT.Square,
                                             accum_out=q2s[0:rows, col]).then_inc(s_sq, 1)
                        nc.scalar.activation(k2[0:rows, t, :], psQ[t % 2][0:rows, NF:2 * NF], ACT.Square,
                                             accum_out=k2s[0:rows, t:t + 1]).then_inc(s_sq, 1)
                        act.wait_ge(s_sq, g * (3 * GT) + 3 * t + 2)
                        nc.scalar.activation(junk[0:rows, 0:NF], q2[0:rows, t, :], ACT.Square,
                                             accum_out=q4s[0:rows, col]).then_inc(s_sq, 1)
                    for t in range(nt):
                        act.wait_ge(s_tr, g * (2 * GT) + nt + t + 1)
                        nc.scalar.copy(qT[:, :, t * P:t * P + rows],
                                       psT[(nt + t) % 2][:, 0:2 * P].rearrange("p (c n) -> p c n", c=KF)[:, :, 0:rows]).then_inc(s_evac, 1)
                    act.wait_ge(s_evac, g * (2 * GT) + 2 * nt)
                    act.dma_start(qT_d[bass.ds(g, 1), :, :, 0:nt * rows].rearrange("o p c n -> p (o c) n"), qT[:, :, 0:nt * rows]).then_inc(s_qTo, 16)
                    act.wait_ge(s_rk, g * 2 + 2)
                    for t in range(nt):
                        nc.scalar.activation(kc[0:rows, t, 0:NF], k2[0:rows, t, :], ACT.Copy, scale=rk[0:rows, t:t + 1]).then_inc(s_act, 1)
                        nc.scalar.activation(kc[0:rows, t, NF:2 * NF], k2[0:rows, t, :], ACT.Square, scale=rk[0:rows, t:t + 1]).then_inc(s_kk, 1)

                for g in range(4):
                    node_group(g, GT, P, g == 0)
                    if g >= 2:
                        for b in range(4):
                            fine(g * 4 - 8 + b, (g % 2) * 4 + b, 16)
                with act.Fori(2, 5) as h:
                    for e in range(2):
                        node_group(h * 2 + e, GT, P, False)
                        for b in range(4):
                            fine(h * 8 + e * 4 - 8 + b, e * 4 + b, h * 16)
                for g in range(10, 12):
                    node_group(g, GT, P, False)
                    for b in range(4):
                        fine(g * 4 - 8 + b, (g % 2) * 4 + b, 80)
                node_group(GROUPS, 1, LAST, False)
                for t in range(40, TILES):
                    fine(t, t % 8, 16 * (t // 8) + 16)

                act.wait_ge(s_kx, TILES)
                nc.scalar.copy(krow[0:1, :], psR[0:1, :]).then_inc(s_act, 1)
                for c in range(KF):
                    nc.scalar.copy(kxT[:, c, :], psKx[c][:, 0:NF]).then_inc(s_act, 1)
                act.wait_ge(s_act, TILES + 1 + KF)
                act.sem_inc(s_at, 1)
                act.wait_ge(s_pt, 1)
                nc.scalar.sqrt(kcol[:, 0:2], psC[:, 510:512]).then_inc(s_at, 1)
                nc.scalar.sqrt(sd[:, :], q4s[:, :]).then_inc(s_at, 1)
                act.wait_ge(s_pt, 2)
                nc.scalar.copy(WvT[:, :, :], psT[1][:, :].rearrange("p (c n) -> p c n", c=KF)).then_inc(s_at, 1)
                act.wait_ge(s_pt, 3)
                nc.scalar.copy(kvT[:, :, :], psQ[0][:, :].rearrange("p (c n) -> p c n", c=KF)).then_inc(s_at, 1)
                act.wait_ge(s_xTo, 16 * (GROUPS + 1))
                act.wait_ge(s_qTo, 16 * (GROUPS + 1))

            @block.tensor
            def _(pe):
                pe.wait_ge(s_const, 2)
                pe.wait_ge(s_cbc, 1)
                nc.tensor.matmul(psC[:, 0:SIDE], ones[0:1, :], crowf[0:1, :], start=True, stop=True).then_inc(s_pc0, 1)
                pe.wait_ge(s_wq, 1)

                def node_group(g, nt, rows, first):
                    for t in range(nt):
                        pe.wait_ge(s_xn, g * GT + t + 1)
                        if not first or t >= 2:
                            pe.wait_ge(s_evac, g * (2 * GT) + t - 1)
                        for c in range(KF):
                            ins = nc.tensor.transpose(psT[t % 2][:, c * P:c * P + rows], xn[0:rows, t, c * P:(c + 1) * P],
                                                      ident[0:rows, 0:rows])
                        ins.then_inc(s_tr, 1)
                    for t in range(nt):
                        pe.wait_ge(s_evac, g * (2 * GT) + t + 1)
                        if not first or t >= 2:
                            pe.wait_ge(s_sq, g * (3 * GT) + 3 * t - 4)
                        for c in range(KF):
                            nc.tensor.matmul(psQ[t % 2][0:rows, :], xT[:, c, t * P:t * P + rows], Wqk[:, c, :],
                                             start=(c == 0), stop=False)
                        nc.tensor.matmul(psQ[t % 2][0:rows, :], ones[0:1, 0:rows], bqk[0:1, 0:2 * NF],
                                         start=False, stop=True).then_inc(s_qk, 1)
                    for t in range(nt):
                        pe.wait_ge(s_sq, g * (3 * GT) + 3 * t + 1)
                        pe.wait_ge(s_evac, g * (2 * GT) + nt + t - 1)
                        for c in range(KF):
                            ins = nc.tensor.transpose(psT[(nt + t) % 2][:, c * P:c * P + rows], q2[0:rows, t, c * P:(c + 1) * P],
                                                      ident[0:rows, 0:rows])
                        ins.then_inc(s_tr, 1)

                def key_group(g, nt, rows, start, stop):
                    for t in range(nt):
                        pe.wait_ge(s_kk, g * GT + t + 1)
                        pe.wait_ge(s_act, g * GT + t + 1)
                        s, e = start and t == 0, stop and t == nt - 1
                        for c in range(KF):
                            nc.tensor.matmul(psKx[c][:, 0:NF], xn[0:rows, t, c * P:(c + 1) * P], kc[0:rows, t, 0:NF], start=s, stop=e)
                        nc.tensor.matmul(psR[0:1, :], ones[0:rows, 0:1], kc[0:rows, t, :], start=s, stop=e).then_inc(s_kx, 1)

                node_group(0, GT, P, True)
                key_group(0, GT, P, True, False)
                with pe.Fori(1, GROUPS) as g:
                    node_group(g, GT, P, False)
                    key_group(g, GT, P, False, False)
                node_group(GROUPS, 1, LAST, False)
                key_group(GROUPS, 1, LAST, False, True)

                pe.wait_ge(s_evac, GROUPS * 2 * GT + 2)
                pe.wait_ge(s_sq, TILES * 3)
                pe.wait_ge(s_at, 1)
                pe.wait_ge(s_csum, TILES)
                for c in range(KF):
                    ins = nc.tensor.matmul(psC[:, 510 + c:511 + c], krow[0:1, NF + c * P:NF + (c + 1) * P], ones[0:1, 0:1],
                                           start=True, stop=True)
                ins.then_inc(s_pt, 1)
                for c in range(KF):
                    for d in range(KF):
                        ins = nc.tensor.transpose(psT[1][:, d * NF + c * P:d * NF + (c + 1) * P], Wv[:, c, d * P:(d + 1) * P], ident[:, :])
                ins.then_inc(s_pt, 1)
                for d in range(KF):
                    o = psQ[0][:, d * NF:(d + 1) * NF]
                    for c in range(KF):
                        nc.tensor.matmul(o, Wv[:, c, d * P:(d + 1) * P], kxT[:, c, :], start=(c == 0), stop=False)
                    ins = nc.tensor.matmul(o, bqk[0:1, 2 * NF + d * P:2 * NF + (d + 1) * P], krow[0:1, 0:NF], start=False, stop=True)
                ins.then_inc(s_pt, 1)
                pe.wait_ge(s_at, 4)
                for c in range(KF):
                    for d in range(KF):
                        nc.tensor.matmul(psQ[1][:, c * NF:(c + 1) * NF], WvT[:, d, c * P:(c + 1) * P], Wo[:, d, :],
                                         start=(d == 0), stop=(d == KF - 1))
                for d in range(KF):
                    nc.tensor.matmul(psR[0:1, 0:NF], bv[:, d:d + 1], Wo[:, d, :], start=(d == 0), stop=(d == KF - 1))
                pe.wait_ge(s_at, 5)
                for c in range(KF):
                    for d in range(KF):
                        ins = nc.tensor.matmul(psQ[0][:, c * NF:(c + 1) * NF], kvT[:, d, c * P:(c + 1) * P], Wo[:, d, :],
                                               start=(d == 0), stop=(d == KF - 1))
                ins.then_inc(s_pt, 1)
                pe.wait_ge(s_max, CHUNKS * TQ + 1)
                pe.wait_ge(s_sum, CHUNKS * TQ + 1)
                pe.wait_ge(s_vc, 1)
                nc.tensor.transpose(psC[0:EF, 0:P], ob[0][:, TQ - 1, 0:EF], ident[:, :])
                nc.tensor.transpose(psC[0:EF, P:2 * P], ob[0][:, TQ - 1, EF:AGG], ident[:, :])
                nc.tensor.matmul(psC[0:EF, 2 * P:3 * P], ones[:, 0:EF], diag[:, :], start=True, stop=True).then_inc(s_pc, 1)
                pe.wait_ge(s_vc, 2)
                for h in range(2):
                    ins = nc.tensor.transpose(psT[0][:, h * P:h * P + EF], cs[:, h, :], ident[0:EF, 0:EF])
                ins.then_inc(s_pc, 1)

        with ExitStack() as ctx:
            sb = lambda n, s, d=f32: ctx.enter_context(nc.sbuf_tensor(n, s, d))
            ps = lambda n, s: ctx.enter_context(nc.psum_tensor(n, s, f32))
            sem = lambda n: ctx.enter_context(nc.semaphore(n))
            W1x = sb("W1x", [P, KF, HID])
            W1a = sb("W1a", [EF, 3, HID])
            W1u = sb("W1u", [GF, HID])
            W2s = sb("W2s", [P, KH, NF])
            u0 = sb("u0", [GF, 1])
            b1c = sb("b1c", [P, KH])
            wrow = sb("wrow", [1, NF + 1])
            wrb = sb("wrb", [P, NF + 1])
            xT2 = [sb(f"xT2{i}", [P, KF, GT * P]) for i in range(2)]
            qT2 = [sb(f"qT2{i}", [P, KF, GT * P]) for i in range(2)]
            xg2 = [sb(f"xg2{i}", [P, GT, NF]) for i in range(2)]
            graw = [sb(f"graw{i}", [P, GT, 4 * EF]) for i in range(2)]
            gscan = [sb(f"gscan{i}", [P, GT, AGG]) for i in range(2)]
            gcar = [sb(f"gcar{i}", [P, GT, AGG]) for i in range(2)]
            ic = [sb(f"ic{i}", [P, 3, GT], i32) for i in range(2)]
            agg = sb("agg", [P, GT, 3 * EF])
            aggT = sb("aggT", [EF, 3, GT * P])
            hT = sb("hT", [P, KH, GT * P])
            x2 = sb("x2", [P, GT, NF])
            yr = sb("yr", [P, GT, YROW])
            prod = sb("prod", [P, NF])
            st2 = sb("st2", [P, GT, 6])
            mean2 = sb("mean2", [P, GT])
            t2 = sb("t2", [P, GT])
            wst = sb("wst", [P, GT])
            va2 = sb("va2", [P, GT])
            sd2 = sb("sd2", [P, GT])
            t1 = sb("t1", [P, GT])
            rs2 = sb("rs2", [P, GT])
            psA = [ps(f"psA{i}", [P, 512]) for i in range(2)]
            psH = [ps(f"psH{i}", [P, 512]) for i in range(3)]
            psO = [ps(f"psO{i}", [P, 512]) for i in range(2)]
            s_w = sem("b_w")
            s_u = sem("b_u")
            s_b1 = sem("b_b1")
            s_ld = [sem(f"b_ld{i}") for i in range(2)]
            s_ga = [sem(f"b_ga{i}") for i in range(2)]
            s_am = sem("b_am")
            s_ic = sem("b_ic")
            s_turn = sem("b_turn")
            s_as = sem("b_as")
            s_A = sem("b_A")
            s_ev = sem("b_ev")
            s_h = sem("b_h")
            s_re = sem("b_re")
            s_o = sem("b_o")
            s_x2a = sem("b_x2a")
            s_x2 = sem("b_x2")
            s_ln2 = sem("b_ln2")
            s_va = sem("b_va")
            s_sq2 = sem("b_sq2")
            s_fin = sem("b_fin")
            s_st = sem("b_st")
            s_wg = sem("b_wg")
            raw_v = edges.rearrange("(q i) f -> q (i f)", i=4)
            NVA = 12
            NFIN = 4

            def shape(g):
                return (1, LAST) if isinstance(g, int) and g == GROUPS else (GT, P)

            block = ctx.enter_context(nc.Block())

            @block.sync
            def _(sp):
                sp.dma_start(W1x[:, :, :], W1[0:NF, :].rearrange("(c p) n -> p c n", p=P)).then_inc(s_w, 16)
                sp.dma_start(W1a[:, :, :], W1[NF:NF + 3 * EF, :].rearrange("(c p) n -> p c n", p=EF)).then_inc(s_w, 16)
                sp.dma_start(W1u[:, :], W1[NF + 3 * EF:NF + 3 * EF + GF, :]).then_inc(s_w, 16)
                sp.dma_start(W2s[:, :, :], W2.rearrange("(c p) n -> p c n", p=P)).then_inc(s_w, 16)
                sp.dma_start(u0[:, :], u[0:1, :].rearrange("a b -> b a")).then_inc(s_w, 16)
                sp.dma_start(b1c[:, :], b1.rearrange("(c p) -> p c", p=P), allow_slow_non_contiguous=True).then_inc(s_w, 16)
                sp.dma_start(wrow[0:1, 0:NF], wr.rearrange("a b -> b a")).then_inc(s_w, 16)
                sp.dma_start(wrow[0:1, NF:NF + 1], br.rearrange("(a b) -> a b", a=1)).then_inc(s_w, 16)

                def load(g, e):
                    nt, rows = shape(g)
                    n = nt * rows
                    sp.dma_start(xT2[e][:, :, 0:n], xT_d[bass.ds(g, 1), :, :, 0:n].rearrange("o p c n -> p (o c) n")).then_inc(s_ld[e], 16)
                    sp.dma_start(qT2[e][:, :, 0:n], qT_d[bass.ds(g, 1), :, :, 0:n].rearrange("o p c n -> p (o c) n")).then_inc(s_ld[e], 16)
                    sp.dma_start(xg2[e][0:rows, 0:nt, :],
                                 x[bass.ds(g * GT * P, n), :].rearrange("(t p) f -> p t f", p=rows)).then_inc(s_ld[e], 16)

                def store(g):
                    nt, rows = shape(g)
                    sp.wait_ge(s_fin, g * (GT * NFIN) + nt * NFIN)
                    r0 = bass.ds(g * GT * P, nt * rows)
                    sp.dma_start(yrow_d[r0, :].rearrange("(t p) f -> p t f", p=rows), yr[0:rows, 0:nt, :]).then_inc(s_st, 16)
                    sp.dma_start(out[r0, :].rearrange("(t p) f -> p t f", p=rows), yr[0:rows, 0:nt, NF:2 * NF]).then_inc(s_st, 16)

                def turn(g, e):
                    nt, rows = shape(g)
                    if not isinstance(g, int) or g >= 1:
                        store(g - 1)
                    if not isinstance(g, int) or g + 2 <= GROUPS:
                        sp.wait_ge(s_o, g * GT + nt)
                        sp.wait_ge(s_x2, g * GT + nt)
                        load(g + 2, e)

                load(0, 0)
                load(1, 1)
                for g in range(2):
                    turn(g, g)
                with sp.Fori(1, 5) as h:
                    for e in range(2):
                        turn(h * 2 + e, e)
                for g in range(10, 13):
                    turn(g, g % 2)
                store(GROUPS)
                sp.wait_ge(s_st, 32 * (GROUPS + 1))

            @block.gpsimd
            def _(pool):
                def gather(g, e):
                    nt, rows = shape(g)
                    if not isinstance(g, int) or g >= 2:
                        pool.wait_ge(s_am, g * (6 * GT) - 6 * GT)
                        pool.wait_ge(s_as, g * (6 * GT) - 6 * GT)
                    nc.gpsimd.tensor_copy(ic[e][0:rows, :, 0:nt], idx[0:rows, :, bass.ds(g * GT, nt)]).then_inc(s_ic, 1)
                    pool.wait_ge(s_ic, g + 1)
                    pool.sem_inc(s_turn, 1)
                    for t in range(nt):
                        for i, (buf, src) in enumerate(((graw, raw_v), (gscan, scan_d), (gcar, carry_d))):
                            nc.gpsimd.indirect_dma_start(
                                out=buf[e][0:rows, t, :], out_offset=None, in_=src,
                                in_offset=bass.IndirectOffsetOnAxis(ap=ic[e][0:rows, i, t:t + 1], axis=0)).then_inc(s_ga[e], 16)
                gather(0, 0)
                gather(1, 1)
                with pool.Fori(1, 6) as h:
                    for e in range(2):
                        gather(h * 2 + e, e)
                gather(GROUPS, 0)

            @block.vector
            def _(dve):
                def gathered(g, e, h):
                    nt, _r = shape(g)
                    dve.wait_ge(s_ga[e], h * (48 * GT) + 48 * nt)

                def aggregate(g, e, h):
                    nt, rows = shape(g)
                    gathered(g, e, h)
                    if not isinstance(g, int) or g >= 1:
                        dve.wait_ge(s_A, g * GT)
                    for t in range(nt):
                        col = bass.ds(g * GT + t, 1)
                        src = [graw[e][0:rows, t, i * EF:(i + 1) * EF] for i in range(3)]
                        mxs = src + [gscan[e][0:rows, t, 0:EF], gcar[e][0:rows, t, 0:EF]]
                        sms = src + [gscan[e][0:rows, t, EF:AGG], gcar[e][0:rows, t, EF:AGG]]
                        am, asum = agg[0:rows, t, EF:2 * EF], agg[0:rows, t, 0:EF]
                        for i in range(5):
                            mcol, kcol_ = mSel[0:rows, i, col], kSel[0:rows, i, col]
                            if i == 0:
                                nc.vector.tensor_scalar(am, mxs[0], mcol, None, ALU.min).then_inc(s_am, 1)
                                nc.vector.tensor_scalar(asum, sms[0], kcol_, None, ALU.mult).then_inc(s_as, 1)
                            else:
                                dve.wait_ge(s_am, g * (6 * GT) + 6 * t + i)
                                nc.vector.scalar_tensor_tensor(am, mxs[i], mcol, am, ALU.min, ALU.max).then_inc(s_am, 1)
                                dve.wait_ge(s_as, g * (6 * GT) + 6 * t + i)
                                nc.vector.scalar_tensor_tensor(asum, sms[i], kcol_, asum, ALU.mult, ALU.add).then_inc(s_as, 1)
                        dve.wait_ge(s_am, g * (6 * GT) + 6 * t + 5)
                        nc.vector.tensor_scalar(am, am, has[0:rows, col], None, ALU.mult).then_inc(s_am, 1)
                        dve.wait_ge(s_as, g * (6 * GT) + 6 * t + 5)
                        nc.vector.tensor_scalar(agg[0:rows, t, 2 * EF:3 * EF], asum, rcnt[0:rows, col], None, ALU.mult).then_inc(s_as, 1)

                def add_up(g, e):
                    nt, rows = shape(g)
                    for t in range(nt):
                        k = g * GT + t
                        dve.wait_ge(s_o, k + 1)
                        nc.vector.scalar_tensor_tensor(x2[0:rows, t, :], psO[t % 2][0:rows, NF:2 * NF], rq[0:rows, bass.ds(k, 1)],
                                                       xg2[e][0:rows, t, :], ALU.mult, ALU.add).then_inc(s_x2a, 1)
                        dve.wait_ge(s_x2a, k + 1)
                        nc.vector.tensor_tensor(x2[0:rows, t, :], x2[0:rows, t, :], psO[t % 2][0:rows, 0:NF], ALU.add).then_inc(s_x2, 1)
                        dve.wait_ge(s_x2, k + 1)
                        nc.vector.bn_stats(st2[0:rows, t, :], x2[0:rows, t, :]).then_inc(s_ln2, 1)
                    dve.wait_ge(s_ln2, g * GT + nt)
                    r, n = slice(0, rows), slice(0, nt)
                    nc.vector.tensor_tensor(mean2[r, n], st2[r, n, 1], st2[r, n, 4], ALU.add).then_inc(s_va, 1)
                    nc.vector.tensor_tensor(t1[r, n], st2[r, n, 1], st2[r, n, 4], ALU.subtract).then_inc(s_va, 1)
                    nc.vector.tensor_tensor(t2[r, n], st2[r, n, 2], st2[r, n, 5], ALU.add).then_inc(s_va, 1)
                    dve.wait_ge(s_va, g * NVA + 3)
                    nc.vector.tensor_scalar(mean2[r, n], mean2[r, n], 0.5, None, ALU.mult).then_inc(s_va, 1)
                    nc.vector.scalar_tensor_tensor(t1[r, n], t1[r, n], 0.25, t1[r, n], ALU.mult, ALU.mult).then_inc(s_va, 1)
                    dve.wait_ge(s_va, g * NVA + 5)
                    nc.vector.scalar_tensor_tensor(va2[r, n], t2[r, n], 1.0 / NF, t1[r, n], ALU.mult, ALU.add).then_inc(s_va, 1)
                    dve.wait_ge(s_va, g * NVA + 6)
                    nc.vector.tensor_scalar(va2[r, n], va2[r, n], EPS, None, ALU.add).then_inc(s_va, 1)

                def finish(g):
                    nt, rows = shape(g)
                    dve.wait_ge(s_sq2, g + 1)
                    r, n = slice(0, rows), slice(0, nt)
                    nc.vector.reciprocal(t1[r, n], sd2[r, n]).then_inc(s_va, 1)
                    dve.wait_ge(s_va, g * NVA + 8)
                    nc.vector.tensor_tensor(t1[r, n], va2[r, n], t1[r, n], ALU.mult).then_inc(s_va, 1)
                    dve.wait_ge(s_va, g * NVA + 9)
                    nc.vector.tensor_tensor(t1[r, n], t1[r, n], sd2[r, n], ALU.add).then_inc(s_va, 1)
                    dve.wait_ge(s_va, g * NVA + 10)
                    nc.vector.tensor_scalar(t1[r, n], t1[r, n], 0.5, None, ALU.mult).then_inc(s_va, 1)
                    dve.wait_ge(s_va, g * NVA + 11)
                    nc.vector.reciprocal(rs2[r, n], t1[r, n]).then_inc(s_va, 1)
                    dve.wait_ge(s_va, g * NVA + 12)
                    if not isinstance(g, int) or g >= 1:
                        dve.wait_ge(s_st, g * 32)
                    for t in range(nt):
                        k0 = g * (GT * NFIN) + t * NFIN
                        y = yr[r, t, 0:NF]
                        nc.vector.tensor_scalar(y, x2[r, t, :], mean2[r, t:t + 1], rs2[r, t:t + 1], ALU.subtract, ALU.mult).then_inc(s_fin, 1)
                        dve.wait_ge(s_fin, k0 + 1)
                        nc.vector.tensor_tensor(yr[r, t, NF:2 * NF], x2[r, t, :], y, ALU.add).then_inc(s_fin, 1)
                        nc.vector.tensor_tensor_reduce(out=prod[r, :], in0=y, in1=wrb[r, 0:NF], scale=1.0, scalar=wrb[r, NF:NF + 1],
                                                       op0=ALU.mult, op1=ALU.add, accum_out=wst[r, t:t + 1]).then_inc(s_fin, 1)
                        dve.wait_ge(s_fin, k0 + 3)
                        nc.vector.tensor_copy(yr[r, t, 2 * NF:YROW], wst[r, t:t + 1].broadcast_to([rows, YROW - 2 * NF])).then_inc(s_fin, 1)
                    nc.vector.tensor_copy(wgt[r, bass.ds(g * GT, nt)], wst[r, n]).then_inc(s_wg, 1)

                nc.vector.memset(wgt[:, :], 0.0).then_inc(s_u, 1)
                dve.wait_ge(s_b1, 2)
                nc.vector.tensor_tensor(b1c[:, :], b1c[:, :], psA[0][:, 0:KH], ALU.add).then_inc(s_u, 1)
                nc.vector.tensor_copy(wrb[:, :], psA[1][:, 0:NF + 1]).then_inc(s_u, 1)
                dve.wait_ge(s_u, 3)
                aggregate(0, 0, 0)

                def turn(g, e, h):
                    if not isinstance(g, int) or g < GROUPS:
                        aggregate(g + 1, 1 - e, h + e)
                    if not isinstance(g, int) or g >= 1:
                        finish(g - 1)
                    add_up(g, e)
                for g in range(2):
                    turn(g, g, 0)
                with dve.Fori(1, 5) as h:
                    for e in range(2):
                        turn(h * 2 + e, e, h)
                for g in range(10, 13):
                    turn(g, g % 2, g // 2)
                finish(GROUPS)

            @block.scalar
            def _(act):
                act.wait_ge(s_u, 3)

                def evac(g):
                    nt, rows = shape(g)
                    if not isinstance(g, int) or g >= 1:
                        act.wait_ge(s_h, g * KH)
                    for t in range(nt):
                        act.wait_ge(s_A, g * GT + t + 1)
                        nc.scalar.copy(aggT[:, :, t * P:t * P + rows],
                                       psA[t % 2][0:EF, 0:3 * P].rearrange("p (c n) -> p c n", c=3)[:, :, 0:rows]).then_inc(s_ev, 1)

                def turn(g):
                    nt, rows = shape(g)
                    n = nt * rows
                    for m in range(KH):
                        act.wait_ge(s_h, g * KH + m + 1)
                        if not isinstance(g, int) or g >= 1:
                            act.wait_ge(s_o, g * GT)
                        nc.scalar.activation(hT[:, m, 0:n], psH[m % 2][:, 0:n], ACT.Relu, bias=b1c[:, m:m + 1]).then_inc(s_re, 1)
                        if m == 3 and (not isinstance(g, int) or g >= 1):
                            root(g - 1)
                    if not isinstance(g, int) or g < GROUPS:
                        evac(g + 1)

                def root(g):
                    nt, rows = shape(g)
                    act.wait_ge(s_va, g * NVA + 7)
                    nc.scalar.sqrt(sd2[0:rows, 0:nt], va2[0:rows, 0:nt]).then_inc(s_sq2, 1)

                evac(0)
                turn(0)
                with act.Fori(1, 11) as g:
                    turn(g)
                turn(11)
                turn(12)
                root(GROUPS)

            @block.tensor
            def _(pe):
                pe.wait_ge(s_w, 16 * 8)
                for m in range(KH):
                    ins = nc.tensor.matmul(psA[0][:, m:m + 1], W1u[:, m * P:(m + 1) * P], u0[:, :], start=True, stop=True)
                ins.then_inc(s_b1, 1)
                nc.tensor.matmul(psA[1][:, 0:NF + 1], ones[0:1, :], wrow[0:1, :], start=True, stop=True).then_inc(s_b1, 1)
                pe.wait_ge(s_u, 3)

                def transposes(g):
                    nt, rows = shape(g)
                    for t in range(nt):
                        pe.wait_ge(s_am, g * (6 * GT) + 6 * t + 6)
                        pe.wait_ge(s_as, g * (6 * GT) + 6 * t + 6)
                        if not isinstance(g, int) or g * GT + t >= 2:
                            pe.wait_ge(s_ev, g * GT + t - 1)
                        for i in range(3):
                            ins = nc.tensor.transpose(psA[t % 2][0:EF, i * P:i * P + rows], agg[0:rows, t, i * EF:(i + 1) * EF],
                                                      ident[0:rows, 0:rows])
                        ins.then_inc(s_A, 1)

                def hidden(g, e, h):
                    nt, rows = shape(g)
                    n = nt * rows
                    pe.wait_ge(s_ld[e], h * 48 + 48)
                    pe.wait_ge(s_ev, g * GT + nt)
                    for m in range(KH):
                        if not isinstance(g, int) or g * KH + m >= 2:
                            pe.wait_ge(s_re, g * KH + m - 1)
                        o, w_ = psH[m % 2][:, 0:n], slice(m * P, (m + 1) * P)
                        for c in range(KF):
                            nc.tensor.matmul(o, W1x[:, c, w_], xT2[e][:, c, 0:n], start=(c == 0), stop=False)
                        for c in range(3):
                            ins = nc.tensor.matmul(o, W1a[:, c, w_], aggT[:, c, 0:n], start=False, stop=(c == 2))
                        ins.then_inc(s_h, 1)

                def output(g, e):
                    nt, rows = shape(g)
                    for t in range(nt):
                        if not isinstance(g, int) or g * GT + t >= 2:
                            pe.wait_ge(s_x2, g * GT + t - 1)
                        o, m_, cols = psO[t % 2][0:rows, 0:NF], psO[t % 2][0:rows, NF:2 * NF], slice(t * P, t * P + rows)
                        for c in range(KF):
                            nc.tensor.matmul(m_, qT2[e][:, c, cols], M[:, c, :], start=(c == 0), stop=(c == KF - 1))
                        nc.tensor.matmul(o, ones[0:1, 0:rows], brow[0:1, :], start=True, stop=False)
                        for c in range(KF):
                            nc.tensor.matmul(o, xT2[e][:, c, cols], WvoI[:, c, :], start=False, stop=False)
                        for m in range(KH):
                            if t == 0:
                                pe.wait_ge(s_re, g * KH + m + 1)
                            ins = nc.tensor.matmul(o, hT[:, m, cols], W2s[:, m, :], start=False, stop=(m == KH - 1))
                        ins.then_inc(s_o, 1)

                def turn(g, e, h):
                    hidden(g, e, h)
                    if not isinstance(g, int) or g < GROUPS:
                        transposes(g + 1)
                    output(g, e)
                transposes(0)
                for g in range(2):
                    turn(g, g, 0)
                with pe.Fori(1, 5) as h:
                    for e in range(2):
                        turn(h * 2 + e, e, h)
                for g in range(10, 13):
                    turn(g, g % 2, g // 2)

        with ExitStack() as ctx:
            sb = lambda n, s, d=f32: ctx.enter_context(nc.sbuf_tensor(n, s, d))
            ps = lambda n, s: ctx.enter_context(nc.psum_tensor(n, s, f32))
            sem = lambda n: ctx.enter_context(nc.semaphore(n))
            valid = sb("valid", [P, TILES])
            v = sb("v", [P, TILES])
            jk = sb("jk", [P, TILES])
            pref = sb("pref", [P, 1], i32)
            bit = sb("bit", [P, 1], i32)
            cand = sb("cand", [P, 1], i32)
            stp = sb("stp", [P, 1], i32)
            acc = sb("acc", [P, 4])
            sgn = sb("sgn", [P, 1])
            kk_ = sb("kk_", [P, 1])
            thr = sb("thr", [P, 1])
            gt = sb("gt", [P, TILES])
            eq = sb("eq", [P, TILES])
            both = sb("both", [P, 2 * TILES])
            zero = sb("zero", [P, TILES])
            rank = sb("rank", [P, TILES])
            need = sb("need", [P, 1])
            tri = sb("tri", [P, P])
            dest = sb("dest", [P, TILES], i32)
            nid = sb("nid", [P, TILES], i32)
            psN = ps("psN", [P, 512])
            psP = ps("psP", [P, 512])
            s_c = sem("c_c")
            s_v = sem("c_v")
            s_n = sem("c_n")
            s_p = sem("c_p")
            s_tri = sem("c_tri")
            s_sc = sem("c_sc")
            s_dest = sem("c_dest")
            s_id = sem("c_id")
            block = ctx.enter_context(nc.Block())

            @block.gpsimd
            def _(pool):
                nc.gpsimd.memset(tri[:, :], 1.0).then_inc(s_id, 1)
                pool.wait_ge(s_id, 1)
                nc.gpsimd.affine_select(out=tri[:, :], in_=tri[:, :], compare_op=ALU.is_gt, fill=0.0, base=0,
                                        pattern=[[1, P]], channel_multiplier=-1).then_inc(s_tri, 1)
                nc.gpsimd.iota(nid[:, :], pattern=[[P, TILES]], base=0, channel_multiplier=1).then_inc(s_tri, 1)
                pool.wait_ge(s_tri, 2)
                pool.wait_ge(s_dest, 1)
                for t in range(TILES):
                    nc.gpsimd.indirect_dma_start(
                        out=list_d, out_offset=bass.IndirectOffsetOnAxis(ap=dest[:, t:t + 1], axis=0),
                        in_=nid[:, t:t + 1], in_offset=None, bounds_check=SEL - 1, oob_is_err=False).then_inc(s_sc, 16)
                pool.wait_ge(s_sc, 16 * TILES)

            @block.vector
            def _(dve):
                nv = [0]

                def step(ins):
                    nv[0] += 1
                    ins.then_inc(s_v, 1)
                    dve.wait_ge(s_v, nv[0])

                def total(col, n):
                    dve.sem_inc(s_c, 1)
                    dve.wait_ge(s_n, n)

                step(nc.vector.memset(zero[:, :], 0.0))
                step(nc.vector.tensor_scalar(valid[:, :], node[:, :], float(NODES), None, ALU.is_lt))
                step(nc.vector.tensor_scalar(v[:, :], wgt[:, :], 0.0, None, ALU.is_ge))
                step(nc.vector.tensor_tensor(v[:, :], v[:, :], valid[:, :], ALU.mult))
                step(nc.vector.tensor_reduce(acc[:, 0:1], v[:, :], mybir.AxisListType.X, ALU.add))
                total(0, 1)
                step(nc.vector.tensor_scalar(acc[:, 1:2], psN[:, 0:1], float(SEL), None, ALU.is_ge))
                step(nc.vector.tensor_scalar(sgn[:, :], acc[:, 1:2], 2.0, -1.0, ALU.mult, ALU.add))
                step(nc.vector.tensor_scalar(kk_[:, :], acc[:, 1:2], float(SEL - (NODES - SEL + 1)), float(NODES - SEL + 1), ALU.mult, ALU.add))
                step(nc.vector.tensor_scalar(v[:, :], wgt[:, :], sgn[:, 0:1], None, ALU.mult))
                step(nc.vector.scalar_tensor_tensor(v[:, :], v[:, :], 1.0, valid[:, :], ALU.mult, ALU.mult))
                step(nc.vector.tensor_scalar(jk[:, :], valid[:, :], 1.0, None, ALU.subtract))
                step(nc.vector.tensor_tensor(v[:, :], v[:, :], jk[:, :], ALU.add))
                step(nc.vector.memset(pref[:, :], 0))
                step(nc.vector.memset(bit[:, :], 1 << 30))
                base = nv[0]
                PER = 6
                with dve.Fori(0, 31) as i:
                    k = i * PER + base
                    nc.vector.tensor_tensor(cand[:, :], pref[:, :], bit[:, :], ALU.bitwise_or).then_inc(s_v, 1)
                    dve.wait_ge(s_v, k + 1)
                    nc.vector.tensor_scalar(jk[:, :], v[:, :], cand[:, :].bitcast(f32), None, ALU.is_ge, ALU.add,
                                            accum_out=acc[:, 0:1]).then_inc(s_v, 1)
                    dve.wait_ge(s_v, k + 2)
                    dve.sem_inc(s_c, 1)
                    dve.wait_ge(s_n, i + 2)
                    nc.vector.tensor_tensor(acc[:, 1:2], psN[:, 0:1], kk_[:, :], ALU.is_ge).then_inc(s_v, 1)
                    dve.wait_ge(s_v, k + 3)
                    nc.vector.tensor_tensor(stp[:, :], acc[:, 1:2], bit[:, :], ALU.mult).then_inc(s_v, 1)
                    dve.wait_ge(s_v, k + 4)
                    nc.vector.tensor_tensor(pref[:, :], pref[:, :], stp[:, :], ALU.bitwise_or).then_inc(s_v, 1)
                    nc.vector.tensor_scalar(bit[:, :], bit[:, :], 1, None, ALU.logical_shift_right).then_inc(s_v, 1)
                    dve.wait_ge(s_v, k + 6)
                nv[0] = base + 31 * PER
                step(nc.vector.tensor_tensor(thr[:, :], pref[:, :].bitcast(f32), sgn[:, :], ALU.mult))
                step(nc.vector.scalar_tensor_tensor(gt[:, :], wgt[:, :], thr[:, 0:1], valid[:, :], ALU.is_gt, ALU.mult))
                step(nc.vector.scalar_tensor_tensor(eq[:, :], wgt[:, :], thr[:, 0:1], valid[:, :], ALU.is_equal, ALU.mult))
                step(nc.vector.tensor_reduce(acc[:, 0:1], gt[:, :], mybir.AxisListType.X, ALU.add))
                total(0, 33)
                step(nc.vector.tensor_scalar(need[:, :], psN[:, 0:1], -1.0, float(SEL), ALU.mult, ALU.add))

                def exclusive_rank(src, n):
                    step(nc.vector.tensor_copy(both[:, 0:TILES], src))
                    dve.sem_inc(s_c, 1)
                    dve.wait_ge(s_p, n)
                    step(nc.vector.tensor_copy(jk[:, :], psP[:, 0:TILES]))
                    step(nc.vector.tensor_tensor_scan(both[:, 0:TILES], zero[:, :], jk[:, :], 0.0, ALU.add, ALU.add))
                    step(nc.vector.tensor_tensor(both[:, 0:TILES], both[:, 0:TILES], jk[:, :], ALU.subtract))
                    step(nc.vector.tensor_tensor(rank[:, :], both[:, 0:TILES], psP[:, 64:64 + TILES], ALU.add))

                exclusive_rank(eq[:, :], 1)
                step(nc.vector.tensor_scalar(rank[:, :], rank[:, :], need[:, 0:1], None, ALU.is_lt))
                step(nc.vector.tensor_tensor(eq[:, :], eq[:, :], rank[:, :], ALU.mult))
                step(nc.vector.tensor_tensor(gt[:, :], gt[:, :], eq[:, :], ALU.add))
                exclusive_rank(gt[:, :], 2)
                step(nc.vector.tensor_scalar(jk[:, :], gt[:, :], -65536.0, 65536.0, ALU.mult, ALU.add))
                step(nc.vector.tensor_tensor(rank[:, :], rank[:, :], jk[:, :], ALU.add))
                step(nc.vector.tensor_copy(dest[:, :], rank[:, :]))
                dve.sem_inc(s_dest, 1)

            @block.tensor
            def _(pe):
                with pe.Fori(0, 33) as i:
                    pe.wait_ge(s_c, i + 1)
                    nc.tensor.matmul(psN[:, 0:1], ones[:, :], acc[:, 0:1], start=True, stop=True).then_inc(s_n, 1)
                pe.wait_ge(s_tri, 1)
                for i in range(2):
                    pe.wait_ge(s_c, 34 + i)
                    nc.tensor.matmul(psP[:, 0:TILES], ones[:, :], both[:, 0:TILES], start=True, stop=True)
                    nc.tensor.matmul(psP[:, 64:64 + TILES], tri[:, :], both[:, 0:TILES], start=True, stop=True).then_inc(s_p, 1)

        with ExitStack() as ctx:
            sb = lambda n, s, d=f32: ctx.enter_context(nc.sbuf_tensor(n, s, d))
            ps = lambda n, s: ctx.enter_context(nc.psum_tensor(n, s, f32))
            sem = lambda n: ctx.enter_context(nc.semaphore(n))
            F1 = sb("F1", [P, KF, HID])
            F2 = sb("F2", [P, KH, NF])
            f1c = sb("f1c", [P, KH])
            f2r = sb("f2r", [1, NF])
            lst = sb("lst", [P, STILES], i32)
            yg = [sb(f"yg{i}", [P, GT, YROW]) for i in range(2)]
            yT = sb("yT", [P, KF, GT * P])
            gT = sb("gT", [P, KH, GT * P])
            zo = sb("zo", [P, GT, NF])
            psY = [ps(f"psY{i}", [P, 512]) for i in range(2)]
            psG = [ps(f"psG{i}", [P, 512]) for i in range(2)]
            psF = [ps(f"psF{i}", [P, 512]) for i in range(2)]
            s_w = sem("d_w")
            s_l = sem("d_l")
            s_g = [sem(f"d_g{i}") for i in range(2)]
            s_y = sem("d_y")
            s_ye = sem("d_ye")
            s_h = sem("d_h")
            s_ge = sem("d_ge")
            s_f = sem("d_f")
            s_z = sem("d_z")
            s_out = sem("d_out")

            def shape(g):
                return (1, SLAST) if g == SGROUPS else (GT, P)

            block = ctx.enter_context(nc.Block())

            @block.sync
            def _(sp):
                sp.dma_start(lst[:, 0:STILES - 1], list_d[0:(STILES - 1) * P, :].rearrange("(t p) o -> p (t o)", p=P), allow_slow_non_contiguous=True).then_inc(s_l, 16)
                sp.dma_start(lst[0:SLAST, STILES - 1:STILES], list_d[(STILES - 1) * P:SEL, :]).then_inc(s_l, 16)
                sp.dma_start(F1[:, :, :], w1.rearrange("(c p) n -> p c n", p=P)).then_inc(s_w, 16)
                sp.dma_start(F2[:, :, :], w2.rearrange("(c p) n -> p c n", p=P)).then_inc(s_w, 16)
                sp.dma_start(f1c[:, :], fb1.rearrange("(c p) -> p c", p=P), allow_slow_non_contiguous=True).then_inc(s_w, 16)
                sp.dma_start(f2r[0:1, :], fb2.rearrange("(a b) -> a b", a=1)).then_inc(s_w, 16)

            @block.gpsimd
            def _(pool):
                pool.wait_ge(s_l, 32)

                def gather(g):
                    nt, rows = shape(g)
                    if g >= 2:
                        pool.wait_ge(s_z, (g - 2) * GT + GT)
                    for t in range(nt):
                        nc.gpsimd.indirect_dma_start(
                            out=yg[g % 2][0:rows, t, :], out_offset=None, in_=yrow_d,
                            in_offset=bass.IndirectOffsetOnAxis(ap=lst[0:rows, g * GT + t:g * GT + t + 1], axis=0)).then_inc(s_g[g % 2], 16)

                def scatter(g):
                    nt, rows = shape(g)
                    for t in range(nt):
                        pool.wait_ge(s_z, g * GT + t + 1)
                        nc.gpsimd.indirect_dma_start(
                            out=out, out_offset=bass.IndirectOffsetOnAxis(ap=lst[0:rows, g * GT + t:g * GT + t + 1], axis=0),
                            in_=zo[0:rows, t, :], in_offset=None).then_inc(s_out, 16)
                gather(0)
                gather(1)
                for g in range(SGROUPS + 1):
                    scatter(g)
                    if g + 2 <= SGROUPS:
                        gather(g + 2)
                pool.wait_ge(s_out, 16 * STILES)

            @block.vector
            def _(dve):
                for g in range(SGROUPS + 1):
                    nt, rows = shape(g)
                    if g:
                        dve.wait_ge(s_out, 16 * g * GT)
                    for t in range(nt):
                        k = g * GT + t
                        dve.wait_ge(s_f, k + 1)
                        nc.vector.scalar_tensor_tensor(zo[0:rows, t, :], psF[k % 2][0:rows, 0:NF], yg[g % 2][0:rows, t, 2 * NF:2 * NF + 1],
                                                       yg[g % 2][0:rows, t, NF:2 * NF], ALU.mult, ALU.add).then_inc(s_z, 1)

            @block.scalar
            def _(act):
                act.wait_ge(s_w, 64)

                def evac(g):
                    nt, rows = shape(g)
                    if g:
                        act.wait_ge(s_h, g * KH)
                    for t in range(nt):
                        act.wait_ge(s_y, g * GT + t + 1)
                        nc.scalar.copy(yT[:, :, t * P:t * P + rows],
                                       psY[t % 2][:, 0:2 * P].rearrange("p (c n) -> p c n", c=KF)[:, :, 0:rows]).then_inc(s_ye, 1)
                evac(0)
                for g in range(SGROUPS + 1):
                    nt, rows = shape(g)
                    n = nt * rows
                    for m in range(KH):
                        act.wait_ge(s_h, g * KH + m + 1)
                        if g:
                            act.wait_ge(s_f, g * GT)
                        nc.scalar.activation(gT[:, m, 0:n], psG[m % 2][:, 0:n], ACT.Gelu_apprx_tanh, bias=f1c[:, m:m + 1]).then_inc(s_ge, 1)
                    if g < SGROUPS:
                        evac(g + 1)

            @block.tensor
            def _(pe):
                pe.wait_ge(s_w, 64)

                def transposes(g):
                    nt, rows = shape(g)
                    pe.wait_ge(s_g[g % 2], 16 * GT * (g // 2) + 16 * nt)
                    for t in range(nt):
                        if g * GT + t >= 2:
                            pe.wait_ge(s_ye, g * GT + t - 1)
                        for c in range(KF):
                            ins = nc.tensor.transpose(psY[t % 2][:, c * P:c * P + rows], yg[g % 2][0:rows, t, c * P:(c + 1) * P],
                                                      ident[0:rows, 0:rows])
                        ins.then_inc(s_y, 1)
                transposes(0)
                for g in range(SGROUPS + 1):
                    nt, rows = shape(g)
                    n = nt * rows
                    pe.wait_ge(s_ye, g * GT + nt)
                    for m in range(KH):
                        if g * KH + m >= 2:
                            pe.wait_ge(s_ge, g * KH + m - 1)
                        for c in range(KF):
                            ins = nc.tensor.matmul(psG[m % 2][:, 0:n], F1[:, c, m * P:(m + 1) * P], yT[:, c, 0:n],
                                                   start=(c == 0), stop=(c == KF - 1))
                        ins.then_inc(s_h, 1)
                    if g < SGROUPS:
                        transposes(g + 1)
                    for t in range(nt):
                        k = g * GT + t
                        if k >= 2:
                            pe.wait_ge(s_z, k - 1)
                        o = psF[k % 2][0:rows, 0:NF]
                        nc.tensor.matmul(o, ones[0:1, 0:rows], f2r[0:1, :], start=True, stop=False)
                        for m in range(KH):
                            if t == 0:
                                pe.wait_ge(s_ge, g * KH + m + 1)
                            ins = nc.tensor.matmul(o, gT[:, m, t * P:t * P + rows], F2[:, m, :], start=False, stop=(m == KH - 1))
                        ins.then_inc(s_f, 1)


_INS = ["x", "dst", "edge_attr_96", "L0_gnn_u", "L0_gnn_W1", "L0_gnn_b1", "L0_gnn_W2", "L0_gnn_b2",
        "L0_mix_W_qkv", "L0_mix_b_qkv", "L0_mix_W_out", "L0_mix_b_out",
        "L0_ffn_wr", "L0_ffn_br", "L0_ffn_w1", "L0_ffn_b1", "L0_ffn_w2", "L0_ffn_b2"]


def kernel(**inputs):
    import numpy as _np
    import concourse.bacc as _bacc
    from concourse import mybir as _mybir
    from concourse.bass_utils import run_bass_kernel_spmd as _run

    nc = _bacc.Bacc("TRN2", target_bir_lowering=False, num_devices=1)
    arrays, args = {}, []
    for name in _INS:
        a = _np.ascontiguousarray(inputs[name])
        if name == "dst":
            a = _np.pad(a, (SIDE, EPAD - EDGES), constant_values=(-1, NODES))
        if name == "edge_attr_96":
            a = _np.pad(a, ((0, EPAD - EDGES), (0, 0)))
        arrays[f"in_{name}"] = a
        args.append(nc.dram_tensor(f"in_{name}", a.shape, _mybir.dt.from_np(a.dtype), kind="ExternalInput").ap())
    args.append(nc.dram_tensor("out_x", (NODES, NF), f32, kind="ExternalOutput").ap())
    build(nc, *args)
    r = _run(nc, [arrays], core_ids=[0])
    return r.results[0]["out_x"]
```

```python
import numpy as np
import concourse.bass as bass
from concourse import mybir
from concourse.alu_op_type import AluOpType as ALU
from contextlib import ExitStack

ACT = mybir.ActivationFunctionType
f32 = mybir.dt.float32
i32 = mybir.dt.int32
f32r = mybir.dt.float32r
FMAX = float(np.finfo(np.float32).max)

P = 128
NODES, NF = 6250, 256
EDGES, EF = 200000, 96
HID = 1024
GF = 64
TILES = -(-NODES // P)
GT = 4
GROUPS = TILES // GT
LAST = NODES - (TILES - 1) * P
SIDE = 448
EPAD = SIDE * SIDE
R = EPAD // P
Q = R // 4
T = 32
TQ = T // 4
CHUNKS = R // T
XB, MB, OB = 4, 2, 2
SEL = NODES // 2 - 1
STILES = -(-SEL // P)
SGROUPS = STILES // GT
SLAST = SEL - (STILES - 1) * P
TAIL = 3 * EF - 2 * P
AW = 2 * P + 3 * TAIL
AGG = 2 * EF
BL = 5
EPS = 1e-5
KF = NF // P
KH = HID // P
YROW = 2 * NF + 8


def split3(nc, out, lhs, rhs, start, stop):
    (lh, ll), (rh, rl) = lhs, rhs
    nc.tensor.matmul(out, lh, rh, start=start, stop=False)
    nc.tensor.matmul(out, lh, rl, start=False, stop=False)
    return nc.tensor.matmul(out, ll, rh, start=False, stop=stop)


def build(nc, x, dstp, edges, u, W1, b1, W2, b2, Wqkv, bqkv, Wout, bout, wr, br, w1, fb1, w2, fb2, out):
    dram = lambda n, s, d=f32: nc.dram_tensor(n, s, d).ap()
    xT_d = dram("xT_d", (GROUPS + 1, P, KF, GT * P))
    qT_d = dram("qT_d", (GROUPS + 1, P, KF, GT * P))
    scan_d = dram("scan_d", (P * Q, AGG))
    carry_d = dram("carry_d", (P, AGG))
    base_d = dram("base_d", (NODES, NF))
    att_d = dram("att_d", (NODES, NF))
    yrow_d = dram("yrow_d", (NODES, YROW))

    keep = ExitStack()
    with keep:
        ksb = lambda n, s, d=f32: keep.enter_context(nc.sbuf_tensor(n, s, d))
        ident = ksb("ident", [P, P])
        ones = ksb("ones", [P, P])
        shift = ksb("shift", [P, P])
        corner = ksb("corner", [P, P])
        node = ksb("node", [P, TILES])
        Eend = ksb("Eend", [P, TILES])
        Sbeg = ksb("Sbeg", [P, TILES])
        idx = ksb("idx", [P, 3, TILES], i32)
        iRaw, iScan, iCarry = (idx[:, i, :] for i in range(3))
        has = ksb("has", [P, TILES])
        rcnt = ksb("rcnt", [P, TILES])
        kSel = ksb("kSel", [P, 5, TILES])
        mSel = ksb("mSel", [P, 5, TILES])
        wgt = ksb("wgt", [P, TILES])
        keepc = ksb("keepc", [P, 1])
        ends = ksb("ends", [P, AGG])
        fsum = ksb("fsum", [P, TILES])
        ridx = ksb("ridx", [P, TILES])

        with ExitStack() as ctx:
            sb = lambda n, s, d=f32: ctx.enter_context(nc.sbuf_tensor(n, s, d))
            ps = lambda n, s: ctx.enter_context(nc.psum_tensor(n, s, f32))
            sem = lambda n: ctx.enter_context(nc.semaphore(n))
            dcur = sb("dcur", [P, R], i32)
            dprv = sb("dprv", [P, R], i32)
            kTri = sb("kTri", [P, Q, 3])
            pTri = sb("pTri", [P, Q, 3])
            kQ = sb("kQ", [P, Q])
            mQ = sb("mQ", [P, Q])
            xb = [sb(f"xb{i}", [P, TQ, 4, EF]) for i in range(XB)]
            mx = [sb(f"mx{i}", [P, TQ, 3, EF]) for i in range(MB)]
            ob = [sb(f"ob{i}", [P, TQ, AGG]) for i in range(OB)]
            xg = [sb(f"xg{i}", [P, GT, NF]) for i in range(2)]
            xn = [sb(f"xn{i}", [P, GT, NF]) for i in range(2)]
            q2s = sb("q2s", [P, TILES])
            q4s = sb("q4s", [P, TILES])
            rq = sb("rq", [P, TILES])
            M = sb("M", [P, KF, NF])
            WvoI = sb("WvoI", [P, KF, NF])
            brow = [sb(f"brow{i}", [1, NF], f32r) for i in range(2)]
            bqs = [sb(f"bqs{i}", [1, 2 * NF], f32r) for i in range(2)]
            one_r = sb("one_r1", [1, P], f32r)
            xT = sb("xT", [P, KF, GT * P])
            qT = sb("qT", [P, KF, GT * P])
            q2 = sb("q2", [P, GT, NF])
            k2 = sb("k2", [P, GT, NF])
            kc = sb("kc", [P, GT, 2 * NF])
            junk = sb("junk", [P, NF])
            jc = [sb(f"jc{i}", [P, SIDE], mybir.dt.bfloat16) for i in range(BL)]
            Wqk = sb("Wqk", [P, KF, 2 * NF])
            Wv = sb("Wv", [P, KF, NF])
            Wo = sb("Wo", [P, KF, NF])
            WvT = sb("WvT", [P, KF, NF])
            kxT = sb("kxT", [P, KF, NF])
            bqk = sb("bqk", [1, 3 * NF])
            bv = sb("bv", [P, KF])
            b2r = sb("b2r", [1, 2, NF])
            wm = sb("wm", [P, 8])
            krow = sb("krow", [1, 2 * NF])
            kcol = sb("kcol", [P, 8])
            st = sb("st", [P, TILES, 6])
            mean = sb("mean", [P, TILES])
            va = sb("va", [P, TILES])
            sd = sb("sd", [P, TILES])
            rstd = sb("rstd", [P, TILES])
            nmr = sb("nmr", [P, TILES])
            k2s = sb("k2s", [P, GT])
            rk = sb("rk", [P, GT])
            nodei = sb("nodei", [P, TILES], i32)
            nhalf = sb("nhalf", [P, TILES])
            csum = sb("csum", [P, TILES])
            ridxi = sb("ridxi", [P, 2 * BL * BL], i32)
            fr = [sb(f"fr{i}", [P, SIDE], i32) for i in range(2 * BL)]
            crow, crowf = fr[0][0:1, :], fr[1][0:1, :].bitcast(f32)
            rcol = [sb(f"rcol{i}", [P, BL], i32) for i in range(2)]
            a1, a2, a3 = (sb(f"a{i}", [P, TILES]) for i in range(3))

            psT = [ps(f"psT{i}", [P, 512]) for i in range(2)]
            psQ = [ps(f"psQ{i}", [P, 512]) for i in range(2)]
            psKx = [ps(f"psKx{i}", [P, 512]) for i in range(2)]
            psR = ps("psR", [P, 512])
            psC = ps("psC", [P, 512])

            s_dst = sem("s_dst")
            s_load = [sem(f"s_load{i}") for i in range(XB)]
            s_dump = [sem(f"s_dump{i}") for i in range(OB)]
            s_const = sem("s_const")
            s_wload = sem("s_wload")
            s_masks = sem("s_masks")
            s_pen = sem("s_pen")
            s_mul = sem("s_mul")
            s_tree = sem("s_tree")
            s_max = sem("s_max")
            s_sum = sem("s_sum")
            s_v = sem("s_v")
            s_stat = sem("s_stat")
            s_sqrt = sem("s_sqrt")
            s_ln = sem("s_ln")
            s_xg = [sem(f"s_xg{i}") for i in range(2)]
            s_xn = sem("s_xn")
            s_trx = sem("s_trx")
            s_trq = sem("s_trq")
            s_evx = sem("s_evx")
            s_evq = sem("s_evq")
            s_qk = sem("s_qk")
            s_sq = sem("s_sq")
            s_rk = sem("s_rk")
            s_kk = sem("s_kk")
            s_kx = sem("s_kx")
            s_xTo = sem("s_xTo")
            s_qTo = sem("s_qTo")
            s_wq = sem("s_wq")
            s_crow = sem("s_crow")
            s_cbc = sem("s_cbc")
            s_csum = sem("s_csum")
            s_ridx = sem("s_ridx")
            s_fr = [sem(f"s_fr{i}") for i in range(2 * BL)]
            s_fs = sem("s_fs")
            s_col = sem("s_col")
            s_turn = sem("s_turn")
            s_pt = sem("s_pt")
            s_at = sem("s_at")
            s_ap = [sem(f"s_ap{i}") for i in range(2)]
            s_qm = sem("s_qm")
            s_t2 = sem("s_t2")
            s_t2o = [sem(f"s_t2o{i}") for i in range(2)]
            s_wv = sem("s_wv")
            s_bw = sem("s_bw")
            s_ba = sem("s_ba")
            s_bs = sem("s_bs")
            s_bo = sem("s_bo")
            s_fac = sem("s_fac")
            s_act = sem("s_act")
            s_pairs = sem("s_pairs")
            s_pc0 = sem("s_pc0")
            s_id = sem("s_id")
            s_xs = [sem(f"s_xs{i}") for i in range(4)]

            ev = edges.rearrange("(p r) f -> p r f", r=R)
            dcur_v = dstp[SIDE:SIDE + EPAD].rearrange("(p r) -> p r", r=R)
            dprv_v = dstp[SIDE - 1:SIDE - 1 + EPAD].rearrange("(p r) -> p r", r=R)
            rows_v = dstp.rearrange("(a b) -> a b", b=SIDE)
            scan_v = scan_d.rearrange("(p q) f -> p q f", q=Q)

            def quads(c):
                return bass.ds(c * TQ, TQ)

            bs = dcur[:, 0:GT * NF].bitcast(f32).rearrange("p (t f) -> p t f", t=GT)
            qT1 = dprv[:, 0:KF * GT * P].bitcast(f32).rearrange("p (c n) -> p c n", c=KF)
            sq, stage = (qT, qT1), (bs, k2)

            def shape(g):
                return (1, LAST) if isinstance(g, int) and g == GROUPS else (GT, P)

            def x_group(g, nt, rows):
                return x[bass.ds(g * GT * P, nt * rows), :].rearrange("(t p) f -> p t f", p=rows)

            xs = [xn[0], xn[1], q2, k2]

            block = ctx.enter_context(nc.Block())

            @block.sync
            def _(sp):
                sp.dma_start(dcur[:, :], dcur_v).then_inc(s_dst, 16)
                sp.dma_start(dprv[:, :], dprv_v).then_inc(s_dst, 16)
                for b in range(XB):
                    if b == 2:
                        sp.wait_ge(s_stat, 4 * GT)
                    sp.dma_start(xb[b][:, :, :, :].rearrange("p q i f -> p (q i) f"),
                                 ev[:, b * T:(b + 1) * T, :]).then_inc(s_load[b], 16)

                def dump_and_load(c, b, load):
                    sp.wait_ge(s_sum, c * TQ + TQ + 1)
                    sp.wait_ge(s_max, c * TQ + TQ + 1)
                    sp.dma_start(scan_v[:, quads(c), :], ob[b % OB][:, :, :]).then_inc(s_dump[b % OB], 16)
                    if load:
                        sp.dma_start(xb[b][:, :, :, :].rearrange("p q i f -> p (q i) f"),
                                     ev[:, bass.ds(c * T + XB * T, T), :]).then_inc(s_load[b], 16)

                with sp.Fori(0, 11) as g:
                    for b in range(XB):
                        dump_and_load(g * XB + b, b, True)
                for c in range(44, CHUNKS):
                    dump_and_load(c, c % XB, c + XB < CHUNKS)
                sp.wait_ge(s_dump[0], 16 * 25)
                sp.wait_ge(s_dump[1], 16 * 24)

            @block.gpsimd
            def _(pool):
                nc.gpsimd.memset(ident[:, :], 0.0).then_inc(s_id, 1)
                pool.wait_ge(s_id, 1)
                nc.gpsimd.affine_select(out=ident[:, :], in_=ident[:, :], compare_op=ALU.not_equal, fill=1.0, base=0,
                                        pattern=[[-1, P]], channel_multiplier=1).then_inc(s_const, 1)
                nc.gpsimd.memset(ones[:, :], 1.0).then_inc(s_const, 1)
                for m, b in ((shift, 1), (corner, 1 - P)):
                    nc.gpsimd.memset(m[:, :], 0.0).then_inc(s_id, 1)
                pool.wait_ge(s_id, 3)
                for m, b in ((shift, 1), (corner, 1 - P)):
                    nc.gpsimd.affine_select(out=m[:, :], in_=m[:, :], compare_op=ALU.not_equal, fill=1.0, base=b,
                                            pattern=[[-1, P]], channel_multiplier=1).then_inc(s_id, 1)
                nc.gpsimd.iota(nodei[:, :], pattern=[[P, TILES]], base=0, channel_multiplier=1).then_inc(s_const, 1)
                pool.wait_ge(s_masks, 1)

                def mask(c, b, g):
                    pool.wait_ge(s_load[b], g * 16 + 16)
                    if not isinstance(c, int) or c >= MB:
                        pool.wait_ge(s_max, c * TQ - TQ * MB + TQ + 1)
                    x3 = xb[b][:, :, 0:3, :]
                    k = kTri[:, quads(c), :].rearrange("p q (i o) -> p q i o", o=1).broadcast_to([P, TQ, 3, EF])
                    p_ = pTri[:, quads(c), :].rearrange("p q (i o) -> p q i o", o=1).broadcast_to([P, TQ, 3, EF])
                    nc.gpsimd.tensor_tensor(mx[b % MB][:, :, :, :], x3, p_, ALU.add).then_inc(s_pen, 1)
                    pool.wait_ge(s_pen, c + 1)
                    nc.gpsimd.tensor_tensor(x3, x3, k, ALU.mult).then_inc(s_mul, 1)

                def columns(j, e):
                    nc.gpsimd.tensor_copy(rcol[e][:, :], ridxi[:, bass.ds(j * BL, BL)]).then_inc(s_col, 1)

                def rows(b, n):
                    pool.wait_ge(s_col, n)
                    pool.sem_inc(s_turn, 1)
                    nc.gpsimd.indirect_dma_start(
                        out=fr[b][:, :], out_offset=None, in_=rows_v,
                        in_offset=bass.IndirectOffsetOnAxis(ap=rcol[b // BL][:, b % BL:b % BL + 1], axis=0)).then_inc(s_fr[b], 16)

                for g in range(2):
                    for b in range(XB):
                        mask(g * XB + b, b, g)
                pool.wait_ge(s_ridx, 1)
                for g in range(2, 4):
                    columns(g - 2, g % 2)
                    for b in range(BL):
                        if b < XB:
                            mask(g * XB + b, b, g)
                        rows((g % 2) * BL + b, g - 1)
                with pool.Fori(2, 6) as h:
                    for e in range(2):
                        for b in range(BL):
                            if b < XB:
                                mask(h * (2 * XB) + e * XB + b, b, h * 2 + e)
                            if b == 0:
                                pool.wait_ge(s_fs, h * (2 * BL) + e * BL - 3 * BL)
                                columns(h * 2 + e - 2, e)
                            rows(e * BL + b, h * 2 + e - 1)
                mask(CHUNKS - 1, 0, 12)

            @block.vector
            def _(dve):
                nv = [0]

                def step(ins, wait=True):
                    nv[0] += 1
                    ins.then_inc(s_v, 1)
                    if wait:
                        dve.wait_ge(s_v, nv[0])

                dve.wait_ge(s_dst, 32)
                cq = dcur[:, :].rearrange("p (q i) -> p q i", i=4)
                pq = dprv[:, :].rearrange("p (q i) -> p q i", i=4)
                step(nc.vector.tensor_tensor(kTri[:, :, :], cq[:, :, 0:3], cq[:, :, 3:4].broadcast_to([P, Q, 3]), ALU.is_equal), False)
                step(nc.vector.tensor_tensor(kQ[:, :], pq[:, :, 0], cq[:, :, 3], ALU.is_equal))
                step(nc.vector.tensor_scalar(pTri[:, :, :], kTri[:, :, :], 1.0, FMAX, ALU.subtract, ALU.mult), False)
                step(nc.vector.tensor_scalar(mQ[:, :], kQ[:, :], 0.5, 2.0, ALU.subtract, ALU.mult))
                step(nc.vector.tensor_scalar(mQ[:, :], mQ[:, :], FMAX, None, ALU.mult))
                step(nc.vector.tensor_tensor(keepc[:, :], dprv[:, 0:1], dcur[:, R - 1:R], ALU.is_equal))
                dve.sem_inc(s_masks, 1)
                nc.vector.memset(ob[1][:, TQ - 1, 0:EF], -FMAX).then_inc(s_max, 1)
                nc.vector.memset(ob[1][:, TQ - 1, EF:AGG], 0.0).then_inc(s_sum, 1)
                dve.wait_ge(s_const, 3)
                step(nc.vector.tensor_copy(node[:, :], nodei[:, :]))
                step(nc.vector.tensor_scalar(nhalf[:, :], node[:, :], 0.5, None, ALU.add))
                dve.wait_ge(s_crow, 16)
                step(nc.vector.tensor_copy(crowf[:, :], crow[:, :]))
                dve.sem_inc(s_cbc, 1)
                def centre_weights():
                    dve.wait_ge(s_wload, 16 * 8)
                    for c in range(KF):
                        for h in range(2):
                            step(nc.vector.tensor_reduce(wm[:, 2 * c + h:2 * c + h + 1], Wqk[:, c, h * NF:(h + 1) * NF],
                                                         mybir.AxisListType.X, ALU.add), False)
                    for h in range(2):
                        step(nc.vector.tensor_reduce(wm[0:1, 4 + h:5 + h], bqk[0:1, h * NF:(h + 1) * NF],
                                                     mybir.AxisListType.X, ALU.add))
                    step(nc.vector.tensor_scalar(wm[:, 0:4], wm[:, 0:4], 1.0 / NF, None, ALU.mult), False)
                    step(nc.vector.tensor_scalar(wm[0:1, 4:6], wm[0:1, 4:6], 1.0 / NF, None, ALU.mult))
                    for c in range(KF):
                        for h in range(2):
                            w_ = Wqk[:, c, h * NF:(h + 1) * NF]
                            step(nc.vector.tensor_scalar(w_, w_, wm[:, 2 * c + h:2 * c + h + 1], None, ALU.subtract), False)
                    for h in range(2):
                        w_ = bqk[0:1, h * NF:(h + 1) * NF]
                        step(nc.vector.tensor_scalar(w_, w_, wm[0:1, 4 + h:5 + h], None, ALU.subtract))
                    step(nc.vector.tensor_copy(one_r[0:1, :], ones[0:1, :]), False)
                    step(nc.vector.tensor_copy(bqs[0][0:1, :], bqk[0:1, 0:2 * NF]))
                    step(nc.vector.tensor_tensor(bqs[1][0:1, :], bqk[0:1, 0:2 * NF], bqs[0][0:1, :].bitcast(f32), ALU.subtract))
                    dve.sem_inc(s_wq, 1)

                step(nc.vector.memset(st[:, :, :], 1.0), False)
                step(nc.vector.memset(q2s[:, :], 1.0), False)
                step(nc.vector.memset(q4s[:, :], 1.0))

                def stats(g, nt, rows, buf, sem_, n):
                    dve.wait_ge(sem_, n)
                    for t in range(nt):
                        k = g * GT + t
                        nc.vector.bn_stats(st[0:rows, k, :], buf[0:rows, t, :]).then_inc(s_stat, 1)

                def stats_quarter(h):
                    for e in range(4):
                        stats(h * 4 + e, GT, P, xs[e], s_xs[e], h * 16 + 16)

                def variances():
                    stats(GROUPS, 1, LAST, xs[0], s_xs[0], 64)
                    dve.wait_ge(s_stat, TILES)
                    step(nc.vector.tensor_tensor(a1[:, :], st[:, :, 1], st[:, :, 4], ALU.add), False)
                    step(nc.vector.tensor_tensor(a2[:, :], st[:, :, 1], st[:, :, 4], ALU.subtract), False)
                    step(nc.vector.tensor_tensor(a3[:, :], st[:, :, 2], st[:, :, 5], ALU.add))
                    step(nc.vector.tensor_scalar(mean[:, :], a1[:, :], 0.5, None, ALU.mult), False)
                    step(nc.vector.scalar_tensor_tensor(a2[:, :], a2[:, :], 0.25, a2[:, :], ALU.mult, ALU.mult))
                    step(nc.vector.scalar_tensor_tensor(va[:, :], a3[:, :], 1.0 / NF, a2[:, :], ALU.mult, ALU.add))
                    step(nc.vector.tensor_scalar(va[:, :], va[:, :], EPS, None, ALU.add))
                    dve.sem_inc(s_ln, 1)

                def deviations():
                    dve.wait_ge(s_sqrt, 1)
                    step(nc.vector.reciprocal(a1[:, :], sd[:, :]))
                    step(nc.vector.tensor_tensor(a1[:, :], va[:, :], a1[:, :], ALU.mult))
                    step(nc.vector.tensor_tensor(a1[:, :], a1[:, :], sd[:, :], ALU.add))
                    step(nc.vector.tensor_scalar(a1[:, :], a1[:, :], 0.5, None, ALU.mult))
                    step(nc.vector.reciprocal(rstd[:, :], a1[:, :]))
                    step(nc.vector.scalar_tensor_tensor(nmr[:, :], mean[:, :], -1.0, rstd[:, :], ALU.mult, ALU.mult))
                    dve.sem_inc(s_ln, 1)

                def rows_of_last_edges():
                    dve.wait_ge(s_csum, TILES)
                    step(nc.vector.tensor_scalar(ridx[:, :], csum[:, :], float(SIDE), 0.5, ALU.add, ALU.mult))
                    step(nc.vector.tensor_scalar(ridx[:, :], ridx[:, :], float(SIDE - 1), None, ALU.min))
                    step(nc.vector.memset(ridxi[:, :], 0))
                    step(nc.vector.tensor_scalar(ridxi[:, 0:TILES], ridx[:, :], 1.0, None, ALU.add))
                    dve.sem_inc(s_ridx, 1)

                def bias_row():
                    dve.wait_ge(s_wv, 2)
                    step(nc.vector.tensor_copy(brow[0][0:1, :], psR[0:1, 0:NF]))
                    step(nc.vector.tensor_tensor(brow[1][0:1, :], psR[0:1, 0:NF], brow[0][0:1, :].bitcast(f32), ALU.subtract))
                    dve.sem_inc(s_bw, 1)

                def edge_chunk(c, b, g):
                    X, m, o, oprev = xb[b], mx[b % MB], ob[b % OB], ob[(b + 1) % OB]
                    dve.wait_ge(s_mul, c + 1)
                    dve.wait_ge(s_pen, c + 1)
                    nc.vector.tensor_tensor(m[:, :, 0, :], m[:, :, 0, :], m[:, :, 1, :], ALU.max).then_inc(s_tree, 1)
                    nc.vector.tensor_tensor(m[:, :, 2, :], m[:, :, 2, :], X[:, :, 3, :], ALU.max).then_inc(s_tree, 1)
                    xp = X[:, :, :, :].rearrange("p q (h two) f -> p q h two f", two=2)
                    for h in range(2):
                        ins = nc.vector.tensor_tensor(X[:, :, 2 * h, :], X[:, :, 2 * h, :], X[:, :, 2 * h + 1, :], ALU.add)
                        ins.then_inc(s_pairs, 1)
                    dve.wait_ge(s_tree, c * 4 + 2)
                    nc.vector.tensor_tensor(m[:, :, 0, :], m[:, :, 0, :], m[:, :, 2, :], ALU.max).then_inc(s_tree, 1)
                    dve.wait_ge(s_pairs, c * 2 + 2)
                    nc.vector.tensor_tensor(X[:, :, 0, :], X[:, :, 0, :], X[:, :, 2, :], ALU.add).then_inc(s_tree, 1)
                    if not isinstance(c, int) or c >= OB:
                        dve.wait_ge(s_dump[b % OB], g * 32 + (b // OB) * 16)
                    dve.wait_ge(s_tree, c * 4 + 4)
                    for q in range(TQ):
                        prev = oprev[:, TQ - 1, :] if q == 0 else o[:, q - 1, :]
                        dve.wait_ge(s_max, c * TQ + q + 1)
                        nc.vector.scalar_tensor_tensor(o[:, q, 0:EF], prev[:, 0:EF], mQ[:, bass.ds(c * TQ + q, 1)],
                                                       m[:, q, 0, :], ALU.min, ALU.max).then_inc(s_max, 1)
                        dve.wait_ge(s_sum, c * TQ + q + 1)
                        nc.vector.scalar_tensor_tensor(o[:, q, EF:AGG], prev[:, EF:AGG], kQ[:, bass.ds(c * TQ + q, 1)],
                                                       X[:, q, 0, :], ALU.mult, ALU.add).then_inc(s_sum, 1)

                def key_norm(g, nt, rows):
                    dve.wait_ge(s_sq, g * (3 * GT) + 3 * nt)
                    nc.vector.tensor_scalar(rk[0:rows, 0:nt], k2s[0:rows, 0:nt], 1e-7, None, ALU.add).then_inc(s_rk, 1)
                    dve.wait_ge(s_rk, g * 2 + 1)
                    nc.vector.reciprocal(rk[0:rows, 0:nt], rk[0:rows, 0:nt]).then_inc(s_rk, 1)

                stats_quarter(0)
                for c in range(8):
                    edge_chunk(c, c % XB, c // XB)
                    if c == 0:
                        centre_weights()
                    if c < 2:
                        stats_quarter(c + 1)
                    if c == 1:
                        variances()
                    if c == 2:
                        bias_row()
                        deviations()
                    if c == 5:
                        rows_of_last_edges()
                    if c in (4, 7):
                        key_norm(int(c == 7), GT, P)

                NORM = {1: 2, 4: 3, 7: 4}

                def eight(h):
                    for j in range(8):
                        edge_chunk(h * 8 + j, j % XB, h * 2 + j // XB)
                        if j in NORM:
                            g = (h - 1) * 3 + NORM[j]
                            key_norm(g, *shape(g))
                with dve.Fori(1, 4) as h:
                    eight(h)
                for c in range(32, CHUNKS):
                    edge_chunk(c, c % XB, c // XB)
                    if c in (33, 36):
                        g = GROUPS - (c == 33)
                        key_norm(g, *shape(g))
                    if c == 38:
                        dve.wait_ge(s_at, 3)
                        step(nc.vector.tensor_scalar(kcol[:, 2:4], kcol[:, 0:2], 1e-12, float(np.sqrt(float(NODES))), ALU.max, ALU.mult))
                        step(nc.vector.reciprocal(kcol[:, 4:6], kcol[:, 2:4]))
                        dve.wait_ge(s_at, 4)
                        step(nc.vector.tensor_scalar(a1[:, :], q2s[:, :], 1e-7, None, ALU.add))
                        step(nc.vector.reciprocal(a2[:, :], a1[:, :]))
                        step(nc.vector.tensor_tensor(a3[:, :], sd[:, :], a2[:, :], ALU.mult))
                        step(nc.vector.tensor_scalar(a3[:, :], a3[:, :], 1e-12, None, ALU.max))
                        step(nc.vector.reciprocal(a3[:, :], a3[:, :]))
                        step(nc.vector.tensor_tensor(rq[:, :], a3[:, :], a2[:, :], ALU.mult))
                        dve.sem_inc(s_fac, 1)
                dve.wait_ge(s_max, CHUNKS * TQ + 1)
                dve.wait_ge(s_sum, CHUNKS * TQ + 1)
                step(nc.vector.tensor_copy(ends[:, :], ob[0][:, TQ - 1, :]))
                dve.wait_ge(s_fs, TILES)
                step(nc.vector.tensor_scalar(a1[:, :], fsum[:, :], float(SIDE), 0.5, ALU.add, ALU.mult))
                step(nc.vector.scalar_tensor_tensor(Eend[:, :], ridx[:, :], float(SIDE), a1[:, :], ALU.mult, ALU.add))

            @block.scalar
            def _(act):
                act.dma_start(crow[0:1, :], rows_v[1:SIDE + 1, SIDE - 1:SIDE].rearrange("a b -> b a"), allow_slow_non_contiguous=True).then_inc(s_crow, 16)
                act.dma_start(Wqk[:, :, :], Wqkv[:, 0:2 * NF].rearrange("(c p) n -> p c n", p=P)).then_inc(s_wload, 16)
                act.dma_start(Wv[:, :, :], Wqkv[:, 2 * NF:3 * NF].rearrange("(c p) n -> p c n", p=P)).then_inc(s_wload, 16)
                act.dma_start(Wo[:, :, :], Wout.rearrange("(c p) n -> p c n", p=P)).then_inc(s_wload, 16)
                act.dma_start(bqk[0:1, :], bqkv.rearrange("(a b) -> a b", a=1)).then_inc(s_wload, 16)
                act.dma_start(bv[:, :], bqkv[2 * NF:3 * NF].rearrange("(c p) -> p c", p=P), allow_slow_non_contiguous=True).then_inc(s_wload, 16)
                act.dma_start(b2r[0:1, 0, :], b2.rearrange("(a b) -> a b", a=1)).then_inc(s_wload, 16)
                act.dma_start(b2r[0:1, 1, :], bout.rearrange("(a b) -> a b", a=1)).then_inc(s_wload, 16)
                act.dma_start(krow[0:1, 0:1], b2[0:1].rearrange("(a b) -> a b", a=1)).then_inc(s_wload, 16)
                for e in range(4):
                    act.dma_start(xs[e][:, :, :], x_group(e, GT, P)).then_inc(s_xs[e], 16)

                act.dma_start(xg[0][:, :, :], x_group(0, GT, P)).then_inc(s_xg[0], 16)
                act.dma_start(xg[1][:, :, :], x_group(1, GT, P)).then_inc(s_xg[1], 16)

                act.wait_ge(s_wv, 1)
                nc.scalar.copy(WvT[:, :, :], psT[1][:, :].rearrange("p (c n) -> p c n", c=KF)).then_inc(s_at, 1)

                def coarse(t, b):
                    if not isinstance(t, int) or t >= 4:
                        act.wait_ge(s_csum, t - 3)
                    nc.scalar.activation(jc[b][:, :], psC[:, 0:SIDE], ACT.Sign, bias=nhalf[:, bass.ds(t, 1)], scale=-1.0,
                                         accum_out=csum[:, bass.ds(t, 1)]).then_inc(s_csum, 1)
                act.wait_ge(s_pc0, 1)
                for t in range(4):
                    coarse(t, t)
                act.wait_ge(s_wv, 2)
                nc.scalar.copy(WvoI[:, :, :], psQ[1][:, :].rearrange("p (c n) -> p c n", c=KF)).then_inc(s_bw, 1)
                with act.Fori(1, GROUPS // 4) as h:
                    for e in range(4):
                        act.wait_ge(s_stat, h * (4 * GT) + e * GT - 3 * GT)
                        act.dma_start(xs[e][:, :, :], x_group(h * 4 + e, GT, P)).then_inc(s_xs[e], 16)
                    for q in range(4):
                        for b in range(4):
                            coarse(h * 16 + (q * 4 + b - 12), b)
                act.wait_ge(s_stat, (GROUPS - 3) * GT)
                act.dma_start(xs[0][0:LAST, 0:1, :], x_group(GROUPS, 1, LAST)).then_inc(s_xs[0], 16)
                with act.Fori(9, TILES // 4) as h:
                    for b in range(4):
                        coarse(h * 4 + b, b)
                coarse(TILES - 1, 0)
                act.wait_ge(s_csum, TILES)
                act.wait_ge(s_ln, 1)
                nc.scalar.sqrt(sd[:, :], va[:, :]).then_inc(s_sqrt, 1)

                def fine(j):
                    for b in range(min(BL, TILES - j * BL)):
                        t = j * BL + b
                        if t >= BL:
                            act.wait_ge(s_fs, t - BL + 1)
                        f = (j % 2) * BL + b
                        act.wait_ge(s_fr[f], 16 * (j // 2) + 16)
                        nc.scalar.activation(jc[b][:, :], fr[f][:, :], ACT.Sign, bias=nhalf[:, t:t + 1], scale=-1.0,
                                             accum_out=fsum[:, t:t + 1]).then_inc(s_fs, 1)

                act.wait_ge(s_ln, 2)

                def normalise(g, e, n):
                    nt, rows = shape(g)
                    act.wait_ge(s_xg[e], n)
                    for t in range(nt):
                        k = g * GT + t
                        if not isinstance(g, int) or g >= 2:
                            act.wait_ge(s_kx, k - 2 * GT + 1)
                        nc.scalar.activation(xn[e][0:rows, t, :], xg[e][0:rows, t, :], ACT.Identity, bias=nmr[0:rows, bass.ds(k, 1)],
                                             scale=rstd[0:rows, bass.ds(k, 1)]).then_inc(s_xn, 1)

                def node_columns(g, t):
                    nt, rows = shape(g)
                    act.wait_ge(s_trx, g * GT + t + 1)
                    nc.scalar.copy(xT[:, :, t * P:t * P + rows],
                                   psT[t % 2][:, 0:2 * P].rearrange("p (c n) -> p c n", c=KF)[:, :, 0:rows]).then_inc(s_evx, 1)
                    if t == nt - 1:
                        act.wait_ge(s_evx, g * GT + nt)
                        act.dma_start(xT_d[bass.ds(g, 1), :, :, 0:nt * rows].rearrange("o p c n -> p (o c) n"), xT[:, :, 0:nt * rows]).then_inc(s_xTo, 16)

                def keys(g, t):
                    nt, rows = shape(g)
                    if t == 0:
                        act.wait_ge(s_rk, g * 2 + 2)
                    nc.scalar.activation(kc[0:rows, t, 0:NF], k2[0:rows, t, :], ACT.Copy, scale=rk[0:rows, t:t + 1]).then_inc(s_act, 1)
                    nc.scalar.activation(kc[0:rows, t, NF:2 * NF], k2[0:rows, t, :], ACT.Square, scale=rk[0:rows, t:t + 1]).then_inc(s_kk, 1)

                def squares(g, t):
                    nt, rows = shape(g)
                    k = g * GT + t
                    act.wait_ge(s_qk, k + 1)
                    if not isinstance(g, int) or g >= 1:
                        act.wait_ge(s_kk, k - GT + 1)
                        act.wait_ge(s_act, k - GT + 1)
                    col = bass.ds(k, 1)
                    nc.scalar.activation(q2[0:rows, t, :], psQ[t % 2][0:rows, 0:NF], ACT.Square,
                                         accum_out=q2s[0:rows, col]).then_inc(s_sq, 1)
                    nc.scalar.activation(k2[0:rows, t, :], psQ[t % 2][0:rows, NF:2 * NF], ACT.Square,
                                         accum_out=k2s[0:rows, t:t + 1]).then_inc(s_sq, 1)
                    act.wait_ge(s_sq, k * 3 + 2)
                    nc.scalar.activation(junk[0:rows, 0:NF], q2[0:rows, t, :], ACT.Square,
                                         accum_out=q4s[0:rows, col]).then_inc(s_sq, 1)

                def base_rows(g, t):
                    nt, rows = shape(g)
                    if t == 0 and (not isinstance(g, int) or g >= 1):
                        act.wait_ge(s_bo, g * 16)
                    act.wait_ge(s_ba, g * GT + t + 1)
                    nc.scalar.copy(bs[0:rows, t, :], psC[0:rows, 0:NF]).then_inc(s_bs, 1)
                    if t == nt - 1:
                        act.wait_ge(s_bs, g * GT + nt)
                        act.dma_start(base_d[bass.ds(g * GT * P, nt * rows), :].rearrange("(t p) f -> p t f", p=rows),
                                      bs[0:rows, 0:nt, :]).then_inc(s_bo, 16)

                def turn(g, e, n):
                    nt, rows = shape(g)
                    if not isinstance(g, int) or g >= 1:
                        act.wait_ge(s_xTo, g * 16)
                    for t in range(min(nt, 2)):
                        node_columns(g, t)
                    for t in range(GT):
                        if not isinstance(g, int) or g >= 1:
                            keys(g - 1, t)
                        if t < nt:
                            squares(g, t)
                            base_rows(g, t)
                        if t + 2 < nt:
                            node_columns(g, t + 2)
                    if not isinstance(g, int) or g + 2 <= GROUPS:
                        nt2, rows2 = shape(g + 2)
                        act.dma_start(xg[e][0:rows2, 0:nt2, :], x_group(g + 2, nt2, rows2)).then_inc(s_xg[e], 16)
                    if not isinstance(g, int) or g + 1 <= GROUPS:
                        normalise(g + 1, 1 - e, n)
                    if not isinstance(g, int) or g >= 1:
                        act.wait_ge(s_qTo, g * 16)
                    for t in range(nt):
                        act.wait_ge(s_trq, g * GT + t + 1)
                        nc.scalar.copy(qT[:, :, t * P:t * P + rows],
                                       psT[(nt + t) % 2][:, 0:2 * P].rearrange("p (c n) -> p c n", c=KF)[:, :, 0:rows]).then_inc(s_evq, 1)
                    act.wait_ge(s_evq, g * GT + nt)
                    act.dma_start(qT_d[bass.ds(g, 1), :, :, 0:nt * rows].rearrange("o p c n -> p (o c) n"), qT[:, :, 0:nt * rows]).then_inc(s_qTo, 16)

                FINE = {4: 0, 5: 1, 6: 2, 8: 3, 9: 4, 11: 5, 12: 6}
                normalise(0, 0, 16)
                for g in range(GROUPS + 1):
                    turn(g, g % 2, (g + 1) // 2 * 16 + 16)
                    if g in FINE:
                        fine(FINE[g])
                keys(GROUPS, 0)

                act.wait_ge(s_kx, TILES)
                nc.scalar.copy(krow[0:1, :], psR[0:1, :]).then_inc(s_act, 1)
                for c in range(KF):
                    nc.scalar.copy(kxT[:, c, :], psKx[c][:, 0:NF]).then_inc(s_act, 1)
                act.wait_ge(s_act, TILES + 1 + KF)
                act.sem_inc(s_at, 1)
                act.wait_ge(s_pt, 1)
                nc.scalar.sqrt(kcol[:, 0:2], psC[:, 510:512]).then_inc(s_at, 1)
                nc.scalar.sqrt(sd[:, :], q4s[:, :]).then_inc(s_at, 1)
                act.wait_ge(s_pt, 2)
                nc.scalar.copy(WvT[:, :, :], psQ[0][:, :].rearrange("p (c n) -> p c n", c=KF)).then_inc(s_at, 1)
                def fetch(g, e):
                    nt, rows = shape(g)
                    n = nt * rows
                    act.dma_start(sq[e][:, :, 0:n], qT_d[bass.ds(g, 1), :, :, 0:n].rearrange("o p c n -> p (o c) n")).then_inc(s_ap[e], 16)
                act.wait_ge(s_qTo, 16 * (GROUPS + 1))
                act.wait_ge(s_bo, 16 * (GROUPS + 1))
                fetch(0, 0)
                fetch(1, 1)
                act.wait_ge(s_fac, 1)
                act.wait_ge(s_pt, 3)
                for c in range(KF):
                    nc.scalar.activation(M[:, c, :], psQ[0][:, c * NF:(c + 1) * NF], ACT.Copy, scale=kcol[:, 4 + c:5 + c]).then_inc(s_at, 1)

                def attention_rows(g, e, n):
                    nt, rows = shape(g)
                    if not isinstance(g, int) or g >= 2:
                        act.wait_ge(s_t2o[e], n)
                    for t in range(nt):
                        k = g * GT + t
                        act.wait_ge(s_qm, k + 1)
                        nc.scalar.activation(stage[e][0:rows, t, :], psT[t % 2][0:rows, 0:NF], ACT.Copy,
                                             scale=rq[0:rows, bass.ds(k, 1)]).then_inc(s_t2, 1)
                    act.wait_ge(s_t2, g * GT + nt)
                    act.dma_start(att_d[bass.ds(g * GT * P, nt * rows), :].rearrange("(t p) f -> p t f", p=rows),
                                  stage[e][0:rows, 0:nt, :]).then_inc(s_t2o[e], 16)
                    if not isinstance(g, int) or g + 2 <= GROUPS:
                        fetch(g + 2, e)
                FINE2 = {2: 7, 9: 8}
                for g in range(GROUPS + 1):
                    attention_rows(g, g % 2, g // 2 * 16)
                    if g in FINE2:
                        fine(FINE2[g])
                fine(9)
                act.wait_ge(s_t2o[0], 16 * 7)
                act.wait_ge(s_t2o[1], 16 * 6)
                act.wait_ge(s_xTo, 16 * (GROUPS + 1))

            @block.tensor
            def _(pe):
                pe.wait_ge(s_const, 2)
                pe.wait_ge(s_cbc, 1)
                nc.tensor.matmul(psC[:, 0:SIDE], ones[0:1, :], crowf[0:1, :], start=True, stop=True).then_inc(s_pc0, 1)
                pe.wait_ge(s_wload, 16 * 8)
                for c in range(KF):
                    for d in range(KF):
                        ins = nc.tensor.transpose(psT[1][:, d * NF + c * P:d * NF + (c + 1) * P], Wv[:, c, d * P:(d + 1) * P], ident[:, :])
                ins.then_inc(s_wv, 1)
                for i in range(2):
                    nc.tensor.matmul(psR[0:1, 0:NF], ones[0:1, 0:1], b2r[0:1, i, :], start=(i == 0), stop=False)
                for d in range(KF):
                    nc.tensor.matmul(psR[0:1, 0:NF], bv[:, d:d + 1], Wo[:, d, :], start=False, stop=(d == KF - 1))
                pe.wait_ge(s_at, 1)
                for c in range(KF):
                    o = psQ[1][:, c * NF:(c + 1) * NF]
                    for d in range(KF):
                        nc.tensor.matmul(o, WvT[:, d, c * P:(c + 1) * P], Wo[:, d, :], start=(d == 0), stop=False)
                    ins = nc.tensor.matmul(psQ[1][:, c * (NF + P):c * (NF + P) + P], ident[:, :], ident[:, :], start=False, stop=True)
                ins.then_inc(s_wv, 1)

                def transpose_nodes(g, e, t):
                    nt, rows = shape(g)
                    k = g * GT + t
                    pe.wait_ge(s_xn, k + 1)
                    if t >= 2:
                        pe.wait_ge(s_evx, k - 1)
                    elif not isinstance(g, int) or g >= 1:
                        pe.wait_ge(s_evq, k - 1)
                    for c in range(KF):
                        ins = nc.tensor.transpose(psT[t % 2][:, c * P:c * P + rows], xn[e][0:rows, t, c * P:(c + 1) * P],
                                                  ident[0:rows, 0:rows])
                    ins.then_inc(s_trx, 1)

                def queries_and_keys(g, t):
                    nt, rows = shape(g)
                    k = g * GT + t
                    pe.wait_ge(s_evx, k + 1)
                    if not isinstance(g, int) or k >= 2:
                        pe.wait_ge(s_sq, k * 3 - 4)
                    o = psQ[t % 2][0:rows, :]
                    for i in range(2):
                        nc.tensor.matmul(o, one_r[0:1, 0:rows], bqs[i][0:1, :], start=(i == 0), stop=False)
                    for c in range(KF):
                        ins = nc.tensor.matmul(o, xT[:, c, t * P:t * P + rows], Wqk[:, c, :], start=False, stop=(c == KF - 1))
                    ins.then_inc(s_qk, 1)

                def base(g, e, t):
                    nt, rows = shape(g)
                    k = g * GT + t
                    if not isinstance(g, int) or k >= 1:
                        pe.wait_ge(s_bs, k)
                    o = psC[0:rows, 0:NF]
                    for i in range(2):
                        nc.tensor.matmul(o, one_r[0:1, 0:rows], brow[i][0:1, :], start=(i == 0), stop=False)
                    for c in range(KF):
                        nc.tensor.matmul(o, xT[:, c, t * P:t * P + rows], WvoI[:, c, :], start=False, stop=False)
                    nc.tensor.matmul(o, ident[0:rows, 0:rows], xg[e][0:rows, t, :], start=False, stop=True).then_inc(s_ba, 1)

                def key_products(g, e):
                    nt, rows = shape(g)
                    for t in range(nt):
                        pe.wait_ge(s_kk, g * GT + t + 1)
                        pe.wait_ge(s_act, g * GT + t + 1)
                        s_, e_ = isinstance(g, int) and g == 0 and t == 0, isinstance(g, int) and g == GROUPS
                        for c in range(KF):
                            nc.tensor.matmul(psKx[c][:, 0:NF], xn[e][0:rows, t, c * P:(c + 1) * P], kc[0:rows, t, 0:NF], start=s_, stop=e_)
                        nc.tensor.matmul(psR[0:1, :], ones[0:rows, 0:1], kc[0:rows, t, :], start=s_, stop=e_).then_inc(s_kx, 1)

                def turn(g, e):
                    nt, rows = shape(g)
                    for t in range(min(nt, 2)):
                        transpose_nodes(g, e, t)
                    for t in range(nt):
                        queries_and_keys(g, t)
                        base(g, e, t)
                        if t + 2 < nt:
                            transpose_nodes(g, e, t + 2)
                    if not isinstance(g, int) or g >= 1:
                        key_products(g - 1, 1 - e)
                    for t in range(nt):
                        k = g * GT + t
                        pe.wait_ge(s_sq, k * 3 + 1)
                        if t >= 2:
                            pe.wait_ge(s_evq, k - 1)
                        elif nt == GT:
                            pe.wait_ge(s_evx, k + 3)
                        else:
                            pe.wait_ge(s_evq, k)
                        for c in range(KF):
                            ins = nc.tensor.transpose(psT[(nt + t) % 2][:, c * P:c * P + rows], q2[0:rows, t, c * P:(c + 1) * P],
                                                      ident[0:rows, 0:rows])
                        ins.then_inc(s_trq, 1)

                pe.wait_ge(s_wq, 1)
                pe.wait_ge(s_bw, 2)
                pe.wait_ge(s_csum, TILES)
                for g in range(2):
                    turn(g, g)
                with pe.Fori(1, 6) as h:
                    for e in range(2):
                        turn(h * 2 + e, e)
                turn(GROUPS, 0)
                key_products(GROUPS, 0)

                pe.wait_ge(s_evq, TILES)
                pe.wait_ge(s_bs, TILES)
                pe.wait_ge(s_at, 2)
                for c in range(KF):
                    ins = nc.tensor.matmul(psC[:, 510 + c:511 + c], krow[0:1, NF + c * P:NF + (c + 1) * P], ones[0:1, 0:1],
                                           start=True, stop=True)
                ins.then_inc(s_pt, 1)
                for d in range(KF):
                    o = psQ[0][:, d * NF:(d + 1) * NF]
                    for c in range(KF):
                        nc.tensor.matmul(o, Wv[:, c, d * P:(d + 1) * P], kxT[:, c, :], start=(c == 0), stop=False)
                    ins = nc.tensor.matmul(o, bqk[0:1, 2 * NF + d * P:2 * NF + (d + 1) * P], krow[0:1, 0:NF], start=False, stop=True)
                ins.then_inc(s_pt, 1)
                pe.wait_ge(s_at, 5)
                for c in range(KF):
                    for d in range(KF):
                        ins = nc.tensor.matmul(psQ[0][:, c * NF:(c + 1) * NF], WvT[:, d, c * P:(c + 1) * P], Wo[:, d, :],
                                               start=(d == 0), stop=(d == KF - 1))
                ins.then_inc(s_pt, 1)
                pe.wait_ge(s_at, 5 + KF)

                def attention(g, e, n):
                    nt, rows = shape(g)
                    pe.wait_ge(s_ap[e], n)
                    for t in range(nt):
                        k = g * GT + t
                        if not isinstance(g, int) or k >= 2:
                            pe.wait_ge(s_t2, k - 1)
                        for c in range(KF):
                            ins = nc.tensor.matmul(psT[t % 2][0:rows, 0:NF], sq[e][:, c, t * P:t * P + rows], M[:, c, :],
                                                   start=(c == 0), stop=(c == KF - 1))
                        ins.then_inc(s_qm, 1)
                for g in range(2):
                    attention(g, g, 16)
                with pe.Fori(1, 6) as h:
                    for e in range(2):
                        attention(h * 2 + e, e, h * 16 + 16)
                attention(GROUPS, 0, 112)


        ctx2 = ExitStack()
        wsb = lambda n, s: [ctx2.enter_context(nc.sbuf_tensor(n + h, s, f32r)) for h in ("_hi", "_lo")]
        W1f = wsb("W1f", [P, 4, HID])
        W1t = ctx2.enter_context(nc.sbuf_tensor("W1t", [3 * TAIL + 2, HID], f32r))
        W2s = wsb("W2s", [P, KH, NF])
        wrb = ctx2.enter_context(nc.sbuf_tensor("wrb", [P, NF + 1], f32))

        with ExitStack() as ctx:
            sb = lambda n, s, d=f32: ctx.enter_context(nc.sbuf_tensor(n, s, d))
            ps = lambda n, s: ctx.enter_context(nc.psum_tensor(n, s, f32))
            sem = lambda n: ctx.enter_context(nc.semaphore(n))
            rW1f = sb("rW1f", [P, 4, HID])
            rW1t = sb("rW1t", [3 * TAIL + 2, HID])
            rW2 = sb("rW2", [P, KH, NF])
            W1u = sb("W1u", [GF, HID])
            u0 = sb("u0", [GF, 1])
            b1r = sb("b1r", [1, HID])
            b1s = sb("b1s", [1, HID])
            b1h = sb("b1h", [1, HID], f32r)
            b1l = sb("b1l", [1, HID], f32r)
            wrow = sb("wrow", [1, NF + 1])
            diag = sb("diag", [P, P])
            cT = sb("cT", [EF, 4, P])
            cs = sb("cs", [EF, 2, P])
            cr = sb("cr", [P, AGG])
            a1, a2, a3, a4, a5 = (sb(f"p{i}", [P, TILES]) for i in range(5))
            ai = sb("ai", [P, TILES], i32)
            psC = ps("psC2", [P, 512])
            psD = ps("psD", [P, 512])
            psS = ps("psS", [P, 512])
            psB = [ps(f"psB{i}", [P, 512]) for i in range(3)]
            s_v = sem("p_v")
            s_diag = sem("p_diag")
            s_t = sem("p_t")
            s_scan = sem("p_scan")
            s_cr = sem("p_cr")
            s_sh = sem("p_sh")
            s_cro = sem("p_cro")
            s_wu = sem("p_wu")
            s_wl = [sem(f"p_wl{i}") for i in range(4)]
            s_b1 = sem("p_b1")
            s_b1s = sem("p_b1s")
            s_b1o = sem("p_b1o")
            s_hi = sem("p_hi")
            s_lo = sem("p_lo")
            s_lo2 = sem("p_lo2")
            s_wrb = sem("p_wrb")
            block = ctx.enter_context(nc.Block())

            @block.sync
            def _(sp):
                sp.wait_ge(s_wu, 16 * 5)
                for i in range(2):
                    sp.dma_start(rW1f[:, 2 * i:2 * i + 2, :],
                                 W1[2 * i * P:(2 * i + 2) * P, :].rearrange("(c p) n -> p c n", p=P)).then_inc(s_wl[i], 16)
                for i in range(3):
                    sp.dma_start(rW1t[i * TAIL:(i + 1) * TAIL, :], W1[4 * P:4 * P + TAIL, :]).then_inc(s_wl[2], 16)
                sp.dma_start(rW2[:, :, :], W2.rearrange("(c p) n -> p c n", p=P)).then_inc(s_wl[3], 16)
                sp.wait_ge(s_cr, 2)
                sp.dma_start(carry_d, cr[:, :]).then_inc(s_cro, 16)
                sp.wait_ge(s_b1s, 4)
                sp.dma_start(rW1t[3 * TAIL:3 * TAIL + 1, :], b1h[0:1, :].bitcast(f32)).then_inc(s_b1o, 16)
                sp.dma_start(rW1t[3 * TAIL + 1:3 * TAIL + 2, :], b1l[0:1, :].bitcast(f32)).then_inc(s_b1o, 16)
                sp.wait_ge(s_cro, 16)
                sp.wait_ge(s_b1o, 32)

            @block.scalar
            def _(act):
                act.dma_start(W1u[:, :], W1[NF + 3 * EF:NF + 3 * EF + GF, :]).then_inc(s_wu, 16)
                act.dma_start(u0[:, :], u[0:1, :].rearrange("a b -> b a")).then_inc(s_wu, 16)
                act.dma_start(b1r[0:1, :], b1.rearrange("(a b) -> a b", a=1)).then_inc(s_wu, 16)
                act.dma_start(wrow[0:1, 0:NF], wr.rearrange("a b -> b a")).then_inc(s_wu, 16)
                act.dma_start(wrow[0:1, NF:NF + 1], br.rearrange("(a b) -> a b", a=1)).then_inc(s_wu, 16)
                act.wait_ge(s_b1, 3)
                nc.scalar.copy(wrb[:, :], psB[2][:, 0:NF + 1]).then_inc(s_wrb, 1)
                for i in range(2):
                    act.wait_ge(s_wl[i], 16)
                    nc.scalar.copy(W1f[0][:, 2 * i:2 * i + 2, :], rW1f[:, 2 * i:2 * i + 2, :]).then_inc(s_hi, 1)
                act.wait_ge(s_wl[2], 48)
                nc.scalar.copy(W1t[0:3 * TAIL, :], rW1t[0:3 * TAIL, :]).then_inc(s_hi, 1)
                act.wait_ge(s_wl[3], 16)
                nc.scalar.copy(W2s[0][:, :, :], rW2[:, :, :]).then_inc(s_hi, 1)
                act.wait_ge(s_b1o, 32)
                nc.scalar.copy(W1t[3 * TAIL:3 * TAIL + 2, :], rW1t[3 * TAIL:3 * TAIL + 2, :]).then_inc(s_hi, 1)

            @block.gpsimd
            def _(pool):
                pool.wait_ge(s_hi, 1)
                nc.gpsimd.tensor_tensor(W1f[1][:, 0:2, :], rW1f[:, 0:2, :], W1f[0][:, 0:2, :].bitcast(f32), ALU.subtract).then_inc(s_lo, 1)
                pool.wait_ge(s_hi, 4)
                nc.gpsimd.tensor_tensor(W2s[1][:, :, :], rW2[:, :, :], W2s[0][:, :, :].bitcast(f32), ALU.subtract).then_inc(s_lo, 1)

            @block.tensor
            def _(pe):
                pe.wait_ge(s_diag, 1)
                nc.tensor.transpose(psC[0:EF, 0:P], ends[:, 0:EF], ident[:, :])
                nc.tensor.transpose(psC[0:EF, P:2 * P], ends[:, EF:AGG], ident[:, :])
                nc.tensor.matmul(psC[0:EF, 2 * P:3 * P], ones[:, 0:EF], diag[:, :], start=True, stop=True).then_inc(s_t, 1)
                nc.tensor.matmul(psS[:, 0:TILES], shift[:, :], Eend[:, :], start=True, stop=False)
                nc.tensor.matmul(psS[:, 1:TILES], corner[:, :], Eend[:, 0:TILES - 1], start=False, stop=True).then_inc(s_sh, 1)
                pe.wait_ge(s_wu, 16 * 5)
                for i in range(2):
                    nc.tensor.matmul(psB[i][0:1, :], u0[:, :], W1u[:, i * 512:(i + 1) * 512], start=True, stop=True).then_inc(s_b1, 1)
                nc.tensor.matmul(psB[2][:, 0:NF + 1], ones[0:1, :], wrow[0:1, :], start=True, stop=True).then_inc(s_b1, 1)
                pe.wait_ge(s_scan, 2)
                for h in range(2):
                    ins = nc.tensor.transpose(psD[:, h * P:h * P + EF], cs[:, h, :], ident[0:EF, 0:EF])
                ins.then_inc(s_t, 1)

            @block.vector
            def _(dve):
                nv = [0]

                def step(ins, wait=True):
                    nv[0] += 1
                    ins.then_inc(s_v, 1)
                    if wait:
                        dve.wait_ge(s_v, nv[0])

                nc.vector.tensor_scalar(diag[:, :], ident[:, :], keepc[:, 0:1], None, ALU.mult).then_inc(s_diag, 1)
                dve.wait_ge(s_t, 1)
                step(nc.vector.tensor_copy(cT[:, 0, :], psC[0:EF, 2 * P:3 * P]), False)
                step(nc.vector.tensor_copy(cT[:, 2, :], psC[0:EF, 0:P]), False)
                step(nc.vector.tensor_copy(cT[:, 3, :], psC[0:EF, P:2 * P]))
                step(nc.vector.tensor_scalar(cT[:, 1, :], cT[:, 0, :], 0.5, 2.0, ALU.subtract, ALU.mult))
                step(nc.vector.tensor_scalar(cT[:, 1, :], cT[:, 1, :], FMAX, None, ALU.mult))
                nc.vector.tensor_tensor_scan(cs[:, 0, :], cT[:, 1, :], cT[:, 2, :], -FMAX, ALU.min, ALU.max).then_inc(s_scan, 1)
                nc.vector.tensor_tensor_scan(cs[:, 1, :], cT[:, 0, :], cT[:, 3, :], 0.0, ALU.mult, ALU.add).then_inc(s_scan, 1)
                dve.wait_ge(s_sh, 1)
                step(nc.vector.tensor_copy(Sbeg[:, :], psS[:, 0:TILES]))
                step(nc.vector.tensor_tensor(a1[:, :], Eend[:, :], Sbeg[:, :], ALU.subtract))
                step(nc.vector.tensor_scalar(has[:, :], a1[:, :], 0.0, None, ALU.is_gt), False)
                step(nc.vector.tensor_scalar(a2[:, :], a1[:, :], 1.0, None, ALU.max))
                step(nc.vector.tensor_scalar(a1[:, :], Eend[:, :], 1.0, 0.0, ALU.subtract, ALU.max))
                step(nc.vector.reciprocal(rcnt[:, :], a2[:, :]), False)
                step(nc.vector.tensor_copy(ai[:, :], a1[:, :]))
                step(nc.vector.tensor_scalar(iRaw, ai[:, :], 2, None, ALU.logical_shift_right))
                step(nc.vector.tensor_copy(a2[:, :], iRaw))
                step(nc.vector.scalar_tensor_tensor(a3[:, :], a2[:, :], -4.0, a1[:, :], ALU.mult, ALU.add))
                step(nc.vector.tensor_scalar(a3[:, :], a3[:, :], 3.0, None, ALU.is_equal))
                dve.wait_ge(s_t, 2)
                for h in range(2):
                    nc.vector.tensor_copy(cr[:, h * EF:(h + 1) * EF], psD[:, h * P:h * P + EF]).then_inc(s_cr, 1)
                dve.wait_ge(s_b1, 2)
                for i in range(2):
                    nc.vector.tensor_tensor(b1s[0:1, i * 512:(i + 1) * 512], b1r[0:1, i * 512:(i + 1) * 512], psB[i][0:1, :],
                                            ALU.add).then_inc(s_b1s, 1)
                dve.wait_ge(s_b1s, 2)
                nc.vector.tensor_copy(b1h[0:1, :], b1s[0:1, :]).then_inc(s_b1s, 1)
                dve.wait_ge(s_b1s, 3)
                nc.vector.tensor_tensor(b1l[0:1, :], b1s[0:1, :], b1h[0:1, :].bitcast(f32), ALU.subtract).then_inc(s_b1s, 1)
                for i in range(3):
                    step(nc.vector.tensor_scalar(a4[:, :], a2[:, :], 4.0, float(i), ALU.mult, ALU.add))
                    step(nc.vector.tensor_tensor(a5[:, :], a4[:, :], a1[:, :], ALU.is_le), False)
                    step(nc.vector.tensor_tensor(a4[:, :], a4[:, :], Sbeg[:, :], ALU.is_ge))
                    step(nc.vector.tensor_tensor(a4[:, :], a4[:, :], a5[:, :], ALU.mult))
                    step(nc.vector.tensor_tensor(a4[:, :], a4[:, :], has[:, :], ALU.mult), False)
                    step(nc.vector.tensor_scalar(a5[:, :], a3[:, :], -1.0, 1.0, ALU.mult, ALU.add))
                    step(nc.vector.tensor_tensor(kSel[:, i, :], a4[:, :], a5[:, :], ALU.mult))
                step(nc.vector.tensor_tensor(a2[:, :], a2[:, :], a3[:, :], ALU.add))
                step(nc.vector.tensor_scalar(a4[:, :], a2[:, :], 4.0, -1.0, ALU.mult, ALU.add), False)
                step(nc.vector.tensor_scalar(a3[:, :], a2[:, :], 1.0, 0.0, ALU.subtract, ALU.max))
                step(nc.vector.tensor_tensor(a4[:, :], Sbeg[:, :], a4[:, :], ALU.is_le), False)
                step(nc.vector.tensor_copy(iScan, a3[:, :]))
                step(nc.vector.tensor_tensor(kSel[:, 3, :], a4[:, :], has[:, :], ALU.mult), False)
                step(nc.vector.tensor_scalar(a2[:, :], a3[:, :], 1.0 / Q, None, ALU.mult))
                step(nc.vector.tensor_copy(ai[:, :], a2[:, :]))
                step(nc.vector.tensor_copy(a2[:, :], ai[:, :]))
                step(nc.vector.scalar_tensor_tensor(a4[:, :], a2[:, :], -float(Q), a3[:, :], ALU.mult, ALU.add))
                step(nc.vector.tensor_scalar(a5[:, :], a4[:, :], 0.0, None, ALU.is_lt), False)
                step(nc.vector.tensor_scalar(a3[:, :], a4[:, :], float(Q), None, ALU.is_ge))
                step(nc.vector.tensor_tensor(a2[:, :], a2[:, :], a5[:, :], ALU.subtract))
                step(nc.vector.tensor_tensor(a2[:, :], a2[:, :], a3[:, :], ALU.add))
                step(nc.vector.tensor_scalar(a4[:, :], a2[:, :], float(R), None, ALU.mult), False)
                step(nc.vector.tensor_scalar(a3[:, :], a2[:, :], 1.0, 0.0, ALU.subtract, ALU.max))
                step(nc.vector.tensor_tensor(a4[:, :], Sbeg[:, :], a4[:, :], ALU.is_lt), False)
                step(nc.vector.tensor_copy(iCarry, a3[:, :]))
                step(nc.vector.tensor_tensor(kSel[:, 4, :], a4[:, :], has[:, :], ALU.mult))
                step(nc.vector.tensor_scalar(mSel[:, :, :], kSel[:, :, :], 0.5, 2.0, ALU.subtract, ALU.mult))
                step(nc.vector.tensor_scalar(mSel[:, :, :], mSel[:, :, :], FMAX, None, ALU.mult))
                dve.wait_ge(s_hi, 3)
                nc.vector.tensor_tensor(W1f[1][:, 2:4, :], rW1f[:, 2:4, :], W1f[0][:, 2:4, :].bitcast(f32), ALU.subtract).then_inc(s_lo2, 1)
                t_ = slice(TAIL, 2 * TAIL)
                nc.vector.tensor_tensor(W1t[t_, :], rW1t[t_, :], W1t[t_, :].bitcast(f32), ALU.subtract).then_inc(s_lo2, 1)

        with ExitStack() as ctx:
            sb = lambda n, s, d=f32: ctx.enter_context(nc.sbuf_tensor(n, s, d))
            ps = lambda n, s: ctx.enter_context(nc.psum_tensor(n, s, f32))
            sem = lambda n: ctx.enter_context(nc.semaphore(n))
            pair = lambda n, s: [sb(n + h, s, f32r) for h in ("_hi", "_lo")]
            xTr = [sb(f"xTr{i}", [P, KF, GT * P]) for i in range(2)]
            xTs = pair("xTs", [P, KF, GT * P])
            bg = [sb(f"bg{i}", [P, GT, NF]) for i in range(2)]
            tg = [sb(f"tg{i}", [P, GT, NF]) for i in range(2)]
            graw = [sb(f"graw{i}", [P, GT, 4 * EF]) for i in range(2)]
            gscan = [sb(f"gscan{i}", [P, GT, AGG]) for i in range(2)]
            gcar = [sb(f"gcar{i}", [P, GT, AGG]) for i in range(2)]
            ic = [sb(f"ic{i}", [P, 3, GT], i32) for i in range(2)]
            agg = sb("agg", [P, GT, AW])
            aggT = pair("aggT", [P, 2, GT * P])
            tailT = sb("tailT", [3 * TAIL + 2, GT * P], f32r)
            hT = pair("hT", [P, KH, GT * P])
            x2 = sb("x2", [P, GT, NF])
            yr = sb("yr", [P, GT, YROW])
            prod = sb("prod", [P, NF])
            st2 = sb("st2", [P, GT, 6])
            mean2 = sb("mean2", [P, GT])
            t2 = sb("t2", [P, GT])
            wst = sb("wst", [P, GT])
            va2 = sb("va2", [P, GT])
            sd2 = sb("sd2", [P, GT])
            t1 = sb("t1", [P, GT])
            rs2 = sb("rs2", [P, GT])
            nm2 = sb("nm2", [P, GT])
            psA = [ps(f"psA{i}", [P, 512]) for i in range(2)]
            psH = [ps(f"psH{i}", [P, 512]) for i in range(4)]
            psO = [ps(f"psO{i}", [P, 512]) for i in range(2)]
            s_one = sem("b_one")
            s_u = sem("b_u")
            s_lb = [sem(f"b_lb{i}") for i in range(2)]
            s_bsum = sem("b_bsum")
            s_ld = [sem(f"b_ld{i}") for i in range(2)]
            s_ga = [sem(f"b_ga{i}") for i in range(2)]
            s_am = sem("b_am")
            s_ic = sem("b_ic")
            s_turn = sem("b_turn")
            s_as = sem("b_as")
            s_A = sem("b_A")
            s_ah = sem("b_ah")
            s_al = sem("b_al")
            s_xh = sem("b_xh")
            s_xl = sem("b_xl")
            s_h = sem("b_h")
            s_rh = sem("b_rh")
            s_rl = sem("b_rl")
            s_o = sem("b_o")
            s_x2 = sem("b_x2")
            s_ln2 = sem("b_ln2")
            s_va = sem("b_va")
            s_sq2 = sem("b_sq2")
            s_fin = sem("b_fin")
            s_dev = sem("b_dev")
            s_y = sem("b_y")
            s_res = sem("b_res")
            s_st = sem("b_st")
            s_wg = sem("b_wg")
            raw_v = edges.rearrange("(q i) f -> q (i f)", i=4)
            NVA = 13
            NAS = 7
            NFIN = 2

            def shape(g):
                return (1, LAST) if isinstance(g, int) and g == GROUPS else (GT, P)

            block = ctx.enter_context(nc.Block())

            @block.sync
            def _(sp):
                def load(g, e):
                    nt, rows = shape(g)
                    n = nt * rows
                    sp.dma_start(xTr[e][:, :, 0:n], xT_d[bass.ds(g, 1), :, :, 0:n].rearrange("o p c n -> p (o c) n")).then_inc(s_ld[e], 16)
                    sp.dma_start(bg[e][0:rows, 0:nt, :],
                                 base_d[bass.ds(g * GT * P, n), :].rearrange("(t p) f -> p t f", p=rows)).then_inc(s_lb[e], 16)
                    sp.dma_start(tg[e][0:rows, 0:nt, :],
                                 att_d[bass.ds(g * GT * P, n), :].rearrange("(t p) f -> p t f", p=rows)).then_inc(s_lb[e], 16)

                def store(g):
                    nt, rows = shape(g)
                    sp.wait_ge(s_fin, g * (GT * NFIN) + nt * NFIN)
                    sp.wait_ge(s_res, g + 1)
                    r0 = bass.ds(g * GT * P, nt * rows)
                    sp.dma_start(yrow_d[r0, :].rearrange("(t p) f -> p t f", p=rows), yr[0:rows, 0:nt, :]).then_inc(s_st, 16)
                    sp.dma_start(out[r0, :].rearrange("(t p) f -> p t f", p=rows), yr[0:rows, 0:nt, NF:2 * NF]).then_inc(s_st, 16)

                def turn(g, e):
                    nt, rows = shape(g)
                    if not isinstance(g, int) or g >= 1:
                        store(g - 1)
                    if not isinstance(g, int) or g + 2 <= GROUPS:
                        sp.wait_ge(s_xl, g + 1)
                        sp.wait_ge(s_x2, g * GT + nt)
                        load(g + 2, e)

                load(0, 0)
                load(1, 1)
                for g in range(2):
                    turn(g, g)
                with sp.Fori(1, 5) as h:
                    for e in range(2):
                        turn(h * 2 + e, e)
                for g in range(10, 13):
                    turn(g, g % 2)
                store(GROUPS)
                sp.wait_ge(s_st, 32 * (GROUPS + 1))

            @block.gpsimd
            def _(pool):
                def gather(g, e):
                    nt, rows = shape(g)
                    if not isinstance(g, int) or g >= 2:
                        pool.wait_ge(s_am, g * (6 * GT) - 6 * GT)
                        pool.wait_ge(s_as, g * (NAS * GT) - NAS * GT)
                    nc.gpsimd.tensor_copy(ic[e][0:rows, :, 0:nt], idx[0:rows, :, bass.ds(g * GT, nt)]).then_inc(s_ic, 1)
                    pool.wait_ge(s_ic, g + 1)
                    pool.sem_inc(s_turn, 1)
                    for t in range(nt):
                        for i, (buf, src) in enumerate(((graw, raw_v), (gscan, scan_d), (gcar, carry_d))):
                            nc.gpsimd.indirect_dma_start(
                                out=buf[e][0:rows, t, :], out_offset=None, in_=src,
                                in_offset=bass.IndirectOffsetOnAxis(ap=ic[e][0:rows, i, t:t + 1], axis=0)).then_inc(s_ga[e], 16)

                def add_attention(g, e, n):
                    nt, rows = shape(g)
                    pool.wait_ge(s_lb[e], n)
                    nc.gpsimd.tensor_tensor(bg[e][0:rows, 0:nt, :], bg[e][0:rows, 0:nt, :], tg[e][0:rows, 0:nt, :], ALU.add).then_inc(s_bsum, 1)

                def residual(g):
                    nt, rows = shape(g)
                    pool.wait_ge(s_y, g * GT + nt)
                    nc.gpsimd.tensor_tensor(yr[0:rows, 0:nt, NF:2 * NF], x2[0:rows, 0:nt, :], yr[0:rows, 0:nt, 0:NF], ALU.add).then_inc(s_res, 1)

                gather(0, 0)
                gather(1, 1)
                add_attention(0, 0, 32)
                add_attention(1, 1, 32)
                gather(2, 0)
                add_attention(2, 0, 64)
                gather(3, 1)
                residual(0)
                add_attention(3, 1, 64)
                with pool.Fori(2, 6) as h:
                    for e in range(2):
                        gather(h * 2 + e, e)
                        residual(h * 2 + e - 3)
                        add_attention(h * 2 + e, e, h * 32 + 32)
                gather(GROUPS, 0)
                residual(GROUPS - 3)
                add_attention(GROUPS, 0, 7 * 32)
                for g in range(GROUPS - 2, GROUPS + 1):
                    residual(g)

            @block.vector
            def _(dve):
                def aggregate(g, e, h, t):
                    nt, rows = shape(g)
                    if t == 0:
                        dve.wait_ge(s_ga[e], h * (48 * GT) + 48 * nt)
                        if not isinstance(g, int) or g >= 1:
                            dve.wait_ge(s_A, g * GT)
                    col = bass.ds(g * GT + t, 1)
                    src = [graw[e][0:rows, t, i * EF:(i + 1) * EF] for i in range(3)]
                    mxs = src + [gscan[e][0:rows, t, 0:EF], gcar[e][0:rows, t, 0:EF]]
                    sms = src + [gscan[e][0:rows, t, EF:AGG], gcar[e][0:rows, t, EF:AGG]]
                    am, asum = agg[0:rows, t, EF:2 * EF], agg[0:rows, t, 0:EF]
                    for i in range(5):
                        mcol, kcol_ = mSel[0:rows, i, col], kSel[0:rows, i, col]
                        if i == 0:
                            nc.vector.tensor_scalar(am, mxs[0], mcol, None, ALU.min).then_inc(s_am, 1)
                            nc.vector.tensor_scalar(asum, sms[0], kcol_, None, ALU.mult).then_inc(s_as, 1)
                        else:
                            dve.wait_ge(s_am, g * (6 * GT) + 6 * t + i)
                            nc.vector.scalar_tensor_tensor(am, mxs[i], mcol, am, ALU.min, ALU.max).then_inc(s_am, 1)
                            dve.wait_ge(s_as, g * (NAS * GT) + NAS * t + i)
                            nc.vector.scalar_tensor_tensor(asum, sms[i], kcol_, asum, ALU.mult, ALU.add).then_inc(s_as, 1)
                    dve.wait_ge(s_am, g * (6 * GT) + 6 * t + 5)
                    nc.vector.tensor_scalar(am, am, has[0:rows, col], None, ALU.mult).then_inc(s_am, 1)
                    dve.wait_ge(s_as, g * (NAS * GT) + NAS * t + 5)
                    nc.vector.tensor_scalar(agg[0:rows, t, 2 * EF:3 * EF], asum, rcnt[0:rows, col], None, ALU.mult).then_inc(s_as, 1)
                    nc.vector.tensor_scalar(agg[0:rows, t, 3 * EF:AW].rearrange("p (c f) -> p c f", c=2),
                                            agg[0:rows, t, EF - TAIL:EF].rearrange("p (c f) -> p c f", c=1).broadcast_to([rows, 2, TAIL]),
                                            rcnt[0:rows, col], None, ALU.mult).then_inc(s_as, 1)

                def aggregates_low(g, t):
                    nt, rows = shape(g)
                    dve.wait_ge(s_ah, g * (2 * GT) + 2 * t + 2)
                    cols, r = slice(t * P, t * P + rows), slice(2 * TAIL, 3 * TAIL)
                    nc.vector.tensor_tensor(aggT[1][:, :, cols],
                                            psA[t % 2][:, 0:2 * P].rearrange("p (c n) -> p c n", c=2)[:, :, 0:rows],
                                            aggT[0][:, :, cols].bitcast(f32), ALU.subtract).then_inc(s_al, 1)
                    nc.vector.tensor_tensor(tailT[r, cols], psA[t % 2][r, 2 * P:2 * P + rows], tailT[r, cols].bitcast(f32),
                                            ALU.subtract).then_inc(s_al, 1)

                def nodes_low(g, e):
                    nt, rows = shape(g)
                    dve.wait_ge(s_xh, g + 1)
                    n = slice(0, nt * rows)
                    nc.vector.tensor_tensor(xTs[1][:, :, n], xTr[e][:, :, n], xTs[0][:, :, n].bitcast(f32), ALU.subtract).then_inc(s_xl, 1)

                def relu_low(g, m):
                    nt, rows = shape(g)
                    n = slice(0, nt * rows)
                    dve.wait_ge(s_rh, g * KH + m + 1)
                    nc.vector.scalar_tensor_tensor(hT[1][:, m, n], psH[m % 4][:, n], 0.0, hT[0][:, m, n].bitcast(f32),
                                                   ALU.max, ALU.subtract).then_inc(s_rl, 1)

                def add_up(g, e, t):
                    nt, rows = shape(g)
                    k = g * GT + t
                    dve.wait_ge(s_o, k + 1)
                    nc.vector.tensor_tensor(x2[0:rows, t, :], bg[e][0:rows, t, :], psO[t % 2][0:rows, 0:NF], ALU.add).then_inc(s_x2, 1)
                    dve.wait_ge(s_x2, k + 1)
                    nc.vector.bn_stats(st2[0:rows, t, :], x2[0:rows, t, :]).then_inc(s_ln2, 1)

                def variances(g):
                    nt, rows = shape(g)
                    dve.wait_ge(s_ln2, g * GT + nt)
                    r, n = slice(0, rows), slice(0, nt)
                    nc.vector.tensor_tensor(mean2[r, n], st2[r, n, 1], st2[r, n, 4], ALU.add).then_inc(s_va, 1)
                    nc.vector.tensor_tensor(t1[r, n], st2[r, n, 1], st2[r, n, 4], ALU.subtract).then_inc(s_va, 1)
                    nc.vector.tensor_tensor(t2[r, n], st2[r, n, 2], st2[r, n, 5], ALU.add).then_inc(s_va, 1)
                    dve.wait_ge(s_va, g * NVA + 3)
                    nc.vector.tensor_scalar(mean2[r, n], mean2[r, n], 0.5, None, ALU.mult).then_inc(s_va, 1)
                    nc.vector.scalar_tensor_tensor(t1[r, n], t1[r, n], 0.25, t1[r, n], ALU.mult, ALU.mult).then_inc(s_va, 1)
                    dve.wait_ge(s_va, g * NVA + 5)
                    nc.vector.scalar_tensor_tensor(va2[r, n], t2[r, n], 1.0 / NF, t1[r, n], ALU.mult, ALU.add).then_inc(s_va, 1)
                    dve.wait_ge(s_va, g * NVA + 6)
                    nc.vector.tensor_scalar(va2[r, n], va2[r, n], EPS, None, ALU.add).then_inc(s_va, 1)

                def deviation(g):
                    nt, rows = shape(g)
                    dve.wait_ge(s_sq2, g + 1)
                    r, n = slice(0, rows), slice(0, nt)
                    nc.vector.reciprocal(t1[r, n], sd2[r, n]).then_inc(s_va, 1)
                    dve.wait_ge(s_va, g * NVA + 8)
                    nc.vector.tensor_tensor(t1[r, n], va2[r, n], t1[r, n], ALU.mult).then_inc(s_va, 1)
                    dve.wait_ge(s_va, g * NVA + 9)
                    nc.vector.tensor_tensor(t1[r, n], t1[r, n], sd2[r, n], ALU.add).then_inc(s_va, 1)
                    dve.wait_ge(s_va, g * NVA + 10)
                    nc.vector.tensor_scalar(t1[r, n], t1[r, n], 0.5, None, ALU.mult).then_inc(s_va, 1)
                    dve.wait_ge(s_va, g * NVA + 11)
                    nc.vector.reciprocal(rs2[r, n], t1[r, n]).then_inc(s_va, 1)
                    dve.wait_ge(s_va, g * NVA + 12)
                    nc.vector.scalar_tensor_tensor(nm2[r, n], mean2[r, n], -1.0, rs2[r, n], ALU.mult, ALU.mult).then_inc(s_va, 1)

                def finish(g, t):
                    nt, rows = shape(g)
                    r = slice(0, rows)
                    k0 = g * (GT * NFIN) + t * NFIN
                    dve.wait_ge(s_y, g * GT + t + 1)
                    nc.vector.tensor_tensor_reduce(out=prod[r, :], in0=yr[r, t, 0:NF], in1=wrb[r, 0:NF], scale=1.0, scalar=wrb[r, NF:NF + 1],
                                                   op0=ALU.mult, op1=ALU.add, accum_out=wst[r, t:t + 1]).then_inc(s_fin, 1)
                    dve.wait_ge(s_fin, k0 + 1)
                    nc.vector.tensor_copy(yr[r, t, 2 * NF:YROW], wst[r, t:t + 1].broadcast_to([rows, YROW - 2 * NF])).then_inc(s_fin, 1)
                    if t == nt - 1:
                        nc.vector.tensor_copy(wgt[r, bass.ds(g * GT, nt)], wst[r, 0:nt]).then_inc(s_wg, 1)

                nc.vector.memset(wgt[:, :], 0.0).then_inc(s_u, 1)
                dve.wait_ge(s_u, 1)
                for t in range(GT):
                    aggregate(0, 0, 0, t)
                    if t >= 2:
                        aggregates_low(0, t - 2)
                nodes_low(0, 0)
                aggregates_low(0, 2)
                aggregates_low(0, 3)

                def turn(g, e, h):
                    nxt = not isinstance(g, int) or g < GROUPS
                    for m in range(KH):
                        relu_low(g, m)
                        if m < GT and nxt and m < shape(g + 1)[0]:
                            aggregate(g + 1, 1 - e, h + e, m)
                        if m == GT - 2 and (not isinstance(g, int) or g >= 1):
                            deviation(g - 1)
                        if m >= GT and (not isinstance(g, int) or g >= 1):
                            finish(g - 1, m - GT)
                    after = shape(g + 1)[0] if nxt else 0
                    for t in range(min(after, 2)):
                        aggregates_low(g + 1, t)
                    if nxt:
                        nodes_low(g + 1, 1 - e)
                    dve.wait_ge(s_bsum, g + 1)
                    if not isinstance(g, int) or g >= 1:
                        dve.wait_ge(s_res, g)
                    for t in range(shape(g)[0]):
                        add_up(g, e, t)
                        if t + 2 < after:
                            aggregates_low(g + 1, t + 2)
                    variances(g)
                for g in range(2):
                    turn(g, g, 0)
                with dve.Fori(1, 5) as h:
                    for e in range(2):
                        turn(h * 2 + e, e, h)
                for g in range(10, 13):
                    turn(g, g % 2, g // 2)
                deviation(GROUPS)
                finish(GROUPS, 0)

            @block.scalar
            def _(act):
                nc.scalar.copy(tailT[3 * TAIL:3 * TAIL + 2, :].rearrange("o (t p) -> o t p", p=P),
                               ones[3 * TAIL:3 * TAIL + 2, :].rearrange("o (t p) -> o t p", t=1).broadcast_to([2, GT, P])).then_inc(s_one, 1)

                def high_parts(g, e, h):
                    nt, rows = shape(g)
                    if not isinstance(g, int) or g >= 1:
                        act.wait_ge(s_h, g * KH)
                    for t in range(nt):
                        act.wait_ge(s_A, g * GT + t + 1)
                        nc.scalar.copy(aggT[0][:, :, t * P:t * P + rows],
                                       psA[t % 2][:, 0:2 * P].rearrange("p (c n) -> p c n", c=2)[:, :, 0:rows]).then_inc(s_ah, 1)
                        nc.scalar.copy(tailT[0:3 * TAIL, t * P:t * P + rows], psA[t % 2][0:3 * TAIL, 2 * P:2 * P + rows]).then_inc(s_ah, 1)
                        if t == min(nt, 2) - 1:
                            act.wait_ge(s_ld[e], h * 16 + 16)
                            n = slice(0, nt * rows)
                            nc.scalar.copy(xTs[0][:, :, n], xTr[e][:, :, n]).then_inc(s_xh, 1)

                def turn(g, e, h):
                    nt, rows = shape(g)
                    n = nt * rows
                    for m in range(KH):
                        act.wait_ge(s_h, g * KH + m + 1)
                        if not isinstance(g, int) or g >= 1:
                            act.wait_ge(s_o, g * GT)
                        nc.scalar.activation(hT[0][:, m, 0:n], psH[m % 4][:, 0:n], ACT.Relu).then_inc(s_rh, 1)
                        if m == 1 and (not isinstance(g, int) or g >= 1):
                            root(g - 1)
                        if m >= GT and (not isinstance(g, int) or g >= 1):
                            norm_rows(g - 1, m - GT)
                    if not isinstance(g, int) or g < GROUPS:
                        high_parts(g + 1, 1 - e, h + e)

                def root(g):
                    nt, rows = shape(g)
                    act.wait_ge(s_va, g * NVA + 7)
                    nc.scalar.sqrt(sd2[0:rows, 0:nt], va2[0:rows, 0:nt]).then_inc(s_sq2, 1)

                def norm_rows(g, t):
                    nt, rows = shape(g)
                    r = slice(0, rows)
                    if t == 0:
                        act.wait_ge(s_va, g * NVA + NVA)
                        if not isinstance(g, int) or g >= 1:
                            act.wait_ge(s_st, g * 32)
                    nc.scalar.activation(yr[r, t, 0:NF], x2[r, t, :], ACT.Identity, bias=nm2[r, t:t + 1], scale=rs2[r, t:t + 1]).then_inc(s_y, 1)

                high_parts(0, 0, 0)
                for g in range(2):
                    turn(g, g, 0)
                with act.Fori(1, 5) as h:
                    for e in range(2):
                        turn(h * 2 + e, e, h)
                for g in range(10, 13):
                    turn(g, g % 2, g // 2)
                root(GROUPS)
                norm_rows(GROUPS, 0)

            @block.tensor
            def _(pe):
                pe.wait_ge(s_one, 1)

                def transposes(g, tiles):
                    nt, rows = shape(g)
                    for t in tiles:
                        pe.wait_ge(s_am, g * (6 * GT) + 6 * t + 6)
                        pe.wait_ge(s_as, g * (NAS * GT) + NAS * t + NAS)
                        if not isinstance(g, int) or g * GT + t >= 2:
                            pe.wait_ge(s_al, g * (2 * GT) + 2 * t - 2)
                        for i in range(3):
                            f = min(P, AW - i * P)
                            ins = nc.tensor.transpose(psA[t % 2][0:f, i * P:i * P + rows], agg[0:rows, t, i * P:i * P + f],
                                                      ident[0:rows, 0:rows])
                        ins.then_inc(s_A, 1)

                def hidden(g):
                    nt, rows = shape(g)
                    n = slice(0, nt * rows)
                    pe.wait_ge(s_xl, g + 1)
                    for m in range(KH):
                        if not isinstance(g, int) or g * KH + m >= 4:
                            pe.wait_ge(s_rl, g * KH + m - 3)
                        o, w_ = psH[m % 4][:, n], slice(m * P, (m + 1) * P)
                        for c in range(KF):
                            split3(nc, o, [w[:, c, w_] for w in W1f], [x_[:, c, n] for x_ in xTs], c == 0, False)
                        if m == 0:
                            pe.wait_ge(s_al, g * (2 * GT) + 2 * nt)
                        for c in range(2):
                            split3(nc, o, [w[:, 2 + c, w_] for w in W1f], [a[:, c, n] for a in aggT], False, False)
                        ins = nc.tensor.matmul(o, W1t[:, w_], tailT[:, n], start=False, stop=True)
                        ins.then_inc(s_h, 1)

                def output(g, t):
                    nt, rows = shape(g)
                    if not isinstance(g, int) or g * GT + t >= 2:
                        pe.wait_ge(s_x2, g * GT + t - 1)
                    o, cols = psO[t % 2][0:rows, 0:NF], slice(t * P, t * P + rows)
                    for m in range(KH):
                        if t == 0:
                            pe.wait_ge(s_rl, g * KH + m + 1)
                        ins = split3(nc, o, [h_[:, m, cols] for h_ in hT], [w[:, m, :] for w in W2s], m == 0, m == KH - 1)
                    ins.then_inc(s_o, 1)

                def turn(g):
                    hidden(g)
                    after = shape(g + 1)[0] if not isinstance(g, int) or g < GROUPS else 0
                    transposes(g + 1, range(min(after, 2)))
                    for t in range(shape(g)[0]):
                        output(g, t)
                        if t + 2 < after:
                            transposes(g + 1, [t + 2])
                transposes(0, range(GT))
                turn(0)
                with pe.Fori(1, 11) as g:
                    turn(g)
                turn(11)
                turn(12)

        ctx2.close()
        ctx3 = ExitStack()
        ctx3pair = lambda n, s: [ctx3.enter_context(nc.sbuf_tensor(n + h, s, f32r)) for h in ("_hi", "_lo")]
        F1 = ctx3pair("F1", [P, KF, HID])
        F2 = ctx3pair("F2", [P, KH, NF])
        f2b = ctx3pair("f2b", [1, NF])
        one_r = ctx3.enter_context(nc.sbuf_tensor("one_r", [1, P], f32r))
        f1c = ctx3.enter_context(nc.sbuf_tensor("f1c", [P, KH], f32))
        lst = ctx3.enter_context(nc.sbuf_tensor("lst", [P, STILES], i32))

        with ExitStack() as ctx:
            sb = lambda n, s, d=f32: ctx.enter_context(nc.sbuf_tensor(n, s, d))
            ps = lambda n, s: ctx.enter_context(nc.psum_tensor(n, s, f32))
            sem = lambda n: ctx.enter_context(nc.semaphore(n))
            DIG = 15
            DTOP = 7
            ROUNDS = 7
            rF1 = sb("rF1", [P, KF, HID])
            rF2 = sb("rF2", [P, KH, NF])
            rfb = sb("rfb", [1, NF])
            valid = sb("valid", [P, TILES])
            v = sb("v", [P, TILES])
            jk = sb("jk", [P, TILES])
            numi = sb("numi", [P, DIG], i32)
            num = sb("num", [P, DIG])
            dtop = sb("dtop", [P, DTOP], i32)
            dig = sb("dig", [P, DIG], i32)
            cand = sb("cand", [P, DIG], i32)
            reach = sb("reach", [P, DIG, TILES])
            cnt = sb("cnt", [P, DIG])
            hit = sb("hit", [P, DIG], i32)
            best = sb("best", [P, 1], i32)
            pref = sb("pref", [P, 1], i32)
            acc = sb("acc", [P, 4])
            sgn = sb("sgn", [P, 1])
            kk_ = sb("kk_", [P, 1])
            thr = sb("thr", [P, 1])
            gt = sb("gt", [P, TILES])
            eq = sb("eq", [P, TILES])
            zero = sb("zero4", [P, TILES])
            rank = sb("rank", [P, TILES])
            diff = sb("diff", [P, TILES])
            cum = sb("cum", [P, TILES])
            need = sb("need", [P, 1])
            tri = sb("tri", [P, P])
            ri = sb("ri", [TILES, STILES * P], i32)
            rf = sb("rf", [TILES, STILES * P])
            step_ = sb("step_", [TILES, STILES * P])
            rows_ = sb("rows_", [TILES, P + 1])
            cumT = sb("cumT", [TILES, 1])
            below = sb("below", [P, P])
            cntp = sb("cntp", [P, STILES])
            first = sb("first", [P, STILES])
            psN = ps("psN", [P, 512])
            psP = ps("psP", [P, 512])
            psT = ps("psT4", [P, 512])
            psL = [ps(f"psL{i}", [P, 512]) for i in range(4)]
            s_w = [sem(f"c_w{i}") for i in range(3)]
            s_f1 = sem("c_f1")
            s_hi = sem("c_hi")
            s_lo = sem("c_lo")
            s_io = sem("c_io")
            s_rf = sem("c_rf")
            s_c = sem("c_c")
            s_v = sem("c_v")
            s_n = sem("c_n")
            s_p = sem("c_p")
            s_tri = sem("c_tri")
            s_tr = sem("c_tr")
            s_rows = sem("c_rows")
            s_L = sem("c_L")
            s_cnt = sem("c_cnt")
            block = ctx.enter_context(nc.Block())

            @block.sync
            def _(sp):
                sp.dma_start(rF1[:, :, :], w1.rearrange("(c p) n -> p c n", p=P)).then_inc(s_w[0], 16)
                sp.dma_start(rF2[:, :, :], w2.rearrange("(c p) n -> p c n", p=P)).then_inc(s_w[1], 16)
                sp.dma_start(rfb[0:1, :], fb2.rearrange("(a b) -> a b", a=1)).then_inc(s_w[2], 16)
                sp.dma_start(f1c[:, :], fb1.rearrange("(c p) -> p c", p=P), allow_slow_non_contiguous=True).then_inc(s_f1, 16)
                sp.wait_ge(s_f1, 16)

            @block.gpsimd
            def _(pool):
                nc.gpsimd.iota(numi[:, :], pattern=[[1, DIG]], base=1, channel_multiplier=0).then_inc(s_io, 1)
                nc.gpsimd.iota(ri[:, :], pattern=[[1, STILES * P]], base=0, channel_multiplier=0).then_inc(s_io, 1)
                nc.gpsimd.memset(tri[:, :], 1.0).then_inc(s_tri, 1)
                pool.wait_ge(s_tri, 1)
                nc.gpsimd.affine_select(out=tri[:, :], in_=tri[:, :], compare_op=ALU.is_gt, fill=0.0, base=0,
                                        pattern=[[1, P]], channel_multiplier=-1).then_inc(s_tri, 1)
                for i, (raw, (hi, lo)) in enumerate(((rF1, F1), (rF2, F2))):
                    pool.wait_ge(s_hi, i + 1)
                    nc.gpsimd.tensor_tensor(lo[:, :, :], raw[:, :, :], hi[:, :, :].bitcast(f32), ALU.subtract).then_inc(s_lo, 1)
                pool.wait_ge(s_hi, 3)
                nc.gpsimd.tensor_tensor(f2b[1][:, :], rfb[:, :], f2b[0][:, :].bitcast(f32), ALU.subtract).then_inc(s_lo, 1)

            @block.scalar
            def _(act):
                act.wait_ge(s_w[0], 16)
                nc.scalar.copy(F1[0][:, :, :], rF1[:, :, :]).then_inc(s_hi, 1)
                act.wait_ge(s_w[1], 16)
                nc.scalar.copy(F2[0][:, :, :], rF2[:, :, :]).then_inc(s_hi, 1)
                act.wait_ge(s_w[2], 16)
                nc.scalar.copy(f2b[0][:, :], rfb[:, :]).then_inc(s_hi, 1)
                nc.scalar.copy(one_r[0:1, :], ones[0:1, :]).then_inc(s_hi, 1)
                act.wait_ge(s_io, 2)
                nc.scalar.copy(rf[:, :], ri[:, :]).then_inc(s_rf, 1)

            @block.vector
            def _(dve):
                nv = [0]

                def step(ins):
                    nv[0] += 1
                    ins.then_inc(s_v, 1)
                    dve.wait_ge(s_v, nv[0])

                step(nc.vector.memset(zero[:, :], 0.0))
                step(nc.vector.tensor_scalar(valid[:, :], node[:, :], float(NODES), None, ALU.is_lt))
                step(nc.vector.tensor_scalar(v[:, :], wgt[:, :], 0.0, None, ALU.is_ge))
                step(nc.vector.tensor_tensor(v[:, :], v[:, :], valid[:, :], ALU.mult))
                step(nc.vector.tensor_reduce(cnt[:, 0:1], v[:, :], mybir.AxisListType.X, ALU.add))
                step(nc.vector.memset(cnt[:, 1:DIG], 0.0))
                dve.sem_inc(s_c, 1)
                dve.wait_ge(s_io, 1)
                step(nc.vector.tensor_copy(num[:, :], numi[:, :]))
                step(nc.vector.tensor_scalar(dtop[:, :], num[:, 0:DTOP], float(1 << 28), None, ALU.mult))
                step(nc.vector.tensor_scalar(dig[:, :], num[:, :], float(1 << 24), None, ALU.mult))
                dve.wait_ge(s_n, 1)
                step(nc.vector.tensor_scalar(acc[:, 1:2], psN[:, 0:1], float(SEL), None, ALU.is_ge))
                step(nc.vector.tensor_scalar(sgn[:, :], acc[:, 1:2], 2.0, -1.0, ALU.mult, ALU.add))
                step(nc.vector.tensor_scalar(kk_[:, :], acc[:, 1:2], float(SEL - (NODES - SEL + 1)), float(NODES - SEL + 1), ALU.mult, ALU.add))
                step(nc.vector.tensor_scalar(v[:, :], wgt[:, :], sgn[:, 0:1], None, ALU.mult))
                step(nc.vector.scalar_tensor_tensor(v[:, :], v[:, :], 1.0, valid[:, :], ALU.mult, ALU.mult))
                step(nc.vector.tensor_scalar(jk[:, :], valid[:, :], 1.0, None, ALU.subtract))
                step(nc.vector.tensor_tensor(v[:, :], v[:, :], jk[:, :], ALU.add))

                def digit(n, digits, i, k):
                    v3 = v[:, :].rearrange("p (o t) -> p o t", o=1).broadcast_to([P, n, TILES])
                    c3 = cand[:, 0:n].bitcast(f32).rearrange("p (d o) -> p d o", o=1).broadcast_to([P, n, TILES])
                    nc.vector.tensor_tensor(reach[:, 0:n, :], v3, c3, ALU.is_ge).then_inc(s_v, 1)
                    dve.wait_ge(s_v, k + 1)
                    nc.vector.tensor_reduce(cnt[:, 0:n], reach[:, 0:n, :], mybir.AxisListType.X, ALU.add).then_inc(s_v, 1)
                    dve.wait_ge(s_v, k + 2)
                    dve.sem_inc(s_c, 1)
                    dve.wait_ge(s_n, i + 2)
                    nc.vector.scalar_tensor_tensor(hit[:, 0:n], psN[:, 0:n], kk_[:, 0:1], digits[:, 0:n], ALU.is_ge, ALU.mult).then_inc(s_v, 1)
                    dve.wait_ge(s_v, k + 3)

                step(nc.vector.tensor_copy(cand[:, 0:DTOP], dtop[:, :]))
                digit(DTOP, dtop, 0, nv[0])
                nv[0] += 3
                step(nc.vector.tensor_reduce(pref[:, :], hit[:, 0:DTOP], mybir.AxisListType.X, ALU.max))
                base = nv[0]
                PER = 7
                with dve.Fori(0, ROUNDS) as i:
                    k = i * PER + base
                    nc.vector.tensor_tensor(cand[:, :], dig[:, :], pref[:, 0:1].broadcast_to([P, DIG]), ALU.bitwise_or).then_inc(s_v, 1)
                    dve.wait_ge(s_v, k + 1)
                    digit(DIG, dig, i + 1, k + 1)
                    nc.vector.tensor_reduce(best[:, :], hit[:, :], mybir.AxisListType.X, ALU.max).then_inc(s_v, 1)
                    dve.wait_ge(s_v, k + 5)
                    nc.vector.tensor_tensor(pref[:, :], pref[:, :], best[:, :], ALU.bitwise_or).then_inc(s_v, 1)
                    nc.vector.tensor_scalar(dig[:, :], dig[:, :], 4, None, ALU.logical_shift_right).then_inc(s_v, 1)
                    dve.wait_ge(s_v, k + 7)
                nv[0] = base + ROUNDS * PER
                step(nc.vector.tensor_tensor(thr[:, :], pref[:, :].bitcast(f32), sgn[:, :], ALU.mult))
                step(nc.vector.scalar_tensor_tensor(gt[:, :], wgt[:, :], thr[:, 0:1], valid[:, :], ALU.is_gt, ALU.mult))
                step(nc.vector.scalar_tensor_tensor(eq[:, :], wgt[:, :], thr[:, 0:1], valid[:, :], ALU.is_equal, ALU.mult))
                step(nc.vector.tensor_reduce(cnt[:, 0:1], gt[:, :], mybir.AxisListType.X, ALU.add))
                dve.sem_inc(s_c, 1)
                dve.wait_ge(s_n, ROUNDS + 3)
                step(nc.vector.tensor_scalar(need[:, :], psN[:, 0:1], -1.0, float(SEL), ALU.mult, ALU.add))

                def exclusive_rank(n):
                    dve.sem_inc(s_c, 1)
                    dve.wait_ge(s_p, n)
                    step(nc.vector.tensor_copy(jk[:, :], psP[:, 0:TILES]))
                    step(nc.vector.tensor_tensor_scan(cum[:, :], zero[:, :], jk[:, :], 0.0, ALU.add, ALU.add))
                    step(nc.vector.tensor_tensor(cum[:, :], cum[:, :], jk[:, :], ALU.subtract))
                    step(nc.vector.tensor_tensor(rank[:, :], cum[:, :], psP[:, 64:64 + TILES], ALU.add))

                exclusive_rank(1)
                step(nc.vector.tensor_scalar(rank[:, :], rank[:, :], need[:, 0:1], None, ALU.is_lt))
                step(nc.vector.tensor_tensor(eq[:, :], eq[:, :], rank[:, :], ALU.mult))
                step(nc.vector.tensor_tensor(gt[:, :], gt[:, :], eq[:, :], ALU.add))
                exclusive_rank(2)
                step(nc.vector.tensor_tensor(rank[:, :], rank[:, :], gt[:, :], ALU.add))
                step(nc.vector.tensor_copy(diff[:, 0:1], rank[:, 0:1]))
                step(nc.vector.tensor_tensor(diff[:, 1:TILES], rank[:, 1:TILES], rank[:, 0:TILES - 1], ALU.subtract))
                dve.sem_inc(s_c, 1)
                dve.wait_ge(s_tr, 1)
                step(nc.vector.tensor_copy(cumT[:, :], psT[0:TILES, P:P + 1]))
                step(nc.vector.tensor_copy(rows_[:, 0:P], psT[0:TILES, 0:P]))
                step(nc.vector.memset(rows_[:, P:P + 1], float(P)))
                step(nc.vector.memset(rows_[0:1, P:P + 1], 0.0))
                dve.wait_ge(s_rf, 1)
                step(nc.vector.tensor_scalar(step_[:, :], rf[:, :], cumT[:, 0:1], None, ALU.is_ge))
                dve.sem_inc(s_rows, 1)
                for s in range(STILES):
                    dve.wait_ge(s_L, s + 1)
                    if s:
                        dve.wait_ge(s_cnt, 2 * s)
                    nc.vector.tensor_scalar(below[:, :], psL[s % 4][:, 0:P], node[:, s:s + 1], None, ALU.is_le, ALU.add,
                                            accum_out=cntp[:, s:s + 1]).then_inc(s_cnt, 1)
                    nc.vector.tensor_copy(first[:, s:s + 1], psL[s % 4][:, P:P + 1]).then_inc(s_cnt, 1)
                dve.wait_ge(s_cnt, 2 * STILES)
                step(nc.vector.tensor_tensor(lst[:, :], first[:, :], cntp[:, :], ALU.add))

            @block.tensor
            def _(pe):
                with pe.Fori(0, ROUNDS + 3) as i:
                    pe.wait_ge(s_c, i + 1)
                    nc.tensor.matmul(psN[:, 0:DIG], ones[:, :], cnt[:, :], start=True, stop=True).then_inc(s_n, 1)
                pe.wait_ge(s_tri, 2)
                for i, marked in enumerate((eq, gt)):
                    pe.wait_ge(s_c, ROUNDS + 4 + i)
                    nc.tensor.matmul(psP[:, 0:TILES], ones[:, :], marked[:, :], start=True, stop=True)
                    nc.tensor.matmul(psP[:, 64:64 + TILES], tri[:, :], marked[:, :], start=True, stop=True).then_inc(s_p, 1)
                pe.wait_ge(s_c, ROUNDS + 6)
                nc.tensor.transpose(psT[0:TILES, 0:P], diff[:, :], ident[:, :])
                nc.tensor.transpose(psT[0:TILES, P:2 * P], cum[:, :], ident[:, :]).then_inc(s_tr, 1)
                pe.wait_ge(s_rows, 1)
                for s in range(STILES):
                    if s >= 4:
                        pe.wait_ge(s_cnt, 2 * s - 6)
                    nc.tensor.matmul(psL[s % 4][:, 0:P + 1], step_[:, s * P:(s + 1) * P], rows_[:, :], start=True, stop=True).then_inc(s_L, 1)

        with ExitStack() as ctx:
            sb = lambda n, s, d=f32: ctx.enter_context(nc.sbuf_tensor(n, s, d))
            ps = lambda n, s: ctx.enter_context(nc.psum_tensor(n, s, f32))
            sem = lambda n: ctx.enter_context(nc.semaphore(n))
            pair = lambda n, s: [sb(n + h, s, f32r) for h in ("_hi", "_lo")]
            yg = [sb(f"yg{i}", [P, GT, YROW]) for i in range(2)]
            yT = pair("yT", [P, KF, GT * P])
            gf = [sb(f"gf{i}", [P, GT * P]) for i in range(4)]
            gT = pair("gT", [P, KH, GT * P])
            zo = sb("zo", [P, GT, NF])
            psY = [ps(f"psY{i}", [P, 512]) for i in range(2)]
            psG = [ps(f"psG{i}", [P, 512]) for i in range(4)]
            psF = [ps(f"psF{i}", [P, 512]) for i in range(2)]
            s_g = [sem(f"d_g{i}") for i in range(2)]
            s_y = sem("d_y")
            s_yh = sem("d_yh")
            s_yl = sem("d_yl")
            s_h = sem("d_h")
            s_ge = sem("d_ge")
            s_gh = sem("d_gh")
            s_gl = sem("d_gl")
            s_f = sem("d_f")
            s_z = sem("d_z")
            s_out = sem("d_out")

            def shape(g):
                return (1, SLAST) if g == SGROUPS else (GT, P)

            block = ctx.enter_context(nc.Block())

            @block.gpsimd
            def _(pool):
                def gather(g):
                    nt, rows = shape(g)
                    if g >= 2:
                        pool.wait_ge(s_z, (g - 2) * GT + GT)
                    for t in range(nt):
                        nc.gpsimd.indirect_dma_start(
                            out=yg[g % 2][0:rows, t, :], out_offset=None, in_=yrow_d,
                            in_offset=bass.IndirectOffsetOnAxis(ap=lst[0:rows, g * GT + t:g * GT + t + 1], axis=0)).then_inc(s_g[g % 2], 16)

                def scatter(g):
                    nt, rows = shape(g)
                    for t in range(nt):
                        pool.wait_ge(s_z, g * GT + t + 1)
                        nc.gpsimd.indirect_dma_start(
                            out=out, out_offset=bass.IndirectOffsetOnAxis(ap=lst[0:rows, g * GT + t:g * GT + t + 1], axis=0),
                            in_=zo[0:rows, t, :], in_offset=None).then_inc(s_out, 16)
                gather(0)
                gather(1)
                for g in range(SGROUPS + 1):
                    scatter(g)
                    if g + 2 <= SGROUPS:
                        gather(g + 2)
                pool.wait_ge(s_out, 16 * STILES)

            @block.vector
            def _(dve):
                def y_low(g):
                    nt, rows = shape(g)
                    for t in range(nt):
                        dve.wait_ge(s_yh, g * GT + t + 1)
                        cols = slice(t * P, t * P + rows)
                        nc.vector.tensor_tensor(yT[1][:, :, cols],
                                                psY[t % 2][:, 0:2 * P].rearrange("p (c n) -> p c n", c=KF)[:, :, 0:rows],
                                                yT[0][:, :, cols].bitcast(f32), ALU.subtract).then_inc(s_yl, 1)
                y_low(0)
                for g in range(SGROUPS + 1):
                    nt, rows = shape(g)
                    n = slice(0, nt * rows)
                    for m in range(KH):
                        k = g * KH + m
                        dve.wait_ge(s_ge, k + 1)
                        if g:
                            dve.wait_ge(s_f, g * GT)
                        nc.vector.tensor_copy(gT[0][:, m, n], gf[m % 4][:, n]).then_inc(s_gh, 1)
                        dve.wait_ge(s_gh, k + 1)
                        nc.vector.tensor_tensor(gT[1][:, m, n], gf[m % 4][:, n], gT[0][:, m, n].bitcast(f32), ALU.subtract).then_inc(s_gl, 1)
                    if g < SGROUPS:
                        y_low(g + 1)
                    if g:
                        dve.wait_ge(s_out, 16 * g * GT)
                    for t in range(nt):
                        k = g * GT + t
                        dve.wait_ge(s_f, k + 1)
                        nc.vector.scalar_tensor_tensor(zo[0:rows, t, :], psF[k % 2][0:rows, 0:NF], yg[g % 2][0:rows, t, 2 * NF:2 * NF + 1],
                                                       yg[g % 2][0:rows, t, NF:2 * NF], ALU.mult, ALU.add).then_inc(s_z, 1)

            @block.scalar
            def _(act):
                def y_high(g):
                    nt, rows = shape(g)
                    if g:
                        act.wait_ge(s_h, g * KH)
                    for t in range(nt):
                        act.wait_ge(s_y, g * GT + t + 1)
                        nc.scalar.copy(yT[0][:, :, t * P:t * P + rows],
                                       psY[t % 2][:, 0:2 * P].rearrange("p (c n) -> p c n", c=KF)[:, :, 0:rows]).then_inc(s_yh, 1)
                y_high(0)
                for g in range(SGROUPS + 1):
                    nt, rows = shape(g)
                    n = nt * rows
                    for m in range(KH):
                        k = g * KH + m
                        act.wait_ge(s_h, k + 1)
                        if k >= 4:
                            act.wait_ge(s_gl, k - 3)
                        nc.scalar.activation(gf[m % 4][:, 0:n], psG[m % 4][:, 0:n], ACT.Gelu_apprx_tanh, bias=f1c[:, m:m + 1]).then_inc(s_ge, 1)
                    if g < SGROUPS:
                        y_high(g + 1)

            @block.tensor
            def _(pe):
                def transposes(g):
                    nt, rows = shape(g)
                    pe.wait_ge(s_g[g % 2], 16 * GT * (g // 2) + 16 * nt)
                    for t in range(nt):
                        if g * GT + t >= 2:
                            pe.wait_ge(s_yl, g * GT + t - 1)
                        for c in range(KF):
                            ins = nc.tensor.transpose(psY[t % 2][:, c * P:c * P + rows], yg[g % 2][0:rows, t, c * P:(c + 1) * P],
                                                      ident[0:rows, 0:rows])
                        ins.then_inc(s_y, 1)
                transposes(0)
                for g in range(SGROUPS + 1):
                    nt, rows = shape(g)
                    n = slice(0, nt * rows)
                    pe.wait_ge(s_yl, g * GT + nt)
                    for m in range(KH):
                        if g * KH + m >= 4:
                            pe.wait_ge(s_ge, g * KH + m - 3)
                        for c in range(KF):
                            ins = split3(nc, psG[m % 4][:, n], [f[:, c, m * P:(m + 1) * P] for f in F1], [y[:, c, n] for y in yT],
                                         c == 0, c == KF - 1)
                        ins.then_inc(s_h, 1)
                    if g < SGROUPS:
                        transposes(g + 1)
                    for t in range(nt):
                        k = g * GT + t
                        if k >= 2:
                            pe.wait_ge(s_z, k - 1)
                        o, cols = psF[k % 2][0:rows, 0:NF], slice(t * P, t * P + rows)
                        for i in range(2):
                            nc.tensor.matmul(o, one_r[0:1, 0:rows], f2b[i][0:1, :], start=(i == 0), stop=False)
                        for m in range(KH):
                            if t == 0:
                                pe.wait_ge(s_gl, g * KH + m + 1)
                            ins = split3(nc, o, [g_[:, m, cols] for g_ in gT], [f[:, m, :] for f in F2], False, m == KH - 1)
                        ins.then_inc(s_f, 1)
        ctx3.close()


_INS = ["x", "dst", "edge_attr_96", "L0_gnn_u", "L0_gnn_W1", "L0_gnn_b1", "L0_gnn_W2", "L0_gnn_b2",
        "L0_mix_W_qkv", "L0_mix_b_qkv", "L0_mix_W_out", "L0_mix_b_out",
        "L0_ffn_wr", "L0_ffn_br", "L0_ffn_w1", "L0_ffn_b1", "L0_ffn_w2", "L0_ffn_b2"]


def kernel(**inputs):
    import numpy as _np
    import concourse.bacc as _bacc
    from concourse import mybir as _mybir
    from concourse.bass_utils import run_bass_kernel_spmd as _run

    nc = _bacc.Bacc("TRN2", target_bir_lowering=False, num_devices=1)
    arrays, args = {}, []
    for name in _INS:
        a = _np.ascontiguousarray(inputs[name])
        if name == "dst":
            a = _np.pad(a, (SIDE, EPAD - EDGES), constant_values=(-1, NODES))
        if name == "edge_attr_96":
            a = _np.pad(a, ((0, EPAD - EDGES), (0, 0)))
        arrays[f"in_{name}"] = a
        args.append(nc.dram_tensor(f"in_{name}", a.shape, _mybir.dt.from_np(a.dtype), kind="ExternalInput").ap())
    args.append(nc.dram_tensor("out_x", (NODES, NF), f32, kind="ExternalOutput").ap())
    build(nc, *args)
    r = _run(nc, [arrays], core_ids=[0])
    return r.results[0]["out_x"]
```
